# Optimizing a Trainium2 kernel written in Bass

```python
import numpy as np
import jax
import jax.numpy as jnp

def _softmax(x, axis=-1):
    return jax.nn.softmax(x, axis=axis)

def _gelu(x):
    return jax.nn.gelu(x, approximate=True)

def _silu(x):
    return jax.nn.silu(x)

def _sigmoid(x):
    return jax.nn.sigmoid(x)

def _layernorm(x, axis=-1, eps=1e-05):
    m = jnp.mean(x, axis=axis, keepdims=True)
    v = jnp.var(x, axis=axis, keepdims=True)
    return (x - m) / jnp.sqrt(v + eps)

def _scatter_add(tgt, idx, src, axis=0):
    return tgt.at[idx].add(src)

def _segment_sum(src, seg, n):
    return jax.ops.segment_sum(src, seg, n)
kernel_name = 'mk_gnn_preln_d4_gnn_r32_9c2d35'

def setup_inputs(seed: int=0):
    np.random.seed(seed)
    _w = jnp.asarray

    def _rec_inputs():
        import jax
        import jax.numpy as jnp
        _gk = jax.random.key(seed)
        x = -0.000202 + 1 * jax.random.normal(jax.random.fold_in(_gk, 1), (3125, 128), jnp.float32)
        src = jax.random.randint(jax.random.fold_in(_gk, 2), (100000,), 0, 3125, jnp.int32)
        dst = jnp.minimum((3125 * jax.random.uniform(jax.random.fold_in(_gk, 3), (100000,)) ** 2.0).astype(jnp.int32), 99999)
        _o = jnp.argsort(dst, stable=True)
        src = src[_o]
        dst = dst[_o]
        edge_attr_26 = 4.66435e-05 + 0.999962 * jax.random.normal(jax.random.fold_in(_gk, 12), (100000, 26), jnp.float32)
        edge_type_8 = jax.random.randint(jax.random.fold_in(_gk, 14), (100000,), 0, 8, jnp.int32)
        edge_weight1 = jax.random.uniform(jax.random.fold_in(_gk, 15), (100000, 1), jnp.float32, 0.0, 1)
        return (x, src, dst, edge_attr_26, edge_type_8, edge_weight1)
    x, src, dst, edge_attr_26, edge_type_8, edge_weight1 = _rec_inputs()

    def _L0_gnn_setup():
        import jax, jax.numpy as jnp
        import numpy as np
        N_NODES = 50000
        N_EDGES = 50000
        IN_FEAT = 128
        OUT_FEAT = 128
        NUM_RELS = 8
        key = jax.random.key(seed)
        k1, k2, k3, k4, k5, k6, k7 = jax.random.split(key, 7)
        x = jax.random.normal(k1, (N_NODES, IN_FEAT), dtype=jnp.float32)
        norm = jax.random.uniform(k2, (N_EDGES, 1), dtype=jnp.float32)
        src = jax.random.randint(k3, (N_EDGES,), 0, N_NODES)
        dst = jax.random.randint(k4, (N_EDGES,), 0, N_NODES)
        rel_type = jax.random.randint(k5, (N_EDGES,), 0, NUM_RELS)
        gain = float(np.sqrt(2.0))
        bound = gain * float(np.sqrt(6.0 / (IN_FEAT + OUT_FEAT)))
        weight = jax.random.uniform(k6, (NUM_RELS, IN_FEAT, OUT_FEAT), dtype=jnp.float32, minval=-bound, maxval=bound)
        bias = jax.random.uniform(k7, (OUT_FEAT,), dtype=jnp.float32, minval=-0.1, maxval=0.1)
        return {'x': x, 'norm': norm, 'weight': weight, 'bias': bias, 'src': src, 'dst': dst, 'rel_type': rel_type}
    _L0_gnn_all = _L0_gnn_setup()
    _L0_gnn_in = {k: v for k, v in _L0_gnn_all.items() if k in ('weight', 'bias')}
    del _L0_gnn_all

    def _L1_gnn_setup():
        import jax, jax.numpy as jnp
        import numpy as np
        N, E, H, EH, R, MH = (50000, 25000, 128, 26, 2, 256)
        IN = 2 * H + EH
        OUT = 2 * H
        key = jax.random.key(seed)
        ks = jax.random.split(key, 10)

        def w(k, shape, fan_in):
            return jax.random.normal(k, shape, jnp.float32) / np.float32(np.sqrt(fan_in))
        return {'hv': jax.random.normal(ks[0], (N, H), jnp.float32), 'he': jax.random.normal(ks[1], (E, EH), jnp.float32), 'src': jax.random.randint(ks[2], (E,), 0, N, jnp.int32), 'dst': jax.random.randint(ks[3], (E,), 0, N, jnp.int32), 'mlp_w1': w(ks[4], (R, IN, MH), IN), 'mlp_b1': jnp.zeros((R, MH), jnp.float32), 'mlp_w2': w(ks[5], (R, MH, OUT), MH), 'mlp_b2': jnp.zeros((R, OUT), jnp.float32), 'gru_wih': w(ks[6], (R, 3 * H, OUT), OUT), 'gru_whh': w(ks[7], (R, 3 * H, H), H), 'gru_bih': jnp.zeros((R, 3 * H), jnp.float32), 'gru_bhh': jnp.zeros((R, 3 * H), jnp.float32)}
    _L1_gnn_all = _L1_gnn_setup()
    _L1_gnn_in = {k: v for k, v in _L1_gnn_all.items() if k in ('mlp_w1', 'mlp_b1', 'mlp_w2', 'mlp_b2', 'gru_wih', 'gru_whh', 'gru_bih', 'gru_bhh')}
    del _L1_gnn_all

    def _L2_gnn_setup():
        import jax, jax.numpy as jnp
        import numpy as np
        N, E, D, H, C = (50000, 25000, 128, 4, 32)
        key = jax.random.key(seed)
        ks = jax.random.split(key, 8)
        s = 0.05
        return {'x': jax.random.normal(ks[0], (N, D), jnp.float32), 'edge_index': jax.random.randint(ks[1], (2, E), 0, N, dtype=jnp.int32), 'gamma': jnp.ones((D,), jnp.float32), 'beta': jnp.zeros((D,), jnp.float32), 'W_gat': jax.random.normal(ks[2], (D, H * C), jnp.float32) * s, 'att_src': jax.random.normal(ks[3], (H, C), jnp.float32) * s, 'att_dst': jax.random.normal(ks[4], (H, C), jnp.float32) * s, 'bias_gat': jnp.zeros((H * C,), jnp.float32), 'W_proj': jax.random.normal(ks[5], (D, H * C), jnp.float32) * s, 'b_proj': jnp.zeros((H * C,), jnp.float32)}
    _L2_gnn_all = _L2_gnn_setup()
    _L2_gnn_in = {k: v for k, v in _L2_gnn_all.items() if k in ('gamma', 'beta', 'W_gat', 'att_src', 'att_dst', 'bias_gat', 'W_proj', 'b_proj')}
    del _L2_gnn_all

    def _L3_gnn_setup():
        import jax, jax.numpy as jnp
        import numpy as np
        N, E, D, H = (500, 8000, 128, 4)
        ALPHA = 0.2
        key = jax.random.key(seed)
        ks = jax.random.split(key, 9)
        s = 0.1
        return {'h': jax.random.normal(ks[0], (N, D), jnp.float32), 'W': jax.random.normal(ks[1], (H, D, D), jnp.float32) * s, 'a': jax.random.normal(ks[2], (H, 2 * D), jnp.float32) * s, 'W_ih': jax.random.normal(ks[3], (3 * D, H * D), jnp.float32) * s, 'W_hh': jax.random.normal(ks[4], (3 * D, D), jnp.float32) * s, 'b_ih': jnp.zeros((3 * D,), jnp.float32), 'b_hh': jnp.zeros((3 * D,), jnp.float32), 'src': jax.random.randint(ks[5], (E,), 0, N, jnp.int32), 'dst': jax.random.randint(ks[6], (E,), 0, N, jnp.int32)}
    _L3_gnn_all = _L3_gnn_setup()
    _L3_gnn_in = {k: v for k, v in _L3_gnn_all.items() if k in ('W', 'a', 'W_ih', 'W_hh', 'b_ih', 'b_hh')}
    del _L3_gnn_all
    return {'x': x, 'src': src, 'dst': dst, 'edge_attr_26': edge_attr_26, 'edge_type_8': edge_type_8, 'edge_weight1': edge_weight1, 'L0_gnn_weight': _L0_gnn_in['weight'], 'L0_gnn_bias': _L0_gnn_in['bias'], 'L1_gnn_mlp_w1': _L1_gnn_in['mlp_w1'], 'L1_gnn_mlp_b1': _L1_gnn_in['mlp_b1'], 'L1_gnn_mlp_w2': _L1_gnn_in['mlp_w2'], 'L1_gnn_mlp_b2': _L1_gnn_in['mlp_b2'], 'L1_gnn_gru_wih': _L1_gnn_in['gru_wih'], 'L1_gnn_gru_whh': _L1_gnn_in['gru_whh'], 'L1_gnn_gru_bih': _L1_gnn_in['gru_bih'], 'L1_gnn_gru_bhh': _L1_gnn_in['gru_bhh'], 'L2_gnn_gamma': _L2_gnn_in['gamma'], 'L2_gnn_beta': _L2_gnn_in['beta'], 'L2_gnn_W_gat': _L2_gnn_in['W_gat'], 'L2_gnn_att_src': _L2_gnn_in['att_src'], 'L2_gnn_att_dst': _L2_gnn_in['att_dst'], 'L2_gnn_bias_gat': _L2_gnn_in['bias_gat'], 'L2_gnn_W_proj': _L2_gnn_in['W_proj'], 'L2_gnn_b_proj': _L2_gnn_in['b_proj'], 'L3_gnn_W': _L3_gnn_in['W'], 'L3_gnn_a': _L3_gnn_in['a'], 'L3_gnn_W_ih': _L3_gnn_in['W_ih'], 'L3_gnn_W_hh': _L3_gnn_in['W_hh'], 'L3_gnn_b_ih': _L3_gnn_in['b_ih'], 'L3_gnn_b_hh': _L3_gnn_in['b_hh']}

def reference(x, src, dst, edge_attr_26, edge_type_8, edge_weight1, L0_gnn_weight, L0_gnn_bias, L1_gnn_mlp_w1, L1_gnn_mlp_b1, L1_gnn_mlp_w2, L1_gnn_mlp_b2, L1_gnn_gru_wih, L1_gnn_gru_whh, L1_gnn_gru_bih, L1_gnn_gru_bhh, L2_gnn_gamma, L2_gnn_beta, L2_gnn_W_gat, L2_gnn_att_src, L2_gnn_att_dst, L2_gnn_bias_gat, L2_gnn_W_proj, L2_gnn_b_proj, L3_gnn_W, L3_gnn_a, L3_gnn_W_ih, L3_gnn_W_hh, L3_gnn_b_ih, L3_gnn_b_hh):
    import jax
    import jax.numpy as jnp

    def _L0_gnn_ref(x, norm, weight, bias, src, dst, rel_type):
        import jax, jax.numpy as jnp
        import numpy as np
        N_NODES = 50000
        N_EDGES = 50000
        IN_FEAT = 128
        OUT_FEAT = 128
        NUM_RELS = 8
        n_nodes = x.shape[0]
        hw = jnp.einsum('ni,rio->rno', x, weight)
        msg = hw[rel_type, src] * norm
        h = jax.ops.segment_sum(msg, dst, num_segments=n_nodes)
        h = jax.nn.relu(h + bias)
        return h

    def _L1_gnn_ref(hv, he, src, dst, mlp_w1, mlp_b1, mlp_w2, mlp_b2, gru_wih, gru_whh, gru_bih, gru_bhh):
        import jax, jax.numpy as jnp
        import numpy as np
        N, E, H, EH, R, MH = (50000, 25000, 128, 26, 2, 256)
        IN = 2 * H + EH
        OUT = 2 * H
        n_nodes, h = hv.shape
        num_rounds = mlp_w1.shape[0]
        for t in range(num_rounds):
            x = jnp.concatenate([hv[dst], hv[src], he], axis=1)
            h1 = jax.nn.relu(x @ mlp_w1[t] + mlp_b1[t])
            m = h1 @ mlp_w2[t] + mlp_b2[t]
            a = jax.ops.segment_sum(m, dst, num_segments=n_nodes)
            gx = a @ gru_wih[t].T + gru_bih[t]
            gh = hv @ gru_whh[t].T + gru_bhh[t]
            r = jax.nn.sigmoid(gx[:, :h] + gh[:, :h])
            z = jax.nn.sigmoid(gx[:, h:2 * h] + gh[:, h:2 * h])
            n = jnp.tanh(gx[:, 2 * h:] + r * gh[:, 2 * h:])
            hv = (1.0 - z) * n + z * hv
        return hv

    def _L2_gnn_ref(x, edge_index, gamma, beta, W_gat, att_src, att_dst, bias_gat, W_proj, b_proj):
        import jax, jax.numpy as jnp
        import numpy as np
        N, E, D, H, C = (50000, 25000, 128, 4, 32)
        n = x.shape[0]
        identity = x @ W_proj + b_proj
        mu = jnp.mean(x, axis=-1, keepdims=True)
        var = jnp.mean((x - mu) ** 2, axis=-1, keepdims=True)
        xn = (x - mu) * jax.lax.rsqrt(var + 1e-05) * gamma + beta
        loops = jnp.arange(n, dtype=edge_index.dtype)
        src = jnp.concatenate([edge_index[0], loops])
        dst = jnp.concatenate([edge_index[1], loops])
        xw = (xn @ W_gat).reshape(n, H, C)
        a_s = jnp.einsum('nhc,hc->nh', xw, att_src)
        a_d = jnp.einsum('nhc,hc->nh', xw, att_dst)
        e = jax.nn.leaky_relu(a_s[src] + a_d[dst], 0.2)
        m = jax.ops.segment_max(e, dst, num_segments=n)
        e = jnp.exp(e - m[dst])
        denom = jax.ops.segment_sum(e, dst, num_segments=n)
        alpha = e / (denom[dst] + 1e-16)
        agg = jax.ops.segment_sum(xw[src] * alpha[:, :, None], dst, num_segments=n)
        out = agg.reshape(n, H * C) + bias_gat
        return jax.nn.relu(identity + out)

    def _L3_gnn_ref(h, W, a, W_ih, W_hh, b_ih, b_hh, src, dst):
        import jax, jax.numpy as jnp
        import numpy as np
        N, E, D, H = (500, 8000, 128, 4)
        ALPHA = 0.2
        n = h.shape[0]
        Wh = jnp.einsum('nd,hde->nhe', h, W)
        a1, a2 = (a[:, :D], a[:, D:])
        s_src = jnp.einsum('nhd,hd->nh', Wh, a1)
        s_dst = jnp.einsum('nhd,hd->nh', Wh, a2)
        e = jax.nn.leaky_relu(s_src[src] + s_dst[dst], ALPHA)
        m = jax.ops.segment_max(e, dst, num_segments=n)
        ex = jnp.exp(e - m[dst])
        denom = jax.ops.segment_sum(ex, dst, num_segments=n)
        att = ex / denom[dst]
        h_prime = jax.ops.segment_sum(att[:, :, None] * Wh[src], dst, num_segments=n)
        x = h_prime.reshape(n, H * D)
        gi = x @ W_ih.T + b_ih
        gh = h @ W_hh.T + b_hh
        i_r, i_z, i_n = jnp.split(gi, 3, axis=1)
        h_r, h_z, h_n = jnp.split(gh, 3, axis=1)
        r = jax.nn.sigmoid(i_r + h_r)
        z = jax.nn.sigmoid(i_z + h_z)
        nvec = jnp.tanh(i_n + r * h_n)
        return (1.0 - z) * nvec + z * h
    edge_index = jnp.stack([src, dst])
    h = jnp.maximum(_layernorm(x, axis=-1), 0.0)
    x = x + _L0_gnn_ref(h, edge_weight1, L0_gnn_weight, L0_gnn_bias, src, dst, edge_type_8)
    h = jnp.maximum(_layernorm(x, axis=-1), 0.0)
    x = x + _L1_gnn_ref(h, edge_attr_26, src, dst, L1_gnn_mlp_w1, L1_gnn_mlp_b1, L1_gnn_mlp_w2, L1_gnn_mlp_b2, L1_gnn_gru_wih, L1_gnn_gru_whh, L1_gnn_gru_bih, L1_gnn_gru_bhh)
    h = jnp.maximum(_layernorm(x, axis=-1), 0.0)
    x = x + _L2_gnn_ref(h, edge_index, L2_gnn_gamma, L2_gnn_beta, L2_gnn_W_gat, L2_gnn_att_src, L2_gnn_att_dst, L2_gnn_bias_gat, L2_gnn_W_proj, L2_gnn_b_proj)
    h = jnp.maximum(_layernorm(x, axis=-1), 0.0)
    x = x + _L3_gnn_ref(h, L3_gnn_W, L3_gnn_a, L3_gnn_W_ih, L3_gnn_W_hh, L3_gnn_b_ih, L3_gnn_b_hh, src, dst)
    return x

_drawn_inputs = setup_inputs


def setup_inputs(seed=0):
    import zlib

    import numpy as np

    out = dict(_drawn_inputs(seed))
    spreads = {'L1_gnn_mlp_b1': (0.0, 0.1),
     'L1_gnn_mlp_b2': (0.0, 0.1),
     'L1_gnn_gru_bih': (0.0, 0.8),
     'L1_gnn_gru_bhh': (0.0, 0.8),
     'L2_gnn_gamma': (1.0, 0.6),
     'L2_gnn_beta': (0.0, 0.8),
     'L2_gnn_bias_gat': (0.0, 0.522),
     'L2_gnn_b_proj': (0.0, 0.639),
     'L3_gnn_b_ih': (0.0, 0.8),
     'L3_gnn_b_hh': (0.0, 0.8)}
    factors = {'L0_gnn_bias': 3.178, 'L2_gnn_att_src': 8.0, 'L2_gnn_att_dst': 158.286, 'L3_gnn_a': 3.864}
    for name, (base, spread) in spreads.items():
        noise = np.random.default_rng([zlib.crc32(name.encode()), seed]).standard_normal(out[name].shape)
        drawn = base * np.exp(spread * noise) if base else spread * noise
        out[name] = jnp.asarray(drawn.astype(out[name].dtype))
    for name, factor in factors.items():
        out[name] = (out[name] * factor).astype(out[name].dtype)
    return out
```

```python
from contextlib import ExitStack

import concourse.bass as bass
from concourse import mybir

F32 = mybir.dt.float32
I32 = mybir.dt.int32
ALU = mybir.AluOpType
ACT = mybir.ActivationFunctionType
AX = mybir.AxisListType

P = 128
N_NODES, D = 3125, 128
N_EDGES = 100000
N_ATTR = 26
N_REL = 8
HEADS = 4
MH = 256
NB = -(-N_NODES // P)
NPAD = NB * P
LAST_ROWS = N_NODES - (NB - 1) * P
G3 = 3 * D

SORT_P = 125
SORT_J = N_EDGES // SORT_P
UNIT = 2 * P
UNITS = -(-(N_EDGES + NB * (UNIT - 1)) // UNIT)
GT = 8
GU = GT // 2
GROUPS = -(-UNITS // GU)
UNITS = GROUPS * GU
TILES = GROUPS * GT
SLOTS = TILES * P
BODIES = GROUPS // 2
BU = 2 * GU
REC = 32
F_NORM, F_DST, F_SRC, F_HW = N_ATTR, N_ATTR + 1, N_ATTR + 2, N_ATTR + 3
BIG = 1.0e30
EPS = 1e-5
SLOPE = 0.2


class Signal:

    def __init__(self, sem):
        self.sem = sem
        self.base = 0

    def at(self, n):
        return n + self.base

    def close(self, n):
        self.base += n


class Program:
    def __init__(self, nc, ctx, dram):
        self.nc, self.ctx, self.d = nc, ctx, dram
        self.signals = {}

    def sig(self, name):
        if name not in self.signals:
            self.signals[name] = Signal(self.ctx.enter_context(self.nc.semaphore(name)))
        return self.signals[name]

    def apart(self, eng):
        eng.sem_inc(self.sig("apart").sem, 1)


def unique(name, used={}):
    used[name] = used.get(name, 0) + 1
    return f"{name}_{used[name]}"


def f32(ctx, nc, name, shape):
    return ctx.enter_context(nc.sbuf_tensor(unique(name), shape, F32))


def i32(ctx, nc, name, shape):
    return ctx.enter_context(nc.sbuf_tensor(unique(name), shape, I32))


def bank(ctx, nc, name):
    return ctx.enter_context(nc.psum_tensor(unique(name), [P, 512], F32))


def link(p, eng, s, ins, count):
    ins.then_inc(s.sem, 1)
    count[0] += 1
    eng.wait_ge(s.sem, s.at(count[0]))


def stage_constants(p, k):
    nc, d = p.nc, p.d
    s_ld, s_c, s_z = p.sig("load"), p.sig("const"), p.sig("zero")
    with nc.Block() as block:
        @block.vector
        def _(dve):
            dve.memset(k["x"][:], 0.0).then_inc(s_z.sem, 1)
            dve.memset(k["ones"][:], 1.0)

        @block.sync
        def _(sp):
            sp.wait_ge(s_z.sem, s_z.at(1))
            xv = d["x"][0:(NB - 1) * P, :].rearrange("(b p) f -> p b f", p=P)
            sp.dma_start(k["x"][:, 0:NB - 1, :], xv).then_inc(s_ld.sem, 16)
            sp.dma_start(k["x"][0:LAST_ROWS, NB - 1, :], d["x"][(NB - 1) * P:N_NODES, :]).then_inc(s_ld.sem, 16)
            sp.wait_ge(s_ld.sem, s_ld.at(32))

        @block.gpsimd
        def _(pool):
            pool.memset(k["ident"][:], 0.0).then_inc(s_c.sem, 1)
            pool.memset(k["tri"][:], 1.0).then_inc(s_c.sem, 1)
            pool.wait_ge(s_c.sem, s_c.at(2))
            pool.affine_select(out=k["ident"][:], in_=k["ident"][:], compare_op=ALU.not_equal, fill=1.0,
                               base=0, pattern=[[-1, P]], channel_multiplier=1)
            pool.affine_select(out=k["tri"][:], in_=k["tri"][:], compare_op=ALU.is_gt, fill=0.0,
                               base=0, pattern=[[1, P]], channel_multiplier=-1)
            pool.iota(k["iota_i"][:], pattern=[[1, UNITS]], base=0, channel_multiplier=0).then_inc(s_c.sem, 1)
            pool.wait_ge(s_c.sem, s_c.at(3))
            pool.tensor_copy(k["iota"][:], k["iota_i"][:])
    s_ld.close(32), s_c.close(3), s_z.close(1)


def stage_positions(p, k, s):
    nc, d = p.nc, p.d
    s_ld, s_dve, s_pe = p.sig("load"), p.sig("dve_chain"), p.sig("pe_out")
    n = [0]
    with ExitStack() as ctx:
        keyf = f32(ctx, nc, "keyf", [SORT_P, SORT_J])
        tmp_i = i32(ctx, nc, "tmp_i", [SORT_P, SORT_J])
        dst_i = i32(ctx, nc, "dst_i", [SORT_P, SORT_J])
        src_i = i32(ctx, nc, "src_i", [SORT_P, SORT_J])
        typ_i = i32(ctx, nc, "typ_i", [SORT_P, SORT_J])
        eq = f32(ctx, nc, "eq", [SORT_P, 2, SORT_J])
        run = f32(ctx, nc, "run", [SORT_P, 2, SORT_J])
        one = f32(ctx, nc, "one", [SORT_P, SORT_J])
        posf = f32(ctx, nc, "posf", [SORT_P, SORT_J])
        cnt = f32(ctx, nc, "cnt", [SORT_P, NB])
        base = f32(ctx, nc, "base", [SORT_P, NB])
        tot_i = i32(ctx, nc, "tot_i", [P, NB])
        totf = f32(ctx, nc, "totf", [P, NB])
        unitf = f32(ctx, nc, "unitf", [P, NB])
        uend = f32(ctx, nc, "uend", [P, NB])
        pads = f32(ctx, nc, "pads", [P, NB])
        bmf = f32(ctx, nc, "bmf", [1, UNITS])
        ps = bank(ctx, nc, "ps")
        meta = s["meta"]
        with nc.Block() as block:
            @block.sync
            def _(sp):
                for t, name in ((dst_i, "dst"), (src_i, "src"), (typ_i, "edge_type_8")):
                    sp.dma_start(t[:], d[name].rearrange("(p j) -> p j", p=SORT_P)).then_inc(s_ld.sem, 16)
                sp.dma_start(one[:], d["edge_weight1"].rearrange("(p j) a -> p (j a)", p=SORT_P)).then_inc(s_ld.sem, 16)

            @block.tensor
            def _(pe):
                pe.wait_ge(p.sig("counts").sem, p.sig("counts").at(1))
                pe.matmul(ps[0:SORT_P, 0:NB], k["tri"][0:SORT_P, 0:SORT_P], cnt[:], start=True, stop=True)
                pe.matmul(ps[:, 32:32 + NB], k["ones"][0:SORT_P, 0:P], cnt[:], start=True, stop=True).then_inc(s_pe.sem, 1)

            @block.vector
            def _(dve):
                def chain(ins):
                    link(p, dve, s_dve, ins, n)
                dve.wait_ge(s_ld.sem, s_ld.at(64))
                chain(dve.tensor_copy(meta[:, :, 0], one[:]))
                chain(dve.tensor_scalar(tmp_i[:], dst_i[:], P - 1, None, ALU.bitwise_and))
                chain(dve.tensor_copy(meta[:, :, 1], tmp_i[:]))
                chain(dve.tensor_scalar(tmp_i[:], dst_i[:], 7, None, ALU.arith_shift_right))
                dve.tensor_copy(keyf[:], tmp_i[:])
                dve.tensor_copy(meta[:, :, 2], src_i[:])
                chain(dve.tensor_copy(posf[:], typ_i[:]))
                chain(dve.scalar_tensor_tensor(out=meta[:, :, 3], in0=meta[:, :, 2], scalar=float(N_REL),
                                               in1=posf[:], op0=ALU.mult, op1=ALU.add))
                dve.memset(one[:], 1.0)
                chain(dve.memset(posf[:], -1.0))
                for b in range(NB):
                    e, r = eq[:, b % 2, :], run[:, b % 2, :]
                    chain(dve.tensor_scalar(e, keyf[:], float(b), None, ALU.is_equal))
                    chain(dve.tensor_tensor_scan(r, one[:], e, 0.0, ALU.mult, ALU.add))
                    dve.tensor_copy(cnt[:, b:b + 1], r[:, SORT_J - 1:SORT_J])
                    chain(dve.tensor_tensor(e, e, r, ALU.mult))
                    chain(dve.tensor_tensor(posf[:], posf[:], e, ALU.add))
                dve.tensor_copy(base[0:1, 0:1], cnt[0:1, 0:1]).then_inc(p.sig("counts").sem, 1)
                dve.wait_ge(s_pe.sem, s_pe.at(1))
                chain(dve.tensor_scalar(totf[:], ps[:, 32:32 + NB], float(UNIT - 1), None, ALU.add))
                chain(dve.tensor_copy(tot_i[:], totf[:]))
                chain(dve.tensor_scalar(tot_i[:], tot_i[:], 8, None, ALU.arith_shift_right))
                chain(dve.tensor_copy(unitf[:], tot_i[:]))
                chain(dve.tensor_tensor_scan(uend[:], k["ones"][:, 0:NB], unitf[:], 0.0, ALU.mult, ALU.add))
                chain(dve.tensor_tensor(pads[:], uend[:], unitf[:], ALU.subtract))
                chain(dve.scalar_tensor_tensor(out=base[:], in0=pads[0:SORT_P, :], scalar=float(UNIT),
                                               in1=ps[0:SORT_P, 0:NB], op0=ALU.mult, op1=ALU.add))
                for b in range(NB):
                    e = eq[:, b % 2, :]
                    chain(dve.tensor_scalar(e, keyf[:], float(b), base[:, b:b + 1], ALU.is_equal, ALU.mult))
                    chain(dve.tensor_tensor(posf[:], posf[:], e, ALU.add))
                pos, part, tile = s["pos"], tmp_i, dst_i
                chain(dve.tensor_copy(pos[:], posf[:]))
                chain(dve.tensor_scalar(part[:], pos[:], P - 1, None, ALU.bitwise_and))
                chain(dve.tensor_scalar(part[:], part[:], 3, None, ALU.logical_shift_left))
                chain(dve.tensor_scalar(tile[:], pos[:], 7, GT - 1, ALU.arith_shift_right, ALU.bitwise_and))
                chain(dve.tensor_tensor(part[:], part[:], tile[:], ALU.bitwise_or))
                chain(dve.tensor_scalar(pos[:], pos[:], 10, None, ALU.arith_shift_right))
                chain(dve.tensor_scalar(pos[:], pos[:], 10, None, ALU.logical_shift_left))
                chain(dve.tensor_tensor(pos[:], pos[:], part[:], ALU.bitwise_or))
                chain(dve.memset(bmf[:], 0.0))
                for b in range(NB - 1):
                    chain(dve.scalar_tensor_tensor(out=bmf[:], in0=k["iota"][0:1, :], scalar=uend[0:1, b:b + 1],
                                                   in1=bmf[:], op0=ALU.is_ge, op1=ALU.add))
                dve.tensor_copy(k["bmap"][:], bmf[:])
        s_ld.close(64), s_dve.close(n[0]), s_pe.close(1), p.sig("counts").close(1)


SJ = 16
STEPS = SORT_J // SJ


def stage_scatter(p, k, s):
    nc, d = p.nc, p.d
    s_init, s_attr = p.sig("init"), [p.sig("attr0"), p.sig("attr1")]
    s_rec, s_idx, s_sc = p.sig("rec"), p.sig("idx"), [p.sig("scat0"), p.sig("scat1")]
    s_z = p.sig("zero")
    INIT = 8
    with ExitStack() as ctx:
        blank = f32(ctx, nc, "blank", [P, TILES // INIT, REC])
        attr = f32(ctx, nc, "attr", [SORT_P, 2, SJ * N_ATTR])
        rec = f32(ctx, nc, "rec", [SORT_P, 2, SJ, REC])
        idx = i32(ctx, nc, "idx", [SORT_P, 2, SJ])
        av = d["edge_attr_26"].rearrange("(p j) f -> p (j f)", p=SORT_P)
        W = SJ * N_ATTR
        with nc.Block() as block:
            @block.sync
            def _(sp):
                sp.wait_ge(s_z.sem, s_z.at(2))
                rv = d["records"].rearrange("(p c r) f -> c p (r f)", p=P, c=INIT)
                for c in range(INIT):
                    sp.dma_start(rv[c], blank[:].rearrange("p r f -> p (r f)")).then_inc(s_init.sem, 16)
                for q in range(2):
                    sp.dma_start(attr[:, q, :], av[:, q * W:(q + 1) * W]).then_inc(s_attr[q].sem, 16)
                with sp.Fori(1, STEPS // 2) as i:
                    for q in range(2):
                        sp.wait_ge(s_rec.sem, s_rec.at(2 * i + q - 1))
                        p.apart(sp)
                        sp.dma_start(attr[:, q, :], av[:, bass.ds((2 * i + q) * W, W)]).then_inc(s_attr[q].sem, 16)

            @block.scalar
            def _(act):
                act.wait_ge(s_z.sem, s_z.at(3))
                def body(i, first):
                    for q in range(2):
                        act.wait_ge(s_attr[q].sem, s_attr[q].at(16 * (i + 1)))
                        p.apart(act)
                        if not first:
                            act.wait_ge(s_sc[q].sem, s_sc[q].at(16 * SJ * i))
                            p.apart(act)
                        act.copy(rec[:, q, :, 0:N_ATTR],
                                 attr[:, q, :].rearrange("p (j f) -> p j f", f=N_ATTR)).then_inc(s_rec.sem, 1)
                body(0, True)
                with act.Fori(1, STEPS // 2) as i:
                    body(i, False)

            @block.vector
            def _(dve):
                dve.memset(blank[:], 0.0).then_inc(s_z.sem, 1)
                dve.wait_ge(s_z.sem, s_z.at(1))
                dve.memset(blank[:, :, F_DST:F_DST + 1], -1.0).then_inc(s_z.sem, 1)
                dve.memset(rec[:], 0.0).then_inc(s_z.sem, 1)
                dve.wait_ge(s_z.sem, s_z.at(3))
                def body(i, first):
                    for q in range(2):
                        j0 = (2 * i + q) * SJ
                        if not first:
                            dve.wait_ge(s_sc[q].sem, s_sc[q].at(16 * SJ * i))
                        dve.tensor_copy(rec[:, q, :, F_NORM:F_NORM + 4], s["meta"][:, bass.ds(j0, SJ), :])
                        dve.tensor_copy(idx[:, q, :], s["pos"][:, bass.ds(j0, SJ)]).then_inc(s_idx.sem, 1)
                body(0, True)
                with dve.Fori(1, STEPS // 2) as i:
                    body(i, False)

            @block.gpsimd
            def _(pool):
                pool.wait_ge(s_init.sem, s_init.at(16 * INIT))
                with pool.Fori(0, STEPS // 2) as i:
                    for q in range(2):
                        pool.wait_ge(s_rec.sem, s_rec.at(2 * i + q + 1))
                        p.apart(pool)
                        pool.wait_ge(s_idx.sem, s_idx.at(2 * i + q + 1))
                        p.apart(pool)
                        for j in range(SJ):
                            pool.indirect_dma_start(
                                out=d["records"], out_offset=bass.IndirectOffsetOnAxis(ap=idx[:, q, j:j + 1], axis=0),
                                in_=rec[:, q, j, :], in_offset=None).then_inc(s_sc[q].sem, 16)
                for q in range(2):
                    pool.wait_ge(s_sc[q].sem, s_sc[q].at(16 * SJ * (STEPS // 2)))
        s_z.close(3), s_init.close(16 * INIT), s_rec.close(STEPS), s_idx.close(STEPS)
        for q in range(2):
            s_attr[q].close(16 * (STEPS // 2)), s_sc[q].close(16 * SJ * (STEPS // 2))


def stage_reload(p, k):
    nc, d = p.nc, p.d
    s_rl, s_t, s_c = [p.sig("attr0"), p.sig("attr1")], p.sig("pe_out"), p.sig("turned")
    s_m, s_st = p.sig("dve_chain"), [p.sig("store0"), p.sig("store1")]
    with ExitStack() as ctx:
        buf = f32(ctx, nc, "rbuf", [P, 2, GT, REC])
        out = f32(ctx, nc, "rout", [P, 2, 2 * P])
        srcf = f32(ctx, nc, "srcf", [P, TILES])
        ps = [bank(ctx, nc, f"ps{q}") for q in range(2)]
        rv = d["records"].rearrange("(g p i) f -> p g (i f)", p=P, i=GT)
        with nc.Block() as block:
            @block.sync
            def _(sp):
                for q in range(2):
                    sp.dma_start(buf[:, q].rearrange("p i f -> p (i f)"), rv[:, q, :]).then_inc(s_rl[q].sem, 16)

                def store(i, q):
                    sp.wait_ge(s_c.sem, s_c.at(2 * i + q + 1))
                    p.apart(sp)
                    sp.dma_start(d["attr_t"][:, bass.ds((2 * i + q) * 2 * P, 2 * P)], out[:, q, :]).then_inc(s_st[q].sem, 16)
                with sp.Fori(0, BODIES - 1) as i:
                    for q in range(2):
                        store(i, q)
                        sp.wait_ge(s_m.sem, s_m.at(2 * i + q + 1))
                        p.apart(sp)
                        sp.wait_ge(s_t.sem, s_t.at(2 * i + q + 1))
                        p.apart(sp)
                        sp.dma_start(buf[:, q].rearrange("p i f -> p (i f)"),
                                     rv[:, bass.ds(2 * i + q + 2, 1), :].rearrange("p g f -> p (g f)")).then_inc(s_rl[q].sem, 16)
                for q in range(2):
                    store(BODIES - 1, q)
                for q in range(2):
                    sp.wait_ge(s_st[q].sem, s_st[q].at(16 * BODIES))

            @block.tensor
            def _(pe):
                def body(i, first):
                    for q in range(2):
                        pe.wait_ge(s_rl[q].sem, s_rl[q].at(16 * (i + 1)))
                        if not first:
                            pe.wait_ge(s_c.sem, s_c.at(2 * i + q - 1))
                        for h in range(2):
                            last = pe.transpose(ps[q][:, h * P:(h + 1) * P],
                                                buf[:, q, 4 * h:4 * h + 4, :].rearrange("p i f -> p (i f)"), k["ident"][:])
                        last.then_inc(s_t.sem, 1)
                body(0, True)
                with pe.Fori(1, BODIES) as i:
                    body(i, False)

            @block.scalar
            def _(act):
                def body(i, first):
                    for q in range(2):
                        act.wait_ge(s_t.sem, s_t.at(2 * i + q + 1))
                        p.apart(act)
                        if not first:
                            act.wait_ge(s_st[q].sem, s_st[q].at(16 * i))
                            p.apart(act)
                        act.copy(out[:, q, :], ps[q][:, 0:2 * P]).then_inc(s_c.sem, 1)
                body(0, True)
                with act.Fori(1, BODIES) as i:
                    body(i, False)

            @block.vector
            def _(dve):
                with dve.Fori(0, BODIES) as i:
                    for q in range(2):
                        dve.wait_ge(s_rl[q].sem, s_rl[q].at(16 * (i + 1)))
                        dve.tensor_copy(k["meta"][:, bass.ds((2 * i + q) * GT, GT), :],
                                        buf[:, q, :, F_NORM:F_NORM + 4]).then_inc(s_m.sem, 1)
                dve.wait_ge(s_m.sem, s_m.at(GROUPS))
                dve.tensor_copy(k["src"][:], k["meta"][:, :, 2])
                dve.tensor_copy(k["hwrow"][:], k["meta"][:, :, 3])
        s_t.close(GROUPS), s_c.close(GROUPS), s_m.close(GROUPS)
        for q in range(2):
            s_rl[q].close(16 * BODIES), s_st[q].close(16 * BODIES)


def norm_steps(dve, x, out, tmp, stat, chain, s_var):
    chain(dve.tensor_reduce(stat[:, 0, :], x[:], AX.X, ALU.add))
    chain(dve.tensor_scalar(stat[:, 0, :], stat[:, 0, :], 1.0 / D, None, ALU.mult))
    mean = stat[:, 0, :].unsqueeze(2).to_broadcast([P, NB, D])
    chain(dve.tensor_tensor(out[:], x[:], mean, ALU.subtract))
    chain(dve.tensor_tensor(tmp[:], out[:], out[:], ALU.mult))
    chain(dve.tensor_reduce(stat[:, 1, :], tmp[:], AX.X, ALU.add))
    dve.tensor_scalar(stat[:, 1, :], stat[:, 1, :], 1.0 / D, EPS, ALU.mult, ALU.add).then_inc(s_var.sem, 1)


def stage_norm(p, x, out, relu=True, gamma=None, beta=None):
    nc = p.nc
    s_dve, s_var, s_std = p.sig("dve_chain"), p.sig("var"), p.sig("std")
    n = [0]
    with ExitStack() as ctx:
        tmp = f32(ctx, nc, "ntmp", [P, NB, D])
        stat = f32(ctx, nc, "nstat", [P, 2, NB])
        with nc.Block() as block:
            @block.vector
            def _(dve):
                def chain(ins):
                    link(p, dve, s_dve, ins, n)
                norm_steps(dve, x, out, tmp, stat, chain, s_var)
                dve.wait_ge(s_std.sem, s_std.at(1))
                chain(dve.reciprocal(stat[:, 1, :], stat[:, 1, :]))
                rstd = stat[:, 1, :].unsqueeze(2).to_broadcast([P, NB, D])
                chain(dve.tensor_tensor(out[:], out[:], rstd, ALU.mult))
                if relu:
                    chain(dve.tensor_scalar(out[:], out[:], 0.0, None, ALU.max))
                if gamma is not None:
                    chain(dve.tensor_tensor(out[:], out[:], gamma.unsqueeze(1).to_broadcast([P, NB, D]), ALU.mult))
                    chain(dve.tensor_tensor(out[:], out[:], beta.unsqueeze(1).to_broadcast([P, NB, D]), ALU.add))

            @block.scalar
            def _(act):
                act.wait_ge(s_var.sem, s_var.at(1))
                act.activation(stat[:, 1, :], stat[:, 1, :], ACT.Sqrt).then_inc(s_std.sem, 1)
        s_dve.close(n[0]), s_var.close(1), s_std.close(1)


def stage_turn(p, k, h, ht):
    nc = p.nc
    s_pe, s_ev = p.sig("pe_out"), p.sig("turned")
    rounds = -(-NB // 4)
    with ExitStack() as ctx:
        ps = [bank(ctx, nc, f"pt{q}") for q in range(2)]
        with nc.Block() as block:
            @block.tensor
            def _(pe):
                for r in range(rounds):
                    if r >= 2:
                        pe.wait_ge(s_ev.sem, s_ev.at(r - 1))
                    for b in range(4 * r, min(NB, 4 * r + 4)):
                        last = pe.transpose(ps[r % 2][:, (b % 4) * P:(b % 4 + 1) * P], h[:, b, :], k["ident"][:])
                    last.then_inc(s_pe.sem, 1)

            @block.scalar
            def _(act):
                for r in range(rounds):
                    w = (min(NB, 4 * r + 4) - 4 * r) * P
                    act.wait_ge(s_pe.sem, s_pe.at(r + 1))
                    act.copy(ht[:, 4 * r * P:4 * r * P + w], ps[r % 2][:, 0:w]).then_inc(s_ev.sem, 1)
        s_pe.close(rounds), s_ev.close(rounds)


def stage_relation_table(p, k, ht):
    nc, d = p.nc, p.d
    s_ld, s_pe = p.sig("load"), p.sig("pe_out")
    s_a, s_v, s_st = p.sig("ev_act"), p.sig("ev_dve"), [p.sig("store0"), p.sig("store1")]
    tv = d["t_rel"].rearrange("(b p r) f -> b p (r f)", p=P, r=N_REL)
    with ExitStack() as ctx:
        w = f32(ctx, nc, "w0", [P, N_REL, D])
        row = f32(ctx, nc, "row0", [P, 2, N_REL * D])
        ps = [bank(ctx, nc, f"ph{q}") for q in range(4)]
        with nc.Block() as block:
            @block.sync
            def _(sp):
                sp.dma_start(w[:], d["L0_gnn_weight"].rearrange("r i o -> i r o")).then_inc(s_ld.sem, 16)
                for b in range(NB):
                    sp.wait_ge(s_a.sem, s_a.at(b + 1))
                    sp.wait_ge(s_v.sem, s_v.at(b + 1))
                    sp.dma_start(tv[b], row[:, b % 2, :]).then_inc(s_st[b % 2].sem, 16)
                for q in range(2):
                    sp.wait_ge(s_st[q].sem, s_st[q].at(16 * ((NB + 1 - q) // 2)))

            @block.tensor
            def _(pe):
                pe.wait_ge(s_ld.sem, s_ld.at(16))
                for b in range(NB):
                    if b >= 2:
                        pe.wait_ge(s_a.sem, s_a.at(b - 1))
                        pe.wait_ge(s_v.sem, s_v.at(b - 1))
                    for h in range(2):
                        last = pe.matmul(ps[2 * (b % 2) + h][:], ht[:, b * P:(b + 1) * P],
                                         w[:, 4 * h:4 * h + 4, :].rearrange("p r f -> p (r f)"), start=True, stop=True)
                    last.then_inc(s_pe.sem, 1)

            def evict(eng, copy, half, s_ev):
                for b in range(NB):
                    eng.wait_ge(s_pe.sem, s_pe.at(b + 1))
                    if b >= 2:
                        eng.wait_ge(s_st[b % 2].sem, s_st[b % 2].at(16 * (b // 2)))
                    copy(row[:, b % 2, 512 * half:512 * half + 512], ps[2 * (b % 2) + half][:]).then_inc(s_ev.sem, 1)

            @block.scalar
            def _(act):
                evict(act, act.copy, 0, s_a)

            @block.vector
            def _(dve):
                evict(dve, dve.tensor_copy, 1, s_v)
        s_ld.close(16), s_pe.close(NB), s_a.close(NB), s_v.close(NB)
        for q in range(2):
            s_st[q].close(16 * ((NB + 1 - q) // 2))


def stage_project(p, k, ht, loads, products, width, out):
    nc = p.nc
    s_ld, s_pe, s_ev = p.sig("load"), p.sig("pe_out"), p.sig("ev_act")
    with ExitStack() as ctx:
        ps = [bank(ctx, nc, f"pj{q}") for q in range(2)]
        with nc.Block() as block:
            @block.sync
            def _(sp):
                for dst, src in loads:
                    sp.dma_start(dst, src).then_inc(s_ld.sem, 16)

            @block.tensor
            def _(pe):
                if loads:
                    pe.wait_ge(s_ld.sem, s_ld.at(16 * len(loads)))
                for b in range(NB):
                    if b >= 2:
                        pe.wait_ge(s_ev.sem, s_ev.at(b - 1))
                    for m, (c0, c1, lhs, rhs) in enumerate(products):
                        last = pe.matmul(ps[b % 2][:, c0:c1], lhs(b), rhs, start=m == 0, stop=m == len(products) - 1)
                    last.then_inc(s_pe.sem, 1)

            @block.scalar
            def _(act):
                for b in range(NB):
                    act.wait_ge(s_pe.sem, s_pe.at(b + 1))
                    act.copy(out[:, b, 0:width], ps[b % 2][:, 0:width]).then_inc(s_ev.sem, 1)
        s_ld.close(16 * len(loads)), s_pe.close(NB), s_ev.close(NB)


def stage_store_rows(p, out_dram, rows):
    nc = p.nc
    s_st = p.sig("store0")
    with nc.Block() as block:
        @block.sync
        def _(sp):
            sp.dma_start(out_dram.rearrange("(b p) f -> p b f", p=P), rows).then_inc(s_st.sem, 16)
            sp.wait_ge(s_st.sem, s_st.at(16))
    s_st.close(16)


def over_bodies(eng, body):
    body(0, True, False)
    with eng.Fori(1, BODIES - 1) as i:
        body(i, False, False)
    body(BODIES - 1, False, True)


class Gather:

    def __init__(self, p, ctx, table, index, width):
        self.p, self.table, self.index, self.width = p, table, index, width
        self.rows = f32(ctx, p.nc, "rows", [P, 2, GT, width])
        self.idx = i32(ctx, p.nc, "gidx", [P, 2, GT])
        self.s_idx = p.sig("idx")
        self.s_row = [p.sig(f"row{u}") for u in range(BU)]

    def feed(self, act, g, q):
        act.copy(self.idx[:, q, :], self.index[:, bass.ds(g * GT, GT)]).then_inc(self.s_idx.sem, 1)

    def program(self, pool):
        p = self.p
        with pool.Fori(0, BODIES) as i:
            for q in range(2):
                pool.wait_ge(self.s_idx.sem, self.s_idx.at(2 * i + q + 1))
                p.apart(pool)
                for t in range(GT):
                    pool.indirect_dma_start(
                        out=self.rows[:, q, t, :], out_offset=None, in_=self.table,
                        in_offset=bass.IndirectOffsetOnAxis(ap=self.idx[:, q, t:t + 1], axis=0),
                    ).then_inc(self.s_row[GU * q + t // 2].sem, 16)

    def close(self):
        self.s_idx.close(GROUPS)
        for s in self.s_row:
            s.close(32 * BODIES)


def onehot(p, dve, k, oh, g, q):
    dst = k["meta"][:, bass.ds(g * GT, GT), 1:2].to_broadcast([P, GT, P])
    nodes = k["iota"][:, 0:P].unsqueeze(1).to_broadcast([P, GT, P])
    return dve.tensor_tensor(oh[:, q], nodes, dst, ALU.is_equal)


def stage_relation_sum(p, k, acc):
    nc, d = p.nc, p.d
    s_oh, s_sc, s_agg, s_acc = p.sig("onehot"), p.sig("scaled"), p.sig("agg"), p.sig("acc")
    s_z = p.sig("zero")
    with ExitStack() as ctx:
        ga = Gather(p, ctx, d["t_rel"], k["hwrow"], D)
        oh = f32(ctx, nc, "oh", [P, 2, GT, P])
        wr = f32(ctx, nc, "wr", [P, 2, GT, D])
        ps = [bank(ctx, nc, f"pa{q}") for q in range(2)]
        with nc.Block() as block:
            @block.gpsimd
            def _(pool):
                ga.program(pool)

            @block.scalar
            def _(act):
                ga.feed(act, 0, 0)

                def body(i, first, last):
                    for q in range(2):
                        g = 2 * i + q
                        if not (last and q == 1):
                            if not (first and q == 0):
                                act.wait_ge(s_sc.sem, s_sc.at(GT * g))
                                p.apart(act)
                            ga.feed(act, g + 1, 1 - q)
                        if not first:
                            act.wait_ge(s_agg.sem, s_agg.at(4 * g - 4))
                            p.apart(act)
                        for t in range(GT):
                            if t % 2 == 0:
                                act.wait_ge(ga.s_row[GU * q + t // 2].sem, ga.s_row[GU * q + t // 2].at(32 * (i + 1)))
                                p.apart(act)
                            act.activation(wr[:, q, t, :], ga.rows[:, q, t, :], ACT.Copy,
                                           scale=k["meta"][:, bass.ds(g * GT + t, 1), 0:1].rearrange("p a b -> p (a b)")
                                           ).then_inc(s_sc.sem, 1)
                over_bodies(act, body)

            @block.tensor
            def _(pe):
                def body(i, first, last):
                    for q in range(2):
                        g = 2 * i + q
                        for v in range(GU):
                            u = 4 * g + v
                            if v == 0:
                                pe.wait_ge(s_oh.sem, s_oh.at(g + 1))
                            pe.wait_ge(s_sc.sem, s_sc.at(2 * u + 2))
                            if not (first and q == 0 and v < 2):
                                pe.wait_ge(s_acc.sem, s_acc.at(u - 1))
                            o = ps[v % 2][:, 0:D]
                            for t in range(2):
                                mm = pe.matmul(o, oh[:, q, 2 * v + t, :], wr[:, q, 2 * v + t, :], start=t == 0, stop=t == 1)
                            mm.then_inc(s_agg.sem, 1)
                over_bodies(pe, body)

            @block.vector
            def _(dve):
                dve.memset(acc[:], 0.0).then_inc(s_z.sem, 1)
                onehot(p, dve, k, oh, 0, 0).then_inc(s_oh.sem, 1)
                dve.wait_ge(s_z.sem, s_z.at(1))

                def body(i, first, last):
                    for q in range(2):
                        g = 2 * i + q
                        for v in range(GU):
                            u = 4 * g + v
                            if v == 1 and not (last and q == 1):
                                if not (first and q == 0):
                                    dve.wait_ge(s_agg.sem, s_agg.at(4 * g))
                                onehot(p, dve, k, oh, g + 1, 1 - q).then_inc(s_oh.sem, 1)
                            b = dve.value_load(k["bmap"][0:1, bass.ds(u, 1)], min_val=0, max_val=NB - 1)
                            dve.wait_ge(s_agg.sem, s_agg.at(u + 1))
                            if not (first and q == 0 and v == 0):
                                dve.wait_ge(s_acc.sem, s_acc.at(u))
                            a = acc[:, bass.ds(b, 1), :].rearrange("p a f -> p (a f)")
                            dve.tensor_tensor(a, a, ps[v % 2][:, 0:D], ALU.add).then_inc(s_acc.sem, 1)
                over_bodies(dve, body)
        ga.close()
        s_z.close(1), s_oh.close(GROUPS), s_sc.close(TILES), s_agg.close(UNITS), s_acc.close(UNITS)


def stage_relation_add(p, k, acc):
    nc, d = p.nc, p.d
    s_ld, s_dve = p.sig("load"), p.sig("dve_chain")
    n = [0]
    with ExitStack() as ctx:
        bias = f32(ctx, nc, "b0", [P, D])
        with nc.Block() as block:
            @block.sync
            def _(sp):
                sp.dma_start(bias[:], d["L0_gnn_bias"].partition_broadcast(P)).then_inc(s_ld.sem, 16)

            @block.vector
            def _(dve):
                def chain(ins):
                    link(p, dve, s_dve, ins, n)
                dve.wait_ge(s_ld.sem, s_ld.at(16))
                chain(dve.tensor_tensor(acc[:], acc[:], bias[:].unsqueeze(1).to_broadcast([P, NB, D]), ALU.add))
                chain(dve.scalar_tensor_tensor(out=k["x"][:], in0=acc[:], scalar=0.0, in1=k["x"][:],
                                               op0=ALU.max, op1=ALU.add))
        s_ld.close(16), s_dve.close(n[0])



def turn_onehots(p, pe, k, oh, tp, q, g, first, s_turn, s_oht):
    for h in range(2):
        if not first:
            pe.wait_ge(s_oht.sem, s_oht.at(2 * g + h - 1))
        for t in range(4):
            mm = pe.transpose(tp[h][:, t * P:(t + 1) * P], oh[:, q, 4 * h + t, :], k["ident"][:])
        mm.then_inc(s_turn.sem, 1)


def stage_edge_mlp(p, k, r, pdst, acc, wc):
    nc, d = p.nc, p.d
    s_oh, s_turn, s_oht = p.sig("onehot"), p.sig("turn"), p.sig("oht")
    s_pre, s_add, s_relu = p.sig("pre"), p.sig("added"), p.sig("relu")
    s_agg, s_acc, s_z = p.sig("agg"), p.sig("acc"), p.sig("zero")
    s_at = [p.sig("attr0"), p.sig("attr1")]
    with ExitStack() as ctx:
        ga = Gather(p, ctx, d["t_mlp"], k["src"], MH)
        oh = f32(ctx, nc, "oh", [P, 2, GT, P])
        oht = f32(ctx, nc, "oht", [P, 2, GT, P])
        at = f32(ctx, nc, "at", [P, 2, 2, P])
        hs = f32(ctx, nc, "hs", [P, 2, 2, MH])
        h1 = f32(ctx, nc, "h1", [P, 2, 2, MH + 1])
        tp = [bank(ctx, nc, f"tp{q}") for q in range(2)]
        pp = [bank(ctx, nc, f"pp{q}") for q in range(2)]
        pa = [bank(ctx, nc, f"pa{q}") for q in range(2)]
        LAG = 2
        with nc.Block() as block:
            @block.gpsimd
            def _(pool):
                ga.program(pool)

            @block.sync
            def _(sp):
                for q in range(2):
                    sp.dma_start(at[:, q].rearrange("p a e -> p (a e)"), d["attr_t"][:, q * 2 * P:(q + 1) * 2 * P]).then_inc(s_at[q].sem, 16)
                with sp.Fori(0, BODIES - 1) as i:
                    for q in range(2):
                        sp.wait_ge(s_pre.sem, s_pre.at(4 * (2 * i + q + 1)))
                        p.apart(sp)
                        sp.dma_start(at[:, q].rearrange("p a e -> p (a e)"),
                                     d["attr_t"][:, bass.ds((2 * i + q + 2) * 2 * P, 2 * P)]).then_inc(s_at[q].sem, 16)

            @block.scalar
            def _(act):
                ga.feed(act, 0, 0)

                def body(i, first, last):
                    for q in range(2):
                        g = 2 * i + q
                        if not (last and q == 1):
                            if not (first and q == 0):
                                act.wait_ge(s_add.sem, s_add.at(4 * g))
                                p.apart(act)
                            ga.feed(act, g + 1, 1 - q)
                        if not first:
                            act.wait_ge(s_pre.sem, s_pre.at(4 * g - 4))
                            p.apart(act)
                        for h in range(2):
                            act.wait_ge(s_turn.sem, s_turn.at(2 * g + h + 1))
                            p.apart(act)
                            act.copy(oht[:, q, 4 * h:4 * h + 4, :].rearrange("p t n -> p (t n)"), tp[h][:]).then_inc(s_oht.sem, 1)
                        for v in range(GU):
                            u = 4 * g + v
                            act.wait_ge(s_add.sem, s_add.at(u + 1))
                            p.apart(act)
                            if not (first and q == 0 and v < 2):
                                act.wait_ge(s_agg.sem, s_agg.at(u - 1))
                                p.apart(act)
                            act.activation(h1[:, v % 2, :, 0:MH], hs[:, v % 2], ACT.Relu).then_inc(s_relu.sem, 1)
                over_bodies(act, body)

            @block.tensor
            def _(pe):
                def agg(u, w):
                    pe.wait_ge(s_relu.sem, s_relu.at(u + 1))
                    if not (isinstance(u, int) and u < 2):
                        pe.wait_ge(s_acc.sem, s_acc.at(u - 1))
                    for t in range(2):
                        mm = pe.matmul(pa[w % 2][:, 0:MH + 1], oh[:, w // GU, 2 * (w % GU) + t, :], h1[:, w % 2, t, :],
                                       start=t == 0, stop=t == 1)
                    mm.then_inc(s_agg.sem, 1)

                def body(i, first, last):
                    for q in range(2):
                        g = 2 * i + q
                        pe.wait_ge(s_oh.sem, s_oh.at(g + 1))
                        turn_onehots(p, pe, k, oh, tp, q, g, first and q == 0, s_turn, s_oht)
                        pe.wait_ge(s_at[q].sem, s_at[q].at(16 * (i + 1)))
                        for v in range(GU):
                            u, w = 4 * g + v, GU * q + v
                            b = pe.value_load(k["bmap"][0:1, bass.ds(u, 1)], min_val=0, max_val=NB - 1)
                            pe.wait_ge(s_oht.sem, s_oht.at(2 * g + v // 2 + 1))
                            if not (first and w < 2):
                                pe.wait_ge(s_add.sem, s_add.at(u - 1))
                            for t in range(2):
                                o = pp[v % 2][:, t * MH:(t + 1) * MH]
                                j = 2 * v + t
                                pe.matmul(o, at[:, q, j // 4, :], wc[:, j % 4, :], start=True, stop=False)
                                mm = pe.matmul(o, oht[:, q, j, :],
                                               pdst[:, bass.ds(b, 1), :].rearrange("p a f -> p (a f)"), start=False, stop=True)
                            mm.then_inc(s_pre.sem, 1)
                            if not (first and w < LAG):
                                agg(u - LAG, (w - LAG) % BU)
                over_bodies(pe, body)
                for u in range(UNITS - LAG, UNITS):
                    agg(u, u % BU)

            @block.vector
            def _(dve):
                dve.memset(acc[:], 0.0).then_inc(s_z.sem, 1)
                dve.memset(h1[:, :, :, MH:MH + 1], 1.0).then_inc(s_z.sem, 1)
                onehot(p, dve, k, oh, 0, 0).then_inc(s_oh.sem, 1)
                dve.wait_ge(s_z.sem, s_z.at(2))

                def add(u, w):
                    b = dve.value_load(k["bmap"][0:1, bass.ds(u, 1)], min_val=0, max_val=NB - 1)
                    dve.wait_ge(s_agg.sem, s_agg.at(u + 1))
                    if not (isinstance(u, int) and u == 0):
                        dve.wait_ge(s_acc.sem, s_acc.at(u))
                    a = acc[:, bass.ds(b, 1), 0:MH + 1].rearrange("p a f -> p (a f)")
                    dve.tensor_tensor(a, a, pa[w % 2][:, 0:MH + 1], ALU.add).then_inc(s_acc.sem, 1)

                def body(i, first, last):
                    for q in range(2):
                        g = 2 * i + q
                        for v in range(GU):
                            u, w = 4 * g + v, GU * q + v
                            dve.wait_ge(ga.s_row[w].sem, ga.s_row[w].at(32 * (i + 1)))
                            dve.wait_ge(s_pre.sem, s_pre.at(u + 1))
                            if not (first and w < 2):
                                dve.wait_ge(s_relu.sem, s_relu.at(u - 1))
                            dve.tensor_tensor(hs[:, v % 2].rearrange("p t f -> p (t f)"), pp[v % 2][:],
                                              ga.rows[:, q, 2 * v:2 * v + 2, :].rearrange("p t f -> p (t f)"),
                                              ALU.add).then_inc(s_add.sem, 1)
                            if not (first and w < LAG):
                                add(u - LAG, (w - LAG) % BU)
                            if v == 2 and not (last and q == 1):
                                if not (first and q == 0):
                                    dve.wait_ge(s_agg.sem, s_agg.at(4 * g))
                                onehot(p, dve, k, oh, g + 1, 1 - q).then_inc(s_oh.sem, 1)
                over_bodies(dve, body)
                for u in range(UNITS - LAG, UNITS):
                    add(u, u % BU)
        ga.close()
        s_z.close(2), s_oh.close(GROUPS), s_turn.close(2 * GROUPS), s_oht.close(2 * GROUPS)
        for s in (s_pre, s_add, s_relu, s_agg, s_acc):
            s.close(UNITS)
        for q in range(2):
            s_at[q].close(16 * BODIES)


def stage_fold(p, loads, products, out):
    nc = p.nc
    s_ld, s_pe, s_ev = p.sig("load"), p.sig("pe_out"), p.sig("ev_act")
    with ExitStack() as ctx:
        ps = [bank(ctx, nc, f"pf{q}") for q in range(2)]
        with nc.Block() as block:
            @block.sync
            def _(sp):
                for dst, src in loads:
                    sp.dma_start(dst, src).then_inc(s_ld.sem, 16)

            @block.tensor
            def _(pe):
                pe.wait_ge(s_ld.sem, s_ld.at(16 * len(loads)))
                for j, (o, pairs) in enumerate(products):
                    if j >= 2:
                        pe.wait_ge(s_ev.sem, s_ev.at(j - 1))
                    for m, (lhs, rhs) in enumerate(pairs):
                        last = pe.matmul(ps[j % 2][0:o.shape[0], 0:o.shape[1]], lhs, rhs,
                                         start=m == 0, stop=m == len(pairs) - 1)
                    last.then_inc(s_pe.sem, 1)

            @block.scalar
            def _(act):
                for j, (o, pairs) in enumerate(products):
                    act.wait_ge(s_pe.sem, s_pe.at(j + 1))
                    act.copy(o, ps[j % 2][0:o.shape[0], 0:o.shape[1]]).then_inc(s_ev.sem, 1)
        s_ld.close(16 * len(loads)), s_pe.close(len(products)), s_ev.close(len(products))


def stage_gates(p, k, sums, folded, tail, tail_w, ht, whh, rz, nn):
    nc = p.nc
    s_pe, s_ev, s_g, s_a, s_v = p.sig("turn"), p.sig("turned"), p.sig("pe_out"), p.sig("ev_act"), p.sig("ev_dve")
    chunks, nt = len(folded), tail_w.shape[0]
    with ExitStack() as ctx:
        tp = [bank(ctx, nc, f"gt{q}") for q in range(2)]
        tq = [bank(ctx, nc, f"gq{q}") for q in range(2)]
        ps = [bank(ctx, nc, f"gp{q}") for q in range(2)]
        st = f32(ctx, nc, "gst", [P, 2, chunks * P])
        tt = f32(ctx, nc, "gtt", [nt, 2, P])
        with nc.Block() as block:
            @block.tensor
            def _(pe):
                def turn(b):
                    if b >= 2:
                        pe.wait_ge(s_ev.sem, s_ev.at(b - 1))
                    for c in range(chunks):
                        pe.transpose(tp[b % 2][:, c * P:(c + 1) * P], sums(b, c), k["ident"][:])
                    pe.transpose(tq[b % 2][0:nt, 0:P], tail(b), k["ident"][:]).then_inc(s_pe.sem, 1)

                turn(0)
                for b in range(NB):
                    if b + 1 < NB:
                        turn(b + 1)
                    pe.wait_ge(s_ev.sem, s_ev.at(b + 1))
                    if b >= 2:
                        pe.wait_ge(s_a.sem, s_a.at(b - 1))
                        pe.wait_ge(s_v.sem, s_v.at(b - 1))
                    o = ps[b % 2]
                    pe.matmul(o[:], tt[:, b % 2, :], tail_w, start=True, stop=False)
                    for c in range(chunks):
                        pe.matmul(o[:, 0:G3], st[:, b % 2, c * P:(c + 1) * P], folded[c], start=False, stop=False)
                    hb = ht[:, b * P:(b + 1) * P]
                    pe.matmul(o[:, 0:2 * D], hb, whh[:, 0:2 * D], start=False, stop=False)
                    pe.matmul(o[:, G3:G3 + D], hb, whh[:, 2 * D:G3], start=False, stop=True).then_inc(s_g.sem, 1)

            @block.scalar
            def _(act):
                def copy(b):
                    act.wait_ge(s_pe.sem, s_pe.at(b + 1))
                    if b >= 2:
                        act.wait_ge(s_g.sem, s_g.at(b - 1))
                    act.copy(st[:, b % 2, :], tp[b % 2][:, 0:chunks * P])
                    act.copy(tt[:, b % 2, :], tq[b % 2][0:nt, 0:P]).then_inc(s_ev.sem, 1)

                copy(0)
                for b in range(NB):
                    if b + 1 < NB:
                        copy(b + 1)
                    act.wait_ge(s_g.sem, s_g.at(b + 1))
                    act.activation(rz[:, b, :], ps[b % 2][:, 0:2 * D], ACT.Sigmoid).then_inc(s_a.sem, 1)

            @block.vector
            def _(dve):
                for b in range(NB):
                    dve.wait_ge(s_a.sem, s_a.at(b + 1))
                    dve.tensor_copy(nn[:, b, :], ps[b % 2][:, 2 * D:4 * D]).then_inc(s_v.sem, 1)
        for s in (s_pe, s_ev, s_g, s_a, s_v):
            s.close(NB)


def stage_gru_end(p, rz, nn, h, extra=None):
    nc = p.nc
    s_dve, s_var, s_std = p.sig("dve_chain"), p.sig("var"), p.sig("std")
    n = [0]
    with nc.Block() as block:
        @block.vector
        def _(dve):
            def chain(ins):
                link(p, dve, s_dve, ins, n)
            r, z = rz[:, :, 0:D], rz[:, :, D:2 * D]
            ni, ns = nn[:, :, 0:D], nn[:, :, D:2 * D]
            chain(dve.tensor_tensor(ns, ns, r, ALU.mult))
            dve.tensor_tensor(ni, ni, ns, ALU.add).then_inc(s_var.sem, 1)
            dve.wait_ge(s_std.sem, s_std.at(1))
            chain(dve.tensor_tensor(h[:], h[:], ni, ALU.subtract))
            chain(dve.tensor_tensor(h[:], h[:], z, ALU.mult))
            chain(dve.tensor_tensor(h[:], h[:], ni, ALU.add))
            if extra is not None:
                chain(dve.tensor_tensor(extra[:], extra[:], h[:], ALU.add))

        @block.scalar
        def _(act):
            act.wait_ge(s_var.sem, s_var.at(1))
            act.activation(nn[:, :, 0:D], nn[:, :, 0:D], ACT.Tanh).then_inc(s_std.sem, 1)
    s_dve.close(n[0]), s_var.close(1), s_std.close(1)


def layer_relational(p, k):
    nc, d = p.nc, p.d
    stage_norm(p, k["x"], k["h"])
    with ExitStack() as ctx:
        ht = f32(ctx, nc, "ht", [P, NPAD])
        stage_turn(p, k, k["h"], ht)
        stage_relation_table(p, k, ht)
    with ExitStack() as ctx:
        acc = f32(ctx, nc, "acc", [P, NB, D])
        stage_relation_sum(p, k, acc)
        stage_relation_add(p, k, acc)


def layer_edge_mlp(p, k, rounds=2):
    nc, d = p.nc, p.d
    stage_norm(p, k["x"], k["h"])
    for r in range(rounds):
        with ExitStack() as ctx:
            ht = f32(ctx, nc, "ht", [P, NPAD])
            pdst = f32(ctx, nc, "pdst", [P, NB, MH])
            acc = f32(ctx, nc, "acc", [P, NB, MH + 3])
            w1 = f32(ctx, nc, "w1", [P, 2, MH])
            b1 = f32(ctx, nc, "b1", [1, MH])
            wc = f32(ctx, nc, "wc", [P, 4, MH])
            with nc.Block() as block:
                @block.vector
                def _(dve):
                    dve.memset(wc[:], 0.0)
            stage_turn(p, k, k["h"], ht)
            w1d = d["L1_gnn_mlp_w1"][r]
            def lhs(b):
                return ht[:, b * P:(b + 1) * P]
            stage_project(p, k, ht, [(w1[:], w1d[0:2 * D, :].rearrange("(a i) o -> i a o", a=2)),
                                     (b1[:], d["L1_gnn_mlp_b1"][r:r + 1, :])] +
                          [(wc[32 * j:32 * j + N_ATTR, j, :], w1d[2 * D:2 * D + N_ATTR, :]) for j in range(4)],
                          [(0, MH, lhs, w1[:, 1, :])], MH, pdst)
            stage_store_rows(p, d["t_mlp"], pdst[:])
            stage_project(p, k, ht, [], [(0, MH, lhs, w1[:, 0, :]), (0, MH, lambda b: k["ones"][0:1, 0:P], b1[:])], MH, pdst)
            stage_edge_mlp(p, k, r, pdst, acc, wc)
            with ExitStack() as c2:
                w2t = f32(c2, nc, "w2t", [P, 2, MH])
                wih = f32(c2, nc, "wih", [P, 2, G3])
                whh = f32(c2, nc, "whh", [P, G3])
                b2 = f32(c2, nc, "b2", [P, 2])
                fold = f32(c2, nc, "fold", [P, 2, G3])
                tail = f32(c2, nc, "tail", [3, 4 * D])
                nn = f32(c2, nc, "nn", [P, NB, 2 * D])
                with nc.Block() as block:
                    @block.vector
                    def _(dve):
                        dve.memset(tail[:], 0.0)
                        dve.memset(acc[:, :, MH + 1:MH + 3], 1.0)
                stage_fold(p, [(w2t[:], d["w2_t"][r].rearrange("(c p) m -> p c m", p=P)),
                               (wih[:], d["wih_t"][r].rearrange("(c p) g -> p c g", p=P)),
                               (whh[:], d["whh_t"][r]),
                               (b2[:], d["b2_c"][r]),
                               (tail[1:2, 0:G3], d["L1_gnn_gru_bih"][r:r + 1, :]),
                               (tail[2:3, 0:2 * D], d["L1_gnn_gru_bhh"][r:r + 1, 0:2 * D]),
                               (tail[2:3, G3:4 * D], d["L1_gnn_gru_bhh"][r:r + 1, 2 * D:G3])],
                           [(fold[:, m, :], [(w2t[:, c, m * P:(m + 1) * P], wih[:, c, :]) for c in range(2)]) for m in range(2)]
                           + [(tail[0:1, 0:G3], [(b2[:, c:c + 1], wih[:, c, :]) for c in range(2)])], None)
                stage_gates(p, k, lambda b, c: acc[:, b, c * P:(c + 1) * P], [fold[:, c, :] for c in range(2)],
                            lambda b: acc[:, b, MH:MH + 3], tail[:], ht, whh[:], pdst, nn)
                stage_gru_end(p, pdst, nn, k["h"], k["x"] if r == rounds - 1 else None)



SC = 4 * HEADS
MASKED = -BIG


def stage_attention_constants(p, a):
    nc = p.nc
    s_c, s_d = p.sig("const"), p.sig("dve_chain")
    n = [0]
    with ExitStack() as ctx:
        row = i32(ctx, nc, "row", [P, 1])
        ri = i32(ctx, nc, "ri", [P, 3])
        rf = f32(ctx, nc, "rf", [P, 3])
        ts = f32(ctx, nc, "ts", [P, GT])
        with nc.Block() as block:
            @block.gpsimd
            def _(pool):
                pool.iota(row[:], pattern=[[0, 1]], base=0, channel_multiplier=1).then_inc(s_c.sem, 1)

            @block.vector
            def _(dve):
                def chain(ins):
                    link(p, dve, s_d, ins, n)
                dve.wait_ge(s_c.sem, s_c.at(1))
                dve.tensor_scalar(ri[:, 0:1], row[:], 3, None, ALU.bitwise_and)
                dve.tensor_scalar(ri[:, 1:2], row[:], SC - 1, None, ALU.bitwise_and)
                chain(dve.tensor_scalar(ri[:, 2:3], row[:], 4, None, ALU.arith_shift_right))
                chain(dve.tensor_copy(rf[:], ri[:]))
                chain(dve.tensor_scalar(rf[:, 1:2], rf[:, 1:2], float(HEADS), None, ALU.is_ge))
                dve.tensor_scalar(a["head"][:], a["iota"][:, 0:HEADS], rf[:, 0:1], rf[:, 1:2], ALU.is_equal, ALU.mult)
                chain(dve.tensor_scalar(ts[:], a["iota"][:, 0:GT], rf[:, 2:3], None, ALU.is_equal))
                dve.tensor_copy(a["tile"][:], ts[:].unsqueeze(2).to_broadcast([P, GT, P]))
                for h in range(HEADS):
                    dve.tensor_scalar(a["masked"][:, h, :], a["ident"][:], MASKED, None, ALU.mult)
        s_c.close(1), s_d.close(n[0])


def stage_score_table(p, score, table):
    nc = p.nc
    s_dve, s_st = p.sig("dve_chain"), p.sig("store0")
    n = [0]
    with ExitStack() as ctx:
        row = f32(ctx, nc, "srow", [P, NB, SC])
        half = ctx.enter_context(nc.sbuf_tensor(unique("half"), [P, NB, HEADS], mybir.dt.bfloat16))
        left = f32(ctx, nc, "left", [P, NB, HEADS])
        with nc.Block() as block:
            @block.vector
            def _(dve):
                def chain(ins):
                    link(p, dve, s_dve, ins, n)
                chain(dve.tensor_copy(row[:, :, 0:HEADS], score))
                chain(dve.tensor_copy(left[:], score))
                for part in range(1, 4):
                    out = row[:, :, part * HEADS:(part + 1) * HEADS]
                    chain(dve.tensor_copy(half[:], left[:]))
                    chain(dve.tensor_copy(out, half[:]))
                    chain(dve.tensor_tensor(left[:], left[:], out, ALU.subtract))

            @block.sync
            def _(sp):
                sp.wait_ge(s_dve.sem, s_dve.at(n[0]))
                sp.dma_start(table.rearrange("(b p) f -> p b f", p=P), row[:]).then_inc(s_st.sem, 16)
                sp.wait_ge(s_st.sem, s_st.at(16))
        s_dve.close(n[0]), s_st.close(16)


def stage_edge_max(p, k, a, score, mx):
    nc, d = p.nc, p.d
    BF = mybir.dt.bfloat16
    s_oh, s_turn, s_spread = p.sig("onehot"), p.sig("turn"), p.sig("spread")
    s_bank, s_red, s_max, s_se = p.sig("pre"), p.sig("added"), p.sig("acc"), p.sig("scaled")
    with ExitStack() as ctx:
        ga = Gather(p, ctx, d["t_score"], k["src"], SC)
        away = ctx.enter_context(nc.sbuf_tensor(unique("away"), [P, 2, GT, P], BF))
        spread = ctx.enter_context(nc.sbuf_tensor(unique("spread"), [P, 2, HEADS, P], BF))
        tmax = f32(ctx, nc, "tmax", [P, 2, HEADS])
        tb = [bank(ctx, nc, f"tb{q}") for q in range(2)]
        vb = ctx.enter_context(nc.psum_tensor(unique("vb"), [P, 4, 512], F32))
        with nc.Block() as block:
            @block.gpsimd
            def _(pool):
                ga.program(pool)

            @block.scalar
            def _(act):
                ga.feed(act, 0, 0)

                def body(i, first, last):
                    for q in range(2):
                        g = 2 * i + q
                        if not (last and q == 1):
                            if not (first and q == 0):
                                act.wait_ge(s_se.sem, s_se.at(g))
                                p.apart(act)
                                act.wait_ge(s_turn.sem, s_turn.at(g))
                                p.apart(act)
                            ga.feed(act, g + 1, 1 - q)
                        for v in range(GU):
                            act.wait_ge(ga.s_row[GU * q + v].sem, ga.s_row[GU * q + v].at(32 * (i + 1)))
                            p.apart(act)
                        act.copy(score[:, bass.ds(g * GT, GT), :], ga.rows[:, q, :, 0:HEADS]).then_inc(s_se.sem, 1)
                over_bodies(act, body)

            @block.tensor
            def _(pe):
                def turn(i, g, q, first):
                    for v in range(GU):
                        pe.wait_ge(ga.s_row[GU * q + v].sem, ga.s_row[GU * q + v].at(32 * (i + 1)))
                    if not first:
                        pe.wait_ge(s_spread.sem, s_spread.at(g - 1))
                    pe.transpose(tb[q][:, 0:P], ga.rows[:, q].rearrange("p t c -> p (t c)"), k["ident"][:]).then_inc(s_turn.sem, 1)
                turn(0, 0, 0, True)

                def body(i, first, last):
                    for q in range(2):
                        g = 2 * i + q
                        pe.wait_ge(s_oh.sem, s_oh.at(g + 1))
                        pe.wait_ge(s_spread.sem, s_spread.at(g + 1))
                        for v in range(GU):
                            u = 4 * g + v
                            if not (first and q == 0 and v < 2):
                                pe.wait_ge(s_red.sem, s_red.at(u - 1))
                            for t in range(2):
                                o, j = vb[:, 2 * (v % 2) + t, :], 2 * v + t
                                pe.matmul(o, away[:, q, j, :], a["masked"][:].rearrange("p h e -> p (h e)"), start=True, stop=False)
                                mm = pe.matmul(o, a["tile"][:, j, :], spread[:, q].rearrange("p h e -> p (h e)"), start=False, stop=True)
                            mm.then_inc(s_bank.sem, 1)
                            if v == 2 and not (last and q == 1):
                                turn(i + q, g + 1, 1 - q, first and q == 0)
                over_bodies(pe, body)

            @block.vector
            def _(dve):
                def masks(g, q):
                    dst = k["meta"][:, bass.ds(g * GT, GT), 1:2].to_broadcast([P, GT, P])
                    nodes = k["iota"][:, 0:P].unsqueeze(1).to_broadcast([P, GT, P])
                    dve.tensor_tensor(away[:, q], nodes, dst, ALU.not_equal).then_inc(s_oh.sem, 1)

                def parts(g, q):
                    dve.wait_ge(s_turn.sem, s_turn.at(g + 1))
                    dve.tensor_tensor(spread[:, q], tb[q][:, 0:P].unsqueeze(1).to_broadcast([P, HEADS, P]),
                                      a["head"][:].unsqueeze(2).to_broadcast([P, HEADS, P]), ALU.mult).then_inc(s_spread.sem, 1)
                masks(0, 0)
                parts(0, 0)

                def body(i, first, last):
                    for q in range(2):
                        g = 2 * i + q
                        for v in range(GU):
                            u = 4 * g + v
                            b = dve.value_load(k["bmap"][0:1, bass.ds(u, 1)], min_val=0, max_val=NB - 1)
                            dve.wait_ge(s_bank.sem, s_bank.at(u + 1))
                            dve.tensor_reduce(tmax[:, v % 2, :], vb[:, 2 * (v % 2):2 * (v % 2) + 2, :].rearrange("p t (h e) -> p h t e", h=HEADS),
                                              AX.XY, ALU.max).then_inc(s_red.sem, 1)
                            if v == 1 and not (last and q == 1):
                                if not (first and q == 0):
                                    dve.wait_ge(s_bank.sem, s_bank.at(4 * g))
                                masks(g + 1, 1 - q)
                            if v == 3 and not (last and q == 1):
                                parts(g + 1, 1 - q)
                            dve.wait_ge(s_red.sem, s_red.at(u + 1))
                            if not (first and q == 0 and v == 0):
                                dve.wait_ge(s_max.sem, s_max.at(u))
                            m = mx[:, bass.ds(b, 1), :].rearrange("p a h -> p (a h)")
                            dve.tensor_tensor(m, m, tmax[:, v % 2, :], ALU.max).then_inc(s_max.sem, 1)
                over_bodies(dve, body)
        ga.close()
        for s in (s_oh, s_turn, s_spread, s_se):
            s.close(GROUPS)
        for s in (s_bank, s_red, s_max):
            s.close(UNITS)


def stage_shift(p, k, sd, mx, adm, ss=None, xw=None, acc=None):
    nc = p.nc
    s_dve, s_var, s_std = p.sig("dve_chain"), p.sig("var"), p.sig("std")
    n = [0]
    with ExitStack() as ctx:
        t = f32(ctx, nc, "shift", [P, NB, HEADS])
        e = f32(ctx, nc, "self", [P, NB, HEADS])
        with nc.Block() as block:
            @block.vector
            def _(dve):
                def chain(ins):
                    link(p, dve, s_dve, ins, n)
                ad, m = adm[:, :, 0:HEADS], adm[:, :, HEADS:2 * HEADS]
                chain(dve.tensor_copy(ad, sd))
                chain(dve.tensor_tensor(t[:], mx[:], ad, ALU.add))
                chain(dve.scalar_tensor_tensor(out=m, in0=t[:], scalar=SLOPE, in1=t[:], op0=ALU.mult, op1=ALU.max))
                if ss is not None:
                    chain(dve.tensor_tensor(e[:], ss, ad, ALU.add))
                    chain(dve.scalar_tensor_tensor(out=t[:], in0=e[:], scalar=SLOPE, in1=e[:], op0=ALU.mult, op1=ALU.max))
                    dve.tensor_tensor(e[:], t[:], m, ALU.subtract).then_inc(s_var.sem, 1)
                    dve.wait_ge(s_std.sem, s_std.at(1))
                    den = acc[:, :, D:D + HEADS]
                    chain(dve.tensor_copy(den, e[:]))
                    c = D // HEADS
                    for h in range(HEADS):
                        chain(dve.tensor_tensor(acc[:, :, h * c:(h + 1) * c], xw[:, :, h * c:(h + 1) * c],
                                                e[:, :, h:h + 1].to_broadcast([P, NB, c]), ALU.mult))
                else:
                    chain(dve.memset(acc[:], 0.0))

            if ss is not None:
                @block.scalar
                def _(act):
                    act.wait_ge(s_var.sem, s_var.at(1))
                    act.activation(e[:], e[:], ACT.Exp).then_inc(s_std.sem, 1)
        s_dve.close(n[0])
        if ss is not None:
            s_var.close(1), s_std.close(1)


def stage_attend(p, k, table, score, adm, acc, wide):
    nc = p.nc
    W = HEADS * D if wide else D
    s_oh, s_turn, s_oht = p.sig("onehot"), p.sig("turn"), p.sig("oht")
    s_em, s_z, s_w, s_c = p.sig("pre"), p.sig("added"), p.sig("relu"), p.sig("dve_chain")
    s_rd, s_ra, s_agg, s_acc = p.sig("scaled"), p.sig("spread"), p.sig("agg"), p.sig("acc")
    DH = HEADS // 2
    with ExitStack() as ctx:
        ga = Gather(p, ctx, table, k["src"], D)
        oh = f32(ctx, nc, "oh", [P, 2, GT, P])
        oht = f32(ctx, nc, "oht", [P, 2, GT, P])
        z = f32(ctx, nc, "z", [P, 2, GT, HEADS])
        y = f32(ctx, nc, "y", [P, 2, GT, HEADS])
        w = f32(ctx, nc, "w", [P, 2, GT, HEADS])
        wr = f32(ctx, nc, "wr", [P, 2, 2, W])
        tp = [bank(ctx, nc, f"tp{q}") for q in range(2)]
        em = [bank(ctx, nc, f"em{q}") for q in range(2)]
        pa = [bank(ctx, nc, f"pa{q}") for q in range(2)]
        pd = [bank(ctx, nc, f"pd{q}") for q in range(2)] if wide else None
        with nc.Block() as block:
            @block.gpsimd
            def _(pool):
                ga.program(pool)

            @block.scalar
            def _(act):
                def turned(g, q, first):
                    if not first:
                        act.wait_ge(s_em.sem, s_em.at(g - 1))
                        p.apart(act)
                    for h in range(2):
                        act.wait_ge(s_turn.sem, s_turn.at(2 * g + h + 1))
                        p.apart(act)
                        act.copy(oht[:, q, 4 * h:4 * h + 4, :].rearrange("p t n -> p (t n)"), tp[h][:]).then_inc(s_oht.sem, 1)

                def weights(g, q):
                    act.wait_ge(s_z.sem, s_z.at(g + 1))
                    p.apart(act)
                    act.activation(w[:, q], z[:, q], ACT.Exp).then_inc(s_w.sem, 1)
                ga.feed(act, 0, 0)
                turned(0, 0, True)
                weights(0, 0)

                def body(i, first, last):
                    for q in range(2):
                        g = 2 * i + q
                        if not (last and q == 1):
                            if not (first and q == 0):
                                act.wait_ge(s_rd.sem, s_rd.at(4 * g))
                                p.apart(act)
                            ga.feed(act, g + 1, 1 - q)
                        for v in range(GU):
                            u = 4 * g + v
                            if wide:
                                if v == 0:
                                    act.wait_ge(s_w.sem, s_w.at(g + 1))
                                    p.apart(act)
                                act.wait_ge(ga.s_row[GU * q + v].sem, ga.s_row[GU * q + v].at(32 * (i + 1)))
                                p.apart(act)
                                if not (first and q == 0 and v < 2):
                                    act.wait_ge(s_agg.sem, s_agg.at(u - 1))
                                    p.apart(act)
                                for t in range(2):
                                    j = 2 * v + t
                                    for h in range(DH, HEADS):
                                        last_i = act.activation(wr[:, v % 2, t, h * D:(h + 1) * D], ga.rows[:, q, j, :], ACT.Copy,
                                                                scale=w[:, q, j, h:h + 1])
                                last_i.then_inc(s_ra.sem, 1)
                            if v == 1 and not (last and q == 1):
                                turned(g + 1, 1 - q, first and q == 0)
                        if not (last and q == 1):
                            weights(g + 1, 1 - q)
                over_bodies(act, body)

            @block.tensor
            def _(pe):
                def turn(g, q, first):
                    pe.wait_ge(s_oh.sem, s_oh.at(g + 1))
                    turn_onehots(p, pe, k, oh, tp, q, g, first, s_turn, s_oht)

                def values(g, q, first):
                    if not first:
                        pe.wait_ge(s_z.sem, s_z.at(g - 1))
                    for v in range(GU):
                        b = pe.value_load(k["bmap"][0:1, bass.ds(4 * g + v, 1)], min_val=0, max_val=NB - 1)
                        if v % 2 == 0:
                            pe.wait_ge(s_oht.sem, s_oht.at(2 * g + v // 2 + 1))
                        for t in range(2):
                            j = 2 * v + t
                            mm = pe.matmul(em[q][:, 8 * j:8 * j + 8], oht[:, q, j, :],
                                           adm[:, bass.ds(b, 1), :].rearrange("p a f -> p (a f)"), start=True, stop=True)
                    mm.then_inc(s_em.sem, 1)
                turn(0, 0, True)
                values(0, 0, True)

                def body(i, first, last):
                    for q in range(2):
                        g = 2 * i + q
                        for v in range(GU):
                            u = 4 * g + v
                            pe.wait_ge(s_rd.sem, s_rd.at(u + 1))
                            if v == 0:
                                pe.wait_ge(s_w.sem, s_w.at(g + 1))
                            if wide:
                                pe.wait_ge(s_ra.sem, s_ra.at(u + 1))
                            if not (first and q == 0 and v < 2):
                                pe.wait_ge(s_acc.sem, s_acc.at(u - 1))
                            for t in range(2):
                                j = 2 * v + t
                                pe.matmul(pa[v % 2][:, 0:W], oh[:, q, j, :], wr[:, v % 2, t, :], start=t == 0, stop=t == 1,
                                          skip_group_check=True)
                                den = pd[v % 2][:, 0:HEADS] if wide else pa[v % 2][:, W:W + HEADS]
                                mm = pe.matmul(den, oh[:, q, j, :], w[:, q, j, :], start=wide and t == 0, stop=t == 1,
                                               skip_group_check=True)
                            mm.then_inc(s_agg.sem, 1)
                            if v == 0 and not (last and q == 1):
                                turn(g + 1, 1 - q, first and q == 0)
                            if v == 1 and not (last and q == 1):
                                values(g + 1, 1 - q, first and q == 0)
                over_bodies(pe, body)

            @block.vector
            def _(dve):
                def onehots(g, q):
                    onehot(p, dve, k, oh, g, q).then_inc(s_oh.sem, 1)

                def exponents(g, q, first):
                    dve.wait_ge(s_em.sem, s_em.at(g + 1))
                    if not first:
                        dve.wait_ge(s_w.sem, s_w.at(g - 1))
                    e = em[q][:, 0:8 * GT].rearrange("p (t f) -> p t f", t=GT)
                    dve.tensor_tensor(y[:, q], e[:, :, 0:HEADS], score[:, bass.ds(g * GT, GT), :], ALU.add).then_inc(s_c.sem, 1)
                    dve.wait_ge(s_c.sem, s_c.at(2 * g + 1))
                    dve.scalar_tensor_tensor(out=y[:, q], in0=y[:, q], scalar=SLOPE, in1=y[:, q],
                                             op0=ALU.mult, op1=ALU.max).then_inc(s_c.sem, 1)
                    dve.wait_ge(s_c.sem, s_c.at(2 * g + 2))
                    dve.tensor_tensor(z[:, q], y[:, q], e[:, :, HEADS:2 * HEADS], ALU.subtract).then_inc(s_z.sem, 1)

                def add(u, x):
                    b = dve.value_load(k["bmap"][0:1, bass.ds(u, 1)], min_val=0, max_val=NB - 1)
                    dve.wait_ge(s_agg.sem, s_agg.at(u + 1))
                    if not (isinstance(u, int) and u == 0):
                        dve.wait_ge(s_acc.sem, s_acc.at(u))
                    n = W if wide else W + HEADS
                    a = acc[:, bass.ds(b, 1), 0:n].rearrange("p a f -> p (a f)")
                    if wide:
                        c = acc[:, bass.ds(b, 1), W:W + HEADS].rearrange("p a f -> p (a f)")
                        dve.tensor_tensor(c, c, pd[x % 2][:, 0:HEADS], ALU.add)
                    dve.tensor_tensor(a, a, pa[x % 2][:, 0:n], ALU.add).then_inc(s_acc.sem, 1)

                onehots(0, 0)
                exponents(0, 0, True)

                def body(i, first, last):
                    for q in range(2):
                        g = 2 * i + q
                        for v in range(GU):
                            u, x = 4 * g + v, GU * q + v
                            dve.wait_ge(ga.s_row[x].sem, ga.s_row[x].at(32 * (i + 1)))
                            if v == 0:
                                dve.wait_ge(s_w.sem, s_w.at(g + 1))
                            if not (first and x < 2):
                                dve.wait_ge(s_agg.sem, s_agg.at(u - 1))
                            for t in range(2):
                                j = 2 * v + t
                                if wide:
                                    last_i = dve.tensor_tensor(wr[:, v % 2, t, 0:DH * D].rearrange("p (h f) -> p h f", h=DH),
                                                               ga.rows[:, q, j, :].unsqueeze(1).to_broadcast([P, DH, D]),
                                                               w[:, q, j, 0:DH].unsqueeze(2).to_broadcast([P, DH, D]), ALU.mult)
                                else:
                                    last_i = dve.tensor_tensor(wr[:, v % 2, t, :].rearrange("p (h f) -> p h f", h=HEADS),
                                                               ga.rows[:, q, j, :].rearrange("p (h f) -> p h f", h=HEADS),
                                                               w[:, q, j, :].unsqueeze(2).to_broadcast([P, HEADS, D // HEADS]), ALU.mult)
                            last_i.then_inc(s_rd.sem, 1)
                            if not (first and x == 0):
                                add(u - 1, (x - 1) % BU)
                            if v == 0 and not (last and q == 1):
                                if not (first and q == 0):
                                    dve.wait_ge(s_agg.sem, s_agg.at(4 * g))
                                onehots(g + 1, 1 - q)
                            if v == 2 and not (last and q == 1):
                                exponents(g + 1, 1 - q, first and q == 0)
                over_bodies(dve, body)
                add(UNITS - 1, BU - 1)
        ga.close()
        s_oh.close(GROUPS), s_turn.close(2 * GROUPS), s_oht.close(2 * GROUPS), s_c.close(2 * GROUPS)
        for s in (s_em, s_z, s_w):
            s.close(GROUPS)
        for s in (s_rd, s_agg, s_acc):
            s.close(UNITS)
        if wide:
            s_ra.close(UNITS)


def stage_vector(p, loads, steps):
    nc = p.nc
    s_ld, s_dve = p.sig("load"), p.sig("dve_chain")
    n = [0]
    with nc.Block() as block:
        @block.sync
        def _(sp):
            for dst, src in loads:
                sp.dma_start(dst, src).then_inc(s_ld.sem, 16)

        @block.vector
        def _(dve):
            if loads:
                dve.wait_ge(s_ld.sem, s_ld.at(16 * len(loads)))
            for step in steps:
                link(p, dve, s_dve, step(dve), n)
    s_ld.close(16 * len(loads)), s_dve.close(n[0])


def layer_attention(p, k):
    nc, d = p.nc, p.d
    BF = mybir.dt.bfloat16
    stage_norm(p, k["x"], k["h"])
    with ExitStack() as ctx:
        acc = f32(ctx, nc, "acc", [P, NB, D + HEADS])
        skip = f32(ctx, nc, "skip", [P, NB, D])
        xw = f32(ctx, nc, "xw", [P, NB, D])
        sc = f32(ctx, nc, "sc", [P, 2, NB, HEADS])
        mx = f32(ctx, nc, "mx", [P, NB, HEADS])
        adm = f32(ctx, nc, "adm", [P, NB, 2 * HEADS])
        with ExitStack() as c2:
            ht = f32(c2, nc, "ht", [P, NPAD])
            xn = f32(c2, nc, "xn", [P, NB, D])
            w = f32(c2, nc, "w2", [P, 2, D])
            bp = f32(c2, nc, "bp", [1, D])
            gb = f32(c2, nc, "gb", [P, 4, D])
            tmp = f32(c2, nc, "stmp", [P, NB, D])

            def lhs(b):
                return ht[:, b * P:(b + 1) * P]
            stage_turn(p, k, k["h"], ht)
            stage_project(p, k, ht, [(w[:, 0, :], d["L2_gnn_W_proj"]), (w[:, 1, :], d["L2_gnn_W_gat"]),
                                     (bp[:], d["L2_gnn_b_proj"].rearrange("(a f) -> a f", a=1))] +
                          [(gb[:, j, :], v.partition_broadcast(P)) for j, v in enumerate(
                              (d["L2_gnn_gamma"], d["L2_gnn_beta"], d["L2_gnn_att_src"].rearrange("h c -> (h c)"),
                               d["L2_gnn_att_dst"].rearrange("h c -> (h c)")))],
                          [(0, D, lhs, w[:, 0, :]), (0, D, lambda b: k["ones"][0:1, 0:P], bp[:])], D, skip)
            stage_norm(p, k["h"], xn, relu=False, gamma=gb[:, 0, :], beta=gb[:, 1, :])
            stage_turn(p, k, xn, ht)
            stage_project(p, k, ht, [], [(0, D, lhs, w[:, 1, :])], D, xw)
            stage_store_rows(p, d["t_att"], xw[:])
            steps = []
            for j in range(2):
                steps.append(lambda dve, j=j: dve.tensor_tensor(tmp[:], xw[:], gb[:, 2 + j, :].unsqueeze(1).to_broadcast([P, NB, D]), ALU.mult))
                steps.append(lambda dve, j=j: dve.tensor_reduce(sc[:, j], tmp[:].rearrange("p b (h c) -> p b h c", h=HEADS), AX.X, ALU.add))
            steps.append(lambda dve: dve.tensor_copy(mx[:], sc[:, 0]))
            stage_vector(p, [], steps)
        stage_score_table(p, sc[:, 0], d["t_score"])
        with ExitStack() as c2:
            es = f32(c2, nc, "es", [P, TILES, HEADS])
            with ExitStack() as c3:
                a = {"iota": k["iota"], "ident": k["ident"], "head": f32(c3, nc, "head", [P, HEADS]),
                     "tile": c3.enter_context(nc.sbuf_tensor(unique("tile"), [P, GT, P], BF)),
                     "masked": c3.enter_context(nc.sbuf_tensor(unique("masked"), [P, HEADS, P], BF))}
                stage_attention_constants(p, a)
                stage_edge_max(p, k, a, es, mx)
            stage_shift(p, k, sc[:, 1], mx, adm, sc[:, 0], xw, acc)
            stage_attend(p, k, d["t_att"], es, adm, acc, False)
        with ExitStack() as c2:
            bias = f32(c2, nc, "bgat", [P, D])
            num, den = acc[:, :, 0:D], acc[:, :, D:D + HEADS]
            c = D // HEADS
            stage_vector(p, [(bias[:], d["L2_gnn_bias_gat"].partition_broadcast(P))], [
                lambda dve: dve.tensor_scalar(den, den, 1e-16, None, ALU.add),
                lambda dve: dve.reciprocal(den, den)] + [
                lambda dve, h=h: dve.tensor_tensor(acc[:, :, h * c:(h + 1) * c], acc[:, :, h * c:(h + 1) * c],
                                                   acc[:, :, D + h:D + h + 1].to_broadcast([P, NB, c]), ALU.mult) for h in range(HEADS)] + [
                lambda dve: dve.tensor_tensor(num, num, bias[:].unsqueeze(1).to_broadcast([P, NB, D]), ALU.add),
                lambda dve: dve.tensor_tensor(num, num, skip[:], ALU.add),
                lambda dve: dve.scalar_tensor_tensor(out=k["x"][:], in0=num, scalar=0.0, in1=k["x"][:], op0=ALU.max, op1=ALU.add)])


def layer_attention_gru(p, k):
    nc, d = p.nc, p.d
    BF = mybir.dt.bfloat16
    stage_norm(p, k["x"], k["h"])
    with ExitStack() as ctx:
        acc = f32(ctx, nc, "acc", [P, NB, HEADS * D + HEADS])
        ht = f32(ctx, nc, "ht", [P, NPAD])
        adm = f32(ctx, nc, "adm", [P, NB, 2 * HEADS])
        fold = f32(ctx, nc, "fold", [P, HEADS, G3])
        whh = f32(ctx, nc, "whh", [P, G3])
        tail = f32(ctx, nc, "tail", [2, 4 * D])
        with ExitStack() as c1:
            es = f32(c1, nc, "es", [P, TILES, HEADS])
            sc = f32(c1, nc, "sc", [P, NB, 2 * HEADS])
            mx = f32(c1, nc, "mx", [P, NB, HEADS])
            with ExitStack() as c2:
                wt = f32(c2, nc, "wt", [P, HEADS, D])
                wih = f32(c2, nc, "wih", [P, HEADS, G3])
                at = f32(c2, nc, "at", [P, 2, HEADS])
                vec = f32(c2, nc, "vec", [P, 2 * HEADS])
                stage_vector(p, [], [lambda dve: dve.memset(tail[:], 0.0), lambda dve: dve.memset(mx[:], MASKED)])
                stage_turn(p, k, k["h"], ht)
                stage_store_rows(p, d["t_att"], k["h"][:])
                stage_fold(p, [(wt[:], d["w3_t"].rearrange("h e d -> e h d")),
                               (wih[:], d["wih3_t"].rearrange("(h e) g -> e h g", h=HEADS)),
                               (whh[:], d["whh3_t"]), (at[:], d["a3_t"]),
                               (tail[0:1, 0:G3], d["L3_gnn_b_ih"].rearrange("(a g) -> a g", a=1)),
                               (tail[1:2, 0:2 * D], d["L3_gnn_b_hh"][0:2 * D].rearrange("(a g) -> a g", a=1)),
                               (tail[1:2, G3:4 * D], d["L3_gnn_b_hh"][2 * D:G3].rearrange("(a g) -> a g", a=1))],
                           [(fold[:, h, :], [(wt[:, h, :], wih[:, h, :])]) for h in range(HEADS)] +
                           [(vec[:, j * HEADS + h:j * HEADS + h + 1], [(wt[:, h, :], at[:, j, h:h + 1])]) for j in range(2) for h in range(HEADS)], None)
                stage_project(p, k, ht, [], [(0, 2 * HEADS, lambda b: ht[:, b * P:(b + 1) * P], vec[:])], 2 * HEADS, sc)
            stage_score_table(p, sc[:, :, 0:HEADS], d["t_score"])
            with ExitStack() as c3:
                a = {"iota": k["iota"], "ident": k["ident"], "head": f32(c3, nc, "head", [P, HEADS]),
                     "tile": c3.enter_context(nc.sbuf_tensor(unique("tile"), [P, GT, P], BF)),
                     "masked": c3.enter_context(nc.sbuf_tensor(unique("masked"), [P, HEADS, P], BF))}
                stage_attention_constants(p, a)
                stage_edge_max(p, k, a, es, mx)
            stage_shift(p, k, sc[:, :, HEADS:2 * HEADS], mx, adm, acc=acc)
            stage_attend(p, k, d["t_att"], es, adm, acc, True)
        W = HEADS * D
        den = acc[:, :, W:W + HEADS]
        stage_vector(p, [], [
            lambda dve: dve.tensor_scalar(den, den, 1e-30, None, ALU.max),
            lambda dve: dve.reciprocal(den, den)] + [
            lambda dve, h=h: dve.tensor_tensor(acc[:, :, h * D:(h + 1) * D], acc[:, :, h * D:(h + 1) * D],
                                               acc[:, :, W + h:W + h + 1].to_broadcast([P, NB, D]), ALU.mult) for h in range(HEADS)])
        with ExitStack() as c2:
            rz = f32(c2, nc, "rz", [P, NB, 2 * D])
            nn = f32(c2, nc, "nn", [P, NB, 2 * D])
            stage_gates(p, k, lambda b, c: acc[:, b, c * P:(c + 1) * P], [fold[:, h, :] for h in range(HEADS)],
                        lambda b: k["ones"][:, 0:2], tail[:], ht, whh[:], rz, nn)
            stage_gru_end(p, rz, nn, k["h"], k["x"])


def build(nc, d, out):
    with ExitStack() as ctx:
        p = Program(nc, ctx, d)
        k = {"x": f32(ctx, nc, "x", [P, NB, D]), "h": f32(ctx, nc, "h", [P, NB, D]),
             "ident": f32(ctx, nc, "ident", [P, P]), "ones": f32(ctx, nc, "ones", [P, P]),
             "tri": f32(ctx, nc, "tri", [P, P]), "iota": f32(ctx, nc, "iota", [P, UNITS]),
             "iota_i": i32(ctx, nc, "iota_i", [P, UNITS]), "bmap": i32(ctx, nc, "bmap", [1, UNITS]),
             "meta": f32(ctx, nc, "meta", [P, TILES, 4]), "src": i32(ctx, nc, "src", [P, TILES]),
             "hwrow": i32(ctx, nc, "hwrow", [P, TILES])}
        stage_constants(p, k)
        with ExitStack() as c2:
            s = {"meta": f32(c2, nc, "smeta", [SORT_P, SORT_J, 4]), "pos": i32(c2, nc, "pos", [SORT_P, SORT_J])}
            stage_positions(p, k, s)
            stage_scatter(p, k, s)
        stage_reload(p, k)
        layer_relational(p, k)
        layer_edge_mlp(p, k)
        layer_attention(p, k)
        layer_attention_gru(p, k)
        s_out = p.sig("out")
        with nc.Block() as block:
            @block.sync
            def _(sp):
                sp.dma_start(out[0:(NB - 1) * P, :].rearrange("(b p) f -> p b f", p=P), k["x"][:, 0:NB - 1, :]).then_inc(s_out.sem, 16)
                sp.dma_start(out[(NB - 1) * P:N_NODES, :], k["x"][0:LAST_ROWS, NB - 1, :]).then_inc(s_out.sem, 16)
                sp.wait_ge(s_out.sem, 32)


_INS = ["x", "src", "dst", "edge_attr_26", "edge_type_8", "edge_weight1", "L0_gnn_weight", "L0_gnn_bias",
        "L1_gnn_mlp_w1", "L1_gnn_mlp_b1", "L1_gnn_gru_bih", "L1_gnn_gru_bhh", "w2_t", "wih_t", "whh_t", "b2_c",
        "L2_gnn_gamma", "L2_gnn_beta", "L2_gnn_W_gat", "L2_gnn_att_src", "L2_gnn_att_dst", "L2_gnn_bias_gat",
        "L2_gnn_W_proj", "L2_gnn_b_proj", "w3_t", "a3_t", "wih3_t", "whh3_t", "L3_gnn_b_ih", "L3_gnn_b_hh"]
_SCRATCH = [("records", (SLOTS, REC)), ("attr_t", (P, GROUPS * 2 * P)), ("t_rel", (NPAD * N_REL, D)), ("t_mlp", (NPAD, MH)),
            ("t_att", (NPAD, D)), ("t_score", (NPAD, SC))]


def kernel(**inputs):
    import numpy as _np
    import concourse.bacc as _bacc
    from concourse import mybir as _mybir
    from concourse.bass_utils import run_bass_kernel_spmd as _run

    inputs = dict(inputs)
    inputs["w2_t"] = _np.transpose(inputs["L1_gnn_mlp_w2"], (0, 2, 1))
    inputs["wih_t"] = _np.transpose(inputs["L1_gnn_gru_wih"], (0, 2, 1))
    inputs["whh_t"] = _np.transpose(inputs["L1_gnn_gru_whh"], (0, 2, 1))
    inputs["b2_c"] = _np.transpose(_np.reshape(inputs["L1_gnn_mlp_b2"], (2, 2, 128)), (0, 2, 1))
    inputs["w3_t"] = _np.transpose(inputs["L3_gnn_W"], (0, 2, 1))
    inputs["a3_t"] = _np.transpose(_np.reshape(inputs["L3_gnn_a"], (4, 2, 128)), (2, 1, 0))
    inputs["wih3_t"] = _np.transpose(inputs["L3_gnn_W_ih"])
    inputs["whh3_t"] = _np.transpose(inputs["L3_gnn_W_hh"])
    nc = _bacc.Bacc("TRN2", target_bir_lowering=False, num_devices=1)
    arrays, d = {}, {}
    for name in _INS:
        a = _np.ascontiguousarray(inputs[name])
        arrays[f"in_{name}"] = a
        d[name] = nc.dram_tensor(f"in_{name}", a.shape, _mybir.dt.from_np(a.dtype), kind="ExternalInput").ap()
    for name, shape in _SCRATCH:
        d[name] = nc.dram_tensor(name, shape, F32).ap()
    out = nc.dram_tensor("out_0", (N_NODES, D), F32, kind="ExternalOutput").ap()
    build(nc, d, out)
    return _run(nc, [arrays], core_ids=[0]).results[0]["out_0"]
```

```python
from contextlib import ExitStack

import concourse.bass as bass
from concourse import mybir

F32 = mybir.dt.float32
I32 = mybir.dt.int32
BF16 = mybir.dt.bfloat16
ALU = mybir.AluOpType
ACT = mybir.ActivationFunctionType
AX = mybir.AxisListType

P = 128
N_NODES, D = 3125, 128
N_EDGES = 100000
N_ATTR = 26
N_REL = 8
HEADS = 4
MH = 256
NB = -(-N_NODES // P)
NPAD = NB * P
LAST_ROWS = N_NODES - (NB - 1) * P
G3 = 3 * D

SORT_P = 125
SORT_J = N_EDGES // SORT_P
UNIT = 2 * P
UNITS = -(-(N_EDGES + NB * (UNIT - 1)) // UNIT)
GT = 8
GU = GT // 2
GROUPS = -(-UNITS // GU)
UNITS = GROUPS * GU
TILES = GROUPS * GT
SLOTS = TILES * P
BODIES = GROUPS // 2
BU = 2 * GU
PARTS = 3
AR = 96
REC = AR // 2 + 4
F_NORM, F_DST, F_SRC, F_HW = (AR // 2 + j for j in range(4))
LAGS = 3
BIG = 1.0e30
EPS = 1e-5
SLOPE = 0.2


class Signal:

    def __init__(self, sem):
        self.sem = sem
        self.base = 0

    def at(self, n):
        return n + self.base

    def close(self, n):
        self.base += n


class Program:
    def __init__(self, nc, ctx, dram):
        self.nc, self.ctx, self.d = nc, ctx, dram
        self.signals = {}

    def sig(self, name):
        if name not in self.signals:
            self.signals[name] = Signal(self.ctx.enter_context(self.nc.semaphore(name)))
        return self.signals[name]

    def apart(self, eng):
        eng.sem_inc(self.sig("apart").sem, 1)


def unique(name, used={}):
    used[name] = used.get(name, 0) + 1
    return f"{name}_{used[name]}"


def f32(ctx, nc, name, shape):
    return ctx.enter_context(nc.sbuf_tensor(unique(name), shape, F32))


def i32(ctx, nc, name, shape):
    return ctx.enter_context(nc.sbuf_tensor(unique(name), shape, I32))


def bf16(ctx, nc, name, shape):
    return ctx.enter_context(nc.sbuf_tensor(unique(name), shape, BF16))


def unit_blocks(nc, eng, k, g, lag=0):
    _, blocks = nc.values_load_multi_w_load_instructions(
        k["bmap"][0:1, lag, bass.ds(4 * g, 4)], engines=[eng.engine], min_val=0, max_val=NB - 1,
        skip_runtime_bounds_check_because="an entry counts which of the first NB - 1 blocks end before the unit")
    return blocks


def bank(ctx, nc, name):
    return ctx.enter_context(nc.psum_tensor(unique(name), [P, 512], F32))


def link(p, eng, s, ins, count):
    ins.then_inc(s.sem, 1)
    count[0] += 1
    eng.wait_ge(s.sem, s.at(count[0]))


def stage_constants(p, k):
    nc, d = p.nc, p.d
    s_ld, s_c, s_z = p.sig("load"), p.sig("const"), p.sig("zero")
    with nc.Block() as block:
        @block.vector
        def _(dve):
            dve.memset(k["x"][:], 0.0).then_inc(s_z.sem, 1)
            dve.memset(k["ones"][:], 1.0)

        @block.sync
        def _(sp):
            sp.wait_ge(s_z.sem, s_z.at(1))
            xv = d["x"][0:(NB - 1) * P, :].rearrange("(b p) f -> p b f", p=P)
            sp.dma_start(k["x"][:, 0:NB - 1, :], xv).then_inc(s_ld.sem, 16)
            sp.dma_start(k["x"][0:LAST_ROWS, NB - 1, :], d["x"][(NB - 1) * P:N_NODES, :]).then_inc(s_ld.sem, 16)
            sp.wait_ge(s_ld.sem, s_ld.at(32))

        @block.gpsimd
        def _(pool):
            pool.memset(k["ident"][:], 0.0).then_inc(s_c.sem, 1)
            pool.memset(k["tri"][:], 1.0).then_inc(s_c.sem, 1)
            pool.wait_ge(s_c.sem, s_c.at(2))
            pool.affine_select(out=k["ident"][:], in_=k["ident"][:], compare_op=ALU.not_equal, fill=1.0,
                               base=0, pattern=[[-1, P]], channel_multiplier=1)
            pool.affine_select(out=k["tri"][:], in_=k["tri"][:], compare_op=ALU.is_gt, fill=0.0,
                               base=0, pattern=[[1, P]], channel_multiplier=-1)
            pool.iota(k["iota_i"][:], pattern=[[1, UNITS]], base=0, channel_multiplier=0).then_inc(s_c.sem, 1)
            pool.wait_ge(s_c.sem, s_c.at(3))
            pool.tensor_copy(k["iota"][:], k["iota_i"][:])
            pool.tensor_copy(k["ident16"][:], k["ident"][:])
            pool.tensor_copy(k["iota16"][:], k["iota_i"][:, 0:P])
    s_ld.close(32), s_c.close(3), s_z.close(1)


def stage_positions(p, k, s):
    nc, d = p.nc, p.d
    s_ld, s_dve, s_pe = p.sig("load"), p.sig("dve_chain"), p.sig("pe_out")
    n = [0]
    with ExitStack() as ctx:
        keyf = f32(ctx, nc, "keyf", [SORT_P, SORT_J])
        tmp_i = i32(ctx, nc, "tmp_i", [SORT_P, SORT_J])
        dst_i = i32(ctx, nc, "dst_i", [SORT_P, SORT_J])
        src_i = i32(ctx, nc, "src_i", [SORT_P, SORT_J])
        typ_i = i32(ctx, nc, "typ_i", [SORT_P, SORT_J])
        eq = f32(ctx, nc, "eq", [SORT_P, 2, SORT_J])
        run = f32(ctx, nc, "run", [SORT_P, 2, SORT_J])
        one = f32(ctx, nc, "one", [SORT_P, SORT_J])
        posf = f32(ctx, nc, "posf", [SORT_P, SORT_J])
        cnt = f32(ctx, nc, "cnt", [SORT_P, NB])
        base = f32(ctx, nc, "base", [SORT_P, NB])
        tot_i = i32(ctx, nc, "tot_i", [P, NB])
        totf = f32(ctx, nc, "totf", [P, NB])
        unitf = f32(ctx, nc, "unitf", [P, NB])
        uend = f32(ctx, nc, "uend", [P, NB])
        pads = f32(ctx, nc, "pads", [P, NB])
        bmf = f32(ctx, nc, "bmf", [1, UNITS])
        ps = bank(ctx, nc, "ps")
        meta = s["meta"]
        with nc.Block() as block:
            @block.sync
            def _(sp):
                for t, name in ((dst_i, "dst"), (src_i, "src"), (typ_i, "edge_type_8")):
                    sp.dma_start(t[:], d[name].rearrange("(p j) -> p j", p=SORT_P)).then_inc(s_ld.sem, 16)
                sp.dma_start(one[:], d["edge_weight1"].rearrange("(p j) a -> p (j a)", p=SORT_P)).then_inc(s_ld.sem, 16)

            @block.tensor
            def _(pe):
                pe.wait_ge(p.sig("counts").sem, p.sig("counts").at(1))
                pe.matmul(ps[0:SORT_P, 0:NB], k["tri"][0:SORT_P, 0:SORT_P], cnt[:], start=True, stop=True)
                pe.matmul(ps[:, 32:32 + NB], k["ones"][0:SORT_P, 0:P], cnt[:], start=True, stop=True).then_inc(s_pe.sem, 1)

            @block.vector
            def _(dve):
                def chain(ins):
                    link(p, dve, s_dve, ins, n)
                dve.wait_ge(s_ld.sem, s_ld.at(64))
                chain(dve.tensor_copy(meta[:, :, 0], one[:]))
                chain(dve.tensor_scalar(tmp_i[:], dst_i[:], P - 1, None, ALU.bitwise_and))
                chain(dve.tensor_copy(meta[:, :, 1], tmp_i[:]))
                chain(dve.tensor_scalar(tmp_i[:], dst_i[:], 7, None, ALU.arith_shift_right))
                dve.tensor_copy(keyf[:], tmp_i[:])
                dve.tensor_copy(meta[:, :, 2], src_i[:])
                chain(dve.tensor_copy(posf[:], typ_i[:]))
                chain(dve.scalar_tensor_tensor(out=meta[:, :, 3], in0=meta[:, :, 2], scalar=float(N_REL),
                                               in1=posf[:], op0=ALU.mult, op1=ALU.add))
                dve.memset(one[:], 1.0)
                chain(dve.memset(posf[:], -1.0))
                for b in range(NB):
                    e, r = eq[:, b % 2, :], run[:, b % 2, :]
                    chain(dve.tensor_scalar(e, keyf[:], float(b), None, ALU.is_equal))
                    chain(dve.tensor_tensor_scan(r, one[:], e, 0.0, ALU.mult, ALU.add))
                    dve.tensor_copy(cnt[:, b:b + 1], r[:, SORT_J - 1:SORT_J])
                    chain(dve.tensor_tensor(e, e, r, ALU.mult))
                    chain(dve.tensor_tensor(posf[:], posf[:], e, ALU.add))
                dve.tensor_copy(base[0:1, 0:1], cnt[0:1, 0:1]).then_inc(p.sig("counts").sem, 1)
                dve.wait_ge(s_pe.sem, s_pe.at(1))
                chain(dve.tensor_scalar(totf[:], ps[:, 32:32 + NB], float(UNIT - 1), None, ALU.add))
                chain(dve.tensor_copy(tot_i[:], totf[:]))
                chain(dve.tensor_scalar(tot_i[:], tot_i[:], 8, None, ALU.arith_shift_right))
                chain(dve.tensor_copy(unitf[:], tot_i[:]))
                chain(dve.tensor_tensor_scan(uend[:], k["ones"][:, 0:NB], unitf[:], 0.0, ALU.mult, ALU.add))
                chain(dve.tensor_tensor(pads[:], uend[:], unitf[:], ALU.subtract))
                chain(dve.scalar_tensor_tensor(out=base[:], in0=pads[0:SORT_P, :], scalar=float(UNIT),
                                               in1=ps[0:SORT_P, 0:NB], op0=ALU.mult, op1=ALU.add))
                for b in range(NB):
                    e = eq[:, b % 2, :]
                    chain(dve.tensor_scalar(e, keyf[:], float(b), base[:, b:b + 1], ALU.is_equal, ALU.mult))
                    chain(dve.tensor_tensor(posf[:], posf[:], e, ALU.add))
                pos, part, tile = s["pos"], tmp_i, dst_i
                chain(dve.tensor_copy(pos[:], posf[:]))
                chain(dve.tensor_scalar(part[:], pos[:], P - 1, None, ALU.bitwise_and))
                chain(dve.tensor_scalar(part[:], part[:], 3, None, ALU.logical_shift_left))
                chain(dve.tensor_scalar(tile[:], pos[:], 7, GT - 1, ALU.arith_shift_right, ALU.bitwise_and))
                chain(dve.tensor_tensor(part[:], part[:], tile[:], ALU.bitwise_or))
                chain(dve.tensor_scalar(pos[:], pos[:], 10, None, ALU.arith_shift_right))
                chain(dve.tensor_scalar(pos[:], pos[:], 10, None, ALU.logical_shift_left))
                chain(dve.tensor_tensor(pos[:], pos[:], part[:], ALU.bitwise_or))
                chain(dve.memset(bmf[:], 0.0))
                for b in range(NB - 1):
                    chain(dve.scalar_tensor_tensor(out=bmf[:], in0=k["iota"][0:1, :], scalar=uend[0:1, b:b + 1],
                                                   in1=bmf[:], op0=ALU.is_ge, op1=ALU.add))
                chain(dve.memset(k["bmap"][:], 0))
                for lag in range(LAGS):
                    dve.tensor_copy(k["bmap"][:, lag, lag:lag + UNITS], bmf[:])
        s_ld.close(64), s_dve.close(n[0]), s_pe.close(1), p.sig("counts").close(1)


SJ = 16
STEPS = SORT_J // SJ


def stage_scatter(p, k, s, ht):
    nc, d = p.nc, p.d
    s_init, s_attr = p.sig("init"), [p.sig("attr0"), p.sig("attr1")]
    s_rec, s_sc, s_c = p.sig("rec"), [p.sig("scat0"), p.sig("scat1")], p.sig("dve_chain")
    s_z, s_ld, s_pe = p.sig("zero"), p.sig("load"), p.sig("pe_out")
    s_a, s_st = p.sig("ev_act"), [p.sig("store0"), p.sig("store1")]
    tv = d["t_rel"].rearrange("(b p r) f -> b p (r f)", p=P, r=N_REL)
    INIT = 8
    W = SJ * N_ATTR
    with ExitStack() as ctx:
        blank = f32(ctx, nc, "blank", [P, TILES // INIT, REC])
        attr = f32(ctx, nc, "attr", [SORT_P, 2, SJ, N_ATTR])
        rest = f32(ctx, nc, "rest", [SORT_P, 2, SJ, N_ATTR])
        rec = f32(ctx, nc, "rec", [SORT_P, 2, SJ, REC])
        idx = i32(ctx, nc, "idx", [SORT_P, 2, SJ])
        w = f32(ctx, nc, "w0", [P, N_REL, D])
        row = f32(ctx, nc, "row0", [P, 2, N_REL * D])
        ps = [bank(ctx, nc, f"ph{q}") for q in range(4)]
        av = d["edge_attr_26"].rearrange("(p j) f -> p (j f)", p=SORT_P)
        with nc.Block() as block:
            @block.sync
            def _(sp):
                def load(i, q):
                    sp.dma_start(attr[:, q].rearrange("p j f -> p (j f)"), av[:, bass.ds((2 * i + q) * W, W)]).then_inc(s_attr[q].sem, 16)
                sp.wait_ge(s_z.sem, s_z.at(2))
                rv = d["records"].rearrange("(p c r) f -> c p (r f)", p=P, c=INIT)
                for c in range(INIT):
                    sp.dma_start(rv[c], blank[:].rearrange("p r f -> p (r f)")).then_inc(s_init.sem, 16)
                for q in range(2):
                    load(0, q)
                sp.dma_start(w[:], d["L0_gnn_weight"].rearrange("r i o -> i r o")).then_inc(s_ld.sem, 16)
                with sp.Fori(1, STEPS // 2) as i:
                    for q in range(2):
                        sp.wait_ge(s_rec.sem, s_rec.at(2 * i + q - 1))
                        p.apart(sp)
                        load(i, q)

            @block.vector
            def _(dve):
                dve.memset(blank[:], 0.0).then_inc(s_z.sem, 1)
                dve.wait_ge(s_z.sem, s_z.at(1))
                dve.memset(blank[:, :, F_DST:F_DST + 1], -1.0).then_inc(s_z.sem, 1)
                dve.memset(rec[:], 0.0).then_inc(s_z.sem, 1)
                dve.wait_ge(s_z.sem, s_z.at(3))

                def body(i, first):
                    for q in range(2):
                        j0, n = (2 * i + q) * SJ, 3 * (2 * i + q)
                        parts = rec[:, q].bitcast(BF16)
                        hi, mid, lo = (parts[:, :, c * N_ATTR:(c + 1) * N_ATTR] for c in range(PARTS))
                        dve.wait_ge(s_attr[q].sem, s_attr[q].at(16 * (i + 1)))
                        if not first:
                            dve.wait_ge(s_sc[q].sem, s_sc[q].at(16 * SJ * i))
                        dve.tensor_copy(hi, attr[:, q]).then_inc(s_c.sem, 1)
                        dve.tensor_scalar(rec[:, q, :, F_NORM:F_NORM + 4], s["meta"][:, bass.ds(j0, SJ), :], 0.0, None, ALU.add)
                        dve.wait_ge(s_c.sem, s_c.at(n + 1))
                        dve.tensor_tensor(rest[:, q], attr[:, q], hi, ALU.subtract).then_inc(s_c.sem, 1)
                        dve.wait_ge(s_c.sem, s_c.at(n + 2))
                        dve.tensor_copy(mid, rest[:, q]).then_inc(s_c.sem, 1)
                        dve.tensor_copy(idx[:, q, :], s["pos"][:, bass.ds(j0, SJ)])
                        dve.wait_ge(s_c.sem, s_c.at(n + 3))
                        dve.tensor_tensor(lo, rest[:, q], mid, ALU.subtract).then_inc(s_rec.sem, 1)
                body(0, True)
                with dve.Fori(1, STEPS // 2) as i:
                    body(i, False)

            @block.gpsimd
            def _(pool):
                pool.wait_ge(s_init.sem, s_init.at(16 * INIT))
                with pool.Fori(0, STEPS // 2) as i:
                    for q in range(2):
                        pool.wait_ge(s_rec.sem, s_rec.at(2 * i + q + 1))
                        p.apart(pool)
                        for j in range(SJ):
                            pool.indirect_dma_start(
                                out=d["records"], out_offset=bass.IndirectOffsetOnAxis(ap=idx[:, q, j:j + 1], axis=0),
                                in_=rec[:, q, j, :], in_offset=None).then_inc(s_sc[q].sem, 16)
                for q in range(2):
                    pool.wait_ge(s_sc[q].sem, s_sc[q].at(16 * SJ * (STEPS // 2)))

            @block.tensor
            def _(pe):
                pe.wait_ge(s_ld.sem, s_ld.at(16))
                for b in range(NB):
                    if b >= 2:
                        pe.wait_ge(s_a.sem, s_a.at(b - 1))
                    for h in range(2):
                        last = pe.matmul(ps[2 * (b % 2) + h][:], ht[:, b * P:(b + 1) * P],
                                         w[:, 4 * h:4 * h + 4, :].rearrange("p r f -> p (r f)"), start=True, stop=True)
                    last.then_inc(s_pe.sem, 1)

            @block.scalar
            def _(act):
                for b in range(NB):
                    act.wait_ge(s_pe.sem, s_pe.at(b + 1))
                    if b >= 2:
                        act.wait_ge(s_st[b % 2].sem, s_st[b % 2].at(16 * (b // 2)))
                    for h in range(2):
                        last = act.copy(row[:, b % 2, 512 * h:512 * h + 512], ps[2 * (b % 2) + h][:])
                    last.then_inc(s_a.sem, 1)
                    act.wait_ge(s_a.sem, s_a.at(b + 1))
                    act.dma_start(tv[b], row[:, b % 2, :]).then_inc(s_st[b % 2].sem, 16)
                for q in range(2):
                    act.wait_ge(s_st[q].sem, s_st[q].at(16 * ((NB + 1 - q) // 2)))
        s_z.close(3), s_init.close(16 * INIT), s_rec.close(STEPS), s_c.close(3 * STEPS)
        s_ld.close(16), s_pe.close(NB), s_a.close(NB)
        for q in range(2):
            s_attr[q].close(16 * (STEPS // 2)), s_sc[q].close(16 * SJ * (STEPS // 2))
            s_st[q].close(16 * ((NB + 1 - q) // 2))


def norm_steps(dve, x, out, tmp, stat, chain, s_var):
    chain(dve.tensor_reduce(stat[:, 0, :], x[:], AX.X, ALU.add))
    chain(dve.tensor_scalar(stat[:, 0, :], stat[:, 0, :], 1.0 / D, None, ALU.mult))
    mean = stat[:, 0, :].unsqueeze(2).to_broadcast([P, NB, D])
    chain(dve.tensor_tensor(out[:], x[:], mean, ALU.subtract))
    chain(dve.tensor_tensor(tmp[:], out[:], out[:], ALU.mult))
    chain(dve.tensor_reduce(stat[:, 1, :], tmp[:], AX.X, ALU.add))
    dve.tensor_scalar(stat[:, 1, :], stat[:, 1, :], 1.0 / D, EPS, ALU.mult, ALU.add).then_inc(s_var.sem, 1)


def stage_norm(p, x, out, relu=True, gamma=None, beta=None):
    nc = p.nc
    s_dve, s_var, s_std = p.sig("dve_chain"), p.sig("var"), p.sig("std")
    n = [0]
    with ExitStack() as ctx:
        tmp = f32(ctx, nc, "ntmp", [P, NB, D])
        stat = f32(ctx, nc, "nstat", [P, 2, NB])
        with nc.Block() as block:
            @block.vector
            def _(dve):
                def chain(ins):
                    link(p, dve, s_dve, ins, n)
                norm_steps(dve, x, out, tmp, stat, chain, s_var)
                dve.wait_ge(s_std.sem, s_std.at(1))
                chain(dve.reciprocal(stat[:, 1, :], stat[:, 1, :]))
                rstd = stat[:, 1, :].unsqueeze(2).to_broadcast([P, NB, D])
                chain(dve.tensor_tensor(out[:], out[:], rstd, ALU.mult))
                if relu:
                    chain(dve.tensor_scalar(out[:], out[:], 0.0, None, ALU.max))
                if gamma is not None:
                    chain(dve.tensor_tensor(out[:], out[:], gamma.unsqueeze(1).to_broadcast([P, NB, D]), ALU.mult))
                    chain(dve.tensor_tensor(out[:], out[:], beta.unsqueeze(1).to_broadcast([P, NB, D]), ALU.add))

            @block.scalar
            def _(act):
                act.wait_ge(s_var.sem, s_var.at(1))
                act.activation(stat[:, 1, :], stat[:, 1, :], ACT.Sqrt).then_inc(s_std.sem, 1)
        s_dve.close(n[0]), s_var.close(1), s_std.close(1)


def stage_turn(p, k, h, ht):
    nc = p.nc
    s_pe, s_ev = p.sig("pe_out"), p.sig("turned")
    rounds = -(-NB // 4)
    with ExitStack() as ctx:
        ps = [bank(ctx, nc, f"pt{q}") for q in range(2)]
        with nc.Block() as block:
            @block.tensor
            def _(pe):
                for r in range(rounds):
                    if r >= 2:
                        pe.wait_ge(s_ev.sem, s_ev.at(r - 1))
                    for b in range(4 * r, min(NB, 4 * r + 4)):
                        last = pe.transpose(ps[r % 2][:, (b % 4) * P:(b % 4 + 1) * P], h[:, b, :], k["ident"][:])
                    last.then_inc(s_pe.sem, 1)

            @block.scalar
            def _(act):
                for r in range(rounds):
                    w = (min(NB, 4 * r + 4) - 4 * r) * P
                    act.wait_ge(s_pe.sem, s_pe.at(r + 1))
                    act.copy(ht[:, 4 * r * P:4 * r * P + w], ps[r % 2][:, 0:w]).then_inc(s_ev.sem, 1)
        s_pe.close(rounds), s_ev.close(rounds)


def stage_project(p, k, ht, loads, products, width, out):
    nc = p.nc
    s_ld, s_pe, s_ev = p.sig("load"), p.sig("pe_out"), p.sig("ev_act")
    with ExitStack() as ctx:
        ps = [bank(ctx, nc, f"pj{q}") for q in range(2)]
        with nc.Block() as block:
            @block.sync
            def _(sp):
                for dst, src in loads:
                    sp.dma_start(dst, src).then_inc(s_ld.sem, 16)

            @block.tensor
            def _(pe):
                if loads:
                    pe.wait_ge(s_ld.sem, s_ld.at(16 * len(loads)))
                for b in range(NB):
                    if b >= 2:
                        pe.wait_ge(s_ev.sem, s_ev.at(b - 1))
                    for m, (c0, c1, lhs, rhs) in enumerate(products):
                        last = pe.matmul(ps[b % 2][:, c0:c1], lhs(b), rhs, start=m == 0, stop=m == len(products) - 1)
                    last.then_inc(s_pe.sem, 1)

            @block.scalar
            def _(act):
                for b in range(NB):
                    act.wait_ge(s_pe.sem, s_pe.at(b + 1))
                    act.copy(out[:, b, 0:width], ps[b % 2][:, 0:width]).then_inc(s_ev.sem, 1)
        s_ld.close(16 * len(loads)), s_pe.close(NB), s_ev.close(NB)


def stage_edge_parts(p, k, r, ht, w1, b1, wf, wc, pds):
    nc, d = p.nc, p.d
    s_ld, s_pe, s_z = p.sig("load"), p.sig("pe_out"), p.sig("zero")
    s_a, s_hi, s_r, s_mid, s_lo = p.sig("ev_act"), p.sig("turn"), p.sig("turned"), p.sig("oht"), p.sig("ev_dve")
    s_st, s_c = [p.sig("store0"), p.sig("store1")], p.sig("dve_chain")
    w1d = d["L1_gnn_mlp_w1"][r]
    loads = 2 + PARTS
    n = [0]
    with ExitStack() as ctx:
        row = f32(ctx, nc, "prow", [P, 2, MH])
        rest = f32(ctx, nc, "prest", [P, 2, MH])
        wrest = f32(ctx, nc, "wrest", [AR, MH])
        ps = [bank(ctx, nc, f"ps{q}") for q in range(2)]
        pd = [bank(ctx, nc, f"pd{q}") for q in range(2)]
        tv = d["t_mlp"].rearrange("(b p) f -> b p f", p=P)
        with nc.Block() as block:
            @block.sync
            def _(sp):
                sp.dma_start(w1[:], w1d[0:2 * D, :].rearrange("(a i) o -> i a o", a=2)).then_inc(s_ld.sem, 16)
                sp.dma_start(b1[:], d["L1_gnn_mlp_b1"][r:r + 1, :]).then_inc(s_ld.sem, 16)
                sp.wait_ge(s_z.sem, s_z.at(1))
                for c in range(PARTS):
                    sp.dma_start(wf[c * N_ATTR:(c + 1) * N_ATTR, :], w1d[2 * D:2 * D + N_ATTR, :]).then_inc(s_ld.sem, 16)
                for b in range(NB):
                    sp.wait_ge(s_a.sem, s_a.at(b + 1))
                    sp.dma_start(tv[b], row[:, b % 2, :]).then_inc(s_st[b % 2].sem, 16)
                for q in range(2):
                    sp.wait_ge(s_st[q].sem, s_st[q].at(16 * ((NB + 1 - q) // 2)))

            @block.tensor
            def _(pe):
                pe.wait_ge(s_ld.sem, s_ld.at(16 * loads))
                for b in range(NB):
                    hb = ht[:, b * P:(b + 1) * P]
                    if b >= 2:
                        pe.wait_ge(s_a.sem, s_a.at(b - 1))
                    pe.matmul(ps[b % 2][:, 0:MH], hb, w1[:, 1, :], start=True, stop=True)
                    if b >= 2:
                        pe.wait_ge(s_r.sem, s_r.at(b - 1))
                    pe.matmul(pd[b % 2][:, 0:MH], hb, w1[:, 0, :], start=True, stop=False)
                    pe.matmul(pd[b % 2][:, 0:MH], k["ones"][0:1, 0:P], b1[:], start=False, stop=True).then_inc(s_pe.sem, 1)

            @block.scalar
            def _(act):
                def middle(b):
                    act.wait_ge(s_r.sem, s_r.at(b + 1))
                    act.copy(pds[:, b, 1, :], rest[:, b % 2, :]).then_inc(s_mid.sem, 1)
                for b in range(NB):
                    act.wait_ge(s_pe.sem, s_pe.at(b + 1))
                    act.copy(pds[:, b, 0, :], pd[b % 2][:, 0:MH]).then_inc(s_hi.sem, 1)
                    if b >= 2:
                        act.wait_ge(s_st[b % 2].sem, s_st[b % 2].at(16 * (b // 2)))
                    act.copy(row[:, b % 2, :], ps[b % 2][:, 0:MH]).then_inc(s_a.sem, 1)
                    if b >= 1:
                        middle(b - 1)
                middle(NB - 1)

            @block.vector
            def _(dve):
                def chain(ins):
                    link(p, dve, s_c, ins, n)
                dve.memset(wf[:], 0.0).then_inc(s_z.sem, 1)

                def low(b):
                    dve.wait_ge(s_mid.sem, s_mid.at(b + 1))
                    dve.tensor_tensor(pds[:, b, 2, :], rest[:, b % 2, :], pds[:, b, 1, :], ALU.subtract).then_inc(s_lo.sem, 1)
                for b in range(NB):
                    dve.wait_ge(s_hi.sem, s_hi.at(b + 1))
                    if b >= 2:
                        dve.wait_ge(s_lo.sem, s_lo.at(b - 1))
                    dve.tensor_tensor(rest[:, b % 2, :], pd[b % 2][:, 0:MH], pds[:, b, 0, :], ALU.subtract).then_inc(s_r.sem, 1)
                    if b >= 1:
                        low(b - 1)
                low(NB - 1)
                dve.wait_ge(s_ld.sem, s_ld.at(16 * loads))
                chain(dve.tensor_copy(wc[:, 0, :], wf[:]))
                chain(dve.tensor_tensor(wrest[:], wf[:], wc[:, 0, :], ALU.subtract))
                chain(dve.tensor_copy(wc[:, 1, :], wrest[:]))
                chain(dve.tensor_tensor(wc[:, 2, :], wrest[:], wc[:, 1, :], ALU.subtract))
        s_ld.close(16 * loads), s_z.close(1), s_c.close(n[0])
        for s in (s_pe, s_a, s_hi, s_r, s_mid, s_lo):
            s.close(NB)
        for q in range(2):
            s_st[q].close(16 * ((NB + 1 - q) // 2))


def stage_store_rows(p, out_dram, rows):
    nc = p.nc
    s_st = p.sig("store0")
    with nc.Block() as block:
        @block.sync
        def _(sp):
            sp.dma_start(out_dram.rearrange("(b p) f -> p b f", p=P), rows).then_inc(s_st.sem, 16)
            sp.wait_ge(s_st.sem, s_st.at(16))
    s_st.close(16)


def over_bodies(eng, body):
    body(0, True, False)
    with eng.Fori(1, BODIES - 1) as i:
        body(i, False, False)
    body(BODIES - 1, False, True)


class Gather:

    def __init__(self, p, ctx, table, index, width):
        self.p, self.table, self.index, self.width = p, table, index, width
        self.rows = f32(ctx, p.nc, "rows", [P, 2, GT, width])
        self.idx = i32(ctx, p.nc, "gidx", [P, 2, GT])
        self.s_idx = p.sig("idx")
        self.s_row = [p.sig(f"row{u}") for u in range(BU)]

    def feed(self, act, g, q):
        act.copy(self.idx[:, q, :], self.index[:, bass.ds(g * GT, GT)]).then_inc(self.s_idx.sem, 1)

    def program(self, pool):
        p = self.p
        with pool.Fori(0, BODIES) as i:
            for q in range(2):
                pool.wait_ge(self.s_idx.sem, self.s_idx.at(2 * i + q + 1))
                p.apart(pool)
                for t in range(GT):
                    pool.indirect_dma_start(
                        out=self.rows[:, q, t, :], out_offset=None, in_=self.table,
                        in_offset=bass.IndirectOffsetOnAxis(ap=self.idx[:, q, t:t + 1], axis=0),
                    ).then_inc(self.s_row[GU * q + t // 2].sem, 16)

    def close(self):
        self.s_idx.close(GROUPS)
        for s in self.s_row:
            s.close(32 * BODIES)


def onehot(p, dve, k, oh, g, q):
    dst = k["meta"][:, bass.ds(g * GT, GT)].unsqueeze(2).to_broadcast([P, GT, P])
    nodes = k["iota"][:, 0:P].unsqueeze(1).to_broadcast([P, GT, P])
    return dve.tensor_tensor(oh[:, q], nodes, dst, ALU.is_equal)


def onehot16(dve, k, oh, g, q, op=ALU.is_equal):
    dst = k["meta16"][:, bass.ds(g * GT, GT)].unsqueeze(2).to_broadcast([P, GT, P])
    nodes = k["iota16"][:].unsqueeze(1).to_broadcast([P, GT, P])
    return dve.tensor_tensor(oh[:, q], nodes, dst, op)


def stage_relation_sum(p, k, acc):
    nc, d = p.nc, p.d
    s_oh, s_agg, s_acc = p.sig("onehot"), p.sig("agg"), p.sig("acc")
    s_z, s_turn, s_cp, s_ra = p.sig("zero"), p.sig("turn"), p.sig("oht"), p.sig("relu")
    s_rl, s_st = [p.sig("attr0"), p.sig("attr1")], [p.sig("store0"), p.sig("store1")]
    with ExitStack() as ctx:
        ga = Gather(p, ctx, d["t_rel"], None, D)
        buf = f32(ctx, nc, "rbuf", [P, 2, GT, REC])
        out = bf16(ctx, nc, "rout", [AR, 2, GT * P])
        oh = f32(ctx, nc, "oh", [P, 2, GT, P])
        wr = f32(ctx, nc, "wr", [P, 2, GT, D])
        ps = [bank(ctx, nc, f"pa{q}") for q in range(2)]
        tp = [ctx.enter_context(nc.psum_tensor(unique("pr"), [P, GT * P], BF16)) for q in range(2)]
        rv = d["records"].rearrange("(g p i) f -> p g (i f)", p=P, i=GT)
        with nc.Block() as block:
            @block.gpsimd
            def _(pool):
                ga.program(pool)

            @block.sync
            def _(sp):
                def load(g, q):
                    sp.dma_start(buf[:, q].rearrange("p i f -> p (i f)"),
                                 rv[:, bass.ds(g, 1), :].rearrange("p g f -> p (g f)")).then_inc(s_rl[q].sem, 16)

                def store(g, q):
                    sp.wait_ge(s_cp.sem, s_cp.at(g + 1))
                    p.apart(sp)
                    sp.dma_start(d["attr_t"][:, bass.ds(g * GT * P, GT * P)], out[:, q, :]).then_inc(s_st[q].sem, 16)
                for q in range(2):
                    load(q, q)
                with sp.Fori(0, BODIES - 1) as i:
                    for q in range(2):
                        g = 2 * i + q
                        store(g, q)
                        sp.wait_ge(s_ra.sem, s_ra.at(4 * g + 4))
                        p.apart(sp)
                        sp.wait_ge(s_oh.sem, s_oh.at(g + 1))
                        p.apart(sp)
                        load(g + 2, q)
                for q in range(2):
                    store(GROUPS - 2 + q, q)
                for q in range(2):
                    sp.wait_ge(s_st[q].sem, s_st[q].at(16 * BODIES))

            @block.scalar
            def _(act):
                def body(i, first, last):
                    for q in range(2):
                        g = 2 * i + q
                        act.wait_ge(s_turn.sem, s_turn.at(g + 1))
                        if not first:
                            p.apart(act)
                            act.wait_ge(s_st[q].sem, s_st[q].at(16 * i))
                        act.copy(out[:, q, :], tp[q][0:AR, :]).then_inc(s_cp.sem, 1)
                        if not first:
                            act.wait_ge(s_agg.sem, s_agg.at(4 * g - 4))
                        for t in range(GT):
                            if t % 2 == 0:
                                row = ga.s_row[GU * q + t // 2]
                                act.wait_ge(row.sem, row.at(32 * (i + 1)))
                            ins = act.activation(wr[:, q, t, :], ga.rows[:, q, t, :], ACT.Copy, scale=buf[:, q, t, F_NORM:F_NORM + 1])
                            if t % 2 == 1:
                                ins.then_inc(s_ra.sem, 1)
                over_bodies(act, body)

            @block.tensor
            def _(pe):
                def body(i, first, last):
                    for q in range(2):
                        g = 2 * i + q
                        pe.wait_ge(s_rl[q].sem, s_rl[q].at(16 * (i + 1)))
                        if not first:
                            pe.wait_ge(s_cp.sem, s_cp.at(g - 1))
                        for t in range(GT):
                            mm = pe.transpose(tp[q][0:AR, t * P:(t + 1) * P], buf[:, q, t, 0:AR // 2].bitcast(BF16), k["ident16"][:])
                        mm.then_inc(s_turn.sem, 1)
                        for v in range(GU):
                            u = 4 * g + v
                            if v == 0:
                                pe.wait_ge(s_oh.sem, s_oh.at(g + 1))
                            pe.wait_ge(s_ra.sem, s_ra.at(u + 1))
                            if not (first and q == 0 and v < 2):
                                pe.wait_ge(s_acc.sem, s_acc.at(u - 1))
                            o = ps[v % 2][:, 0:D]
                            for t in range(2):
                                mm = pe.matmul(o, oh[:, q, 2 * v + t, :], wr[:, q, 2 * v + t, :], start=t == 0, stop=t == 1)
                            mm.then_inc(s_agg.sem, 1)
                over_bodies(pe, body)

            @block.vector
            def _(dve):
                dve.memset(acc[:], 0.0).then_inc(s_z.sem, 1)

                def prepare(i, g, q, first):
                    dve.wait_ge(s_rl[q].sem, s_rl[q].at(16 * (i + 1)))
                    if not first:
                        dve.wait_ge(s_ra.sem, s_ra.at(4 * g - 4))
                    dve.tensor_scalar(ga.idx[:, q, :], buf[:, q, :, F_HW], 0.0, None, ALU.add).then_inc(ga.s_idx.sem, 1)
                    dve.tensor_scalar(k["meta"][:, bass.ds(g * GT, GT)], buf[:, q, :, F_DST], 0.0, None, ALU.add)
                    dve.tensor_scalar(k["meta16"][:, bass.ds(g * GT, GT)], buf[:, q, :, F_DST], 0.0, None, ALU.add)
                    dve.tensor_scalar(k["src"][:, bass.ds(g * GT, GT)], buf[:, q, :, F_SRC], 0.0, None, ALU.add)
                    if not first:
                        dve.wait_ge(s_agg.sem, s_agg.at(4 * g - 4))
                    dve.tensor_tensor(oh[:, q], k["iota"][:, 0:P].unsqueeze(1).to_broadcast([P, GT, P]),
                                      buf[:, q, :, F_DST:F_DST + 1].to_broadcast([P, GT, P]), ALU.is_equal).then_inc(s_oh.sem, 1)
                prepare(0, 0, 0, True)
                dve.wait_ge(s_z.sem, s_z.at(1))

                def body(i, first, last):
                    for q in range(2):
                        g = 2 * i + q
                        blocks = unit_blocks(nc, dve, k, g)
                        for v in range(GU):
                            u = 4 * g + v
                            dve.wait_ge(s_agg.sem, s_agg.at(u + 1))
                            if not (first and q == 0 and v == 0):
                                dve.wait_ge(s_acc.sem, s_acc.at(u))
                            a = acc[:, bass.ds(blocks[v], 1), :].rearrange("p a f -> p (a f)")
                            dve.tensor_tensor(a, a, ps[v % 2][:, 0:D], ALU.add).then_inc(s_acc.sem, 1)
                            if v == 0 and not (last and q == 1):
                                prepare(i + q, g + 1, 1 - q, first and q == 0)
                over_bodies(dve, body)
        ga.close()
        s_z.close(1), s_acc.close(UNITS), s_agg.close(UNITS), s_ra.close(UNITS)
        for s in (s_oh, s_turn, s_cp):
            s.close(GROUPS)
        for q in range(2):
            s_rl[q].close(16 * BODIES), s_st[q].close(16 * BODIES)


def stage_relation_add(p, k, acc):
    nc, d = p.nc, p.d
    s_ld, s_dve = p.sig("load"), p.sig("dve_chain")
    n = [0]
    with ExitStack() as ctx:
        bias = f32(ctx, nc, "b0", [P, D])
        with nc.Block() as block:
            @block.sync
            def _(sp):
                sp.dma_start(bias[:], d["L0_gnn_bias"].partition_broadcast(P)).then_inc(s_ld.sem, 16)

            @block.vector
            def _(dve):
                def chain(ins):
                    link(p, dve, s_dve, ins, n)
                dve.wait_ge(s_ld.sem, s_ld.at(16))
                chain(dve.tensor_tensor(acc[:], acc[:], bias[:].unsqueeze(1).to_broadcast([P, NB, D]), ALU.add))
                chain(dve.scalar_tensor_tensor(out=k["x"][:], in0=acc[:], scalar=0.0, in1=k["x"][:],
                                               op0=ALU.max, op1=ALU.add))
        s_ld.close(16), s_dve.close(n[0])



def turn_onehots(pe, k, oh, tp, q, s_turn):
    for t in range(GT):
        mm = pe.transpose(tp[q][:, t * P:(t + 1) * P], oh[:, q, t, :], k["ident16"][:])
    mm.then_inc(s_turn.sem, 1)


def stage_edge_mlp(p, k, r, pdst, acc, wc):
    nc, d = p.nc, p.d
    s_oh, s_oh16, s_turn, s_oht = p.sig("onehot"), p.sig("onehot16"), p.sig("turn"), p.sig("oht")
    s_pre, s_add, s_relu = p.sig("pre"), p.sig("added"), p.sig("relu")
    s_agg, s_acc, s_z = p.sig("agg"), p.sig("acc"), p.sig("zero")
    s_at = [p.sig("attr0"), p.sig("attr1")]
    with ExitStack() as ctx:
        ga = Gather(p, ctx, d["t_mlp"], k["src"], MH)
        oh = f32(ctx, nc, "oh", [P, 2, GT, P])
        oh16 = bf16(ctx, nc, "oh16", [P, 2, GT, P])
        oht = bf16(ctx, nc, "oht", [P, 2, GT, P])
        at = bf16(ctx, nc, "at", [AR, 2, GT, P])
        hs = f32(ctx, nc, "hs", [P, 2, 2, MH])
        h1 = f32(ctx, nc, "h1", [P, 2, 2, MH + 1])
        tp = [ctx.enter_context(nc.psum_tensor(unique("tp"), [P, GT * P], BF16)) for q in range(2)]
        pp = [bank(ctx, nc, f"pp{q}") for q in range(2)]
        pa = [bank(ctx, nc, f"pa{q}") for q in range(2)]
        LAG = 2
        with nc.Block() as block:
            @block.gpsimd
            def _(pool):
                ga.program(pool)

            @block.sync
            def _(sp):
                def load(g, q):
                    sp.dma_start(at[:, q].rearrange("p t e -> p (t e)"), d["attr_t"][:, bass.ds(g * GT * P, GT * P)]).then_inc(s_at[q].sem, 16)
                for q in range(2):
                    load(q, q)
                with sp.Fori(0, BODIES - 1) as i:
                    for q in range(2):
                        sp.wait_ge(s_pre.sem, s_pre.at(4 * (2 * i + q + 1)))
                        p.apart(sp)
                        load(2 * i + q + 2, q)

            @block.scalar
            def _(act):
                def turned(g, q, first):
                    if not first:
                        act.wait_ge(s_pre.sem, s_pre.at(4 * g - 4))
                        p.apart(act)
                    act.wait_ge(s_turn.sem, s_turn.at(g + 1))
                    act.copy(oht[:, q].rearrange("p t n -> p (t n)"), tp[q][:]).then_inc(s_oht.sem, 1)
                ga.feed(act, 0, 0)
                turned(0, 0, True)

                def body(i, first, last):
                    for q in range(2):
                        g = 2 * i + q
                        if not (last and q == 1):
                            if not (first and q == 0):
                                act.wait_ge(s_add.sem, s_add.at(4 * g))
                                p.apart(act)
                            ga.feed(act, g + 1, 1 - q)
                        for v in range(GU):
                            u = 4 * g + v
                            act.wait_ge(s_add.sem, s_add.at(u + 1))
                            p.apart(act)
                            if not (first and q == 0 and v < 2):
                                act.wait_ge(s_agg.sem, s_agg.at(u - 1))
                                p.apart(act)
                            act.activation(h1[:, v % 2, :, 0:MH], hs[:, v % 2], ACT.Relu).then_inc(s_relu.sem, 1)
                            if v == 1 and not (last and q == 1):
                                turned(g + 1, 1 - q, first and q == 0)
                over_bodies(act, body)

            @block.tensor
            def _(pe):
                def agg(u, w):
                    pe.wait_ge(s_relu.sem, s_relu.at(u + 1))
                    if not (isinstance(u, int) and u < 2):
                        pe.wait_ge(s_acc.sem, s_acc.at(u - 1))
                    for t in range(2):
                        mm = pe.matmul(pa[w % 2][:, 0:MH + 1], oh[:, w // GU, 2 * (w % GU) + t, :], h1[:, w % 2, t, :],
                                       start=t == 0, stop=t == 1)
                    mm.then_inc(s_agg.sem, 1)

                def turn(g, q, first):
                    pe.wait_ge(s_oh16.sem, s_oh16.at(g + 1))
                    if not first:
                        pe.wait_ge(s_oht.sem, s_oht.at(g - 1))
                    turn_onehots(pe, k, oh16, tp, q, s_turn)
                turn(0, 0, True)

                def body(i, first, last):
                    for q in range(2):
                        g = 2 * i + q
                        blocks = unit_blocks(nc, pe, k, g)
                        pe.wait_ge(s_at[q].sem, s_at[q].at(16 * (i + 1)))
                        for v in range(GU):
                            u, w = 4 * g + v, GU * q + v
                            if v == 0:
                                pe.wait_ge(s_oht.sem, s_oht.at(g + 1))
                            if v == LAG:
                                pe.wait_ge(s_oh.sem, s_oh.at(g + 1))
                            if not (first and w < 2):
                                pe.wait_ge(s_add.sem, s_add.at(u - 1))
                            for t in range(2):
                                o = pp[v % 2][:, t * MH:(t + 1) * MH]
                                j = 2 * v + t
                                for c in range(PARTS):
                                    pe.matmul(o, at[:, q, j, :], wc[:, c, :], start=c == 0, stop=False)
                                for c in range(PARTS):
                                    mm = pe.matmul(o, oht[:, q, j, :], pdst[:, bass.ds(blocks[v], 1), c, :].rearrange("p a f -> p (a f)"),
                                                   start=False, stop=c == PARTS - 1)
                            mm.then_inc(s_pre.sem, 1)
                            if not (first and w < LAG):
                                agg(u - LAG, (w - LAG) % BU)
                            if v == 1 and not (last and q == 1):
                                turn(g + 1, 1 - q, first and q == 0)
                over_bodies(pe, body)
                for u in range(UNITS - LAG, UNITS):
                    agg(u, u % BU)

            @block.vector
            def _(dve):
                dve.memset(acc[:], 0.0).then_inc(s_z.sem, 1)
                dve.memset(h1[:, :, :, MH:MH + 1], 1.0).then_inc(s_z.sem, 1)
                onehot16(dve, k, oh16, 0, 0).then_inc(s_oh16.sem, 1)
                onehot(p, dve, k, oh, 0, 0).then_inc(s_oh.sem, 1)
                dve.wait_ge(s_z.sem, s_z.at(2))

                def add(u, w, b):
                    dve.wait_ge(s_agg.sem, s_agg.at(u + 1))
                    if not (isinstance(u, int) and u == 0):
                        dve.wait_ge(s_acc.sem, s_acc.at(u))
                    a = acc[:, bass.ds(b, 1), 0:MH + 1].rearrange("p a f -> p (a f)")
                    dve.tensor_tensor(a, a, pa[w % 2][:, 0:MH + 1], ALU.add).then_inc(s_acc.sem, 1)

                def body(i, first, last):
                    for q in range(2):
                        g = 2 * i + q
                        blocks = unit_blocks(nc, dve, k, g, LAG)
                        for v in range(GU):
                            u, w = 4 * g + v, GU * q + v
                            dve.wait_ge(ga.s_row[w].sem, ga.s_row[w].at(32 * (i + 1)))
                            dve.wait_ge(s_pre.sem, s_pre.at(u + 1))
                            if not (first and w < 2):
                                dve.wait_ge(s_relu.sem, s_relu.at(u - 1))
                            dve.tensor_tensor(hs[:, v % 2].rearrange("p t f -> p (t f)"), pp[v % 2][:],
                                              ga.rows[:, q, 2 * v:2 * v + 2, :].rearrange("p t f -> p (t f)"),
                                              ALU.add).then_inc(s_add.sem, 1)
                            if not (first and w < LAG):
                                add(u - LAG, (w - LAG) % BU, blocks[v])
                            if v == 0 and not (last and q == 1):
                                if not (first and q == 0):
                                    dve.wait_ge(s_turn.sem, s_turn.at(g))
                                onehot16(dve, k, oh16, g + 1, 1 - q).then_inc(s_oh16.sem, 1)
                            if v == 2 and not (last and q == 1):
                                if not (first and q == 0):
                                    dve.wait_ge(s_agg.sem, s_agg.at(4 * g))
                                onehot(p, dve, k, oh, g + 1, 1 - q).then_inc(s_oh.sem, 1)
                over_bodies(dve, body)
                blocks = unit_blocks(nc, dve, k, GROUPS, LAG)
                for v in range(LAG):
                    u = UNITS - LAG + v
                    add(u, u % BU, blocks[v])
        ga.close()
        s_z.close(2), s_oh.close(GROUPS), s_oh16.close(GROUPS), s_turn.close(GROUPS), s_oht.close(GROUPS)
        for s in (s_pre, s_add, s_relu, s_agg, s_acc):
            s.close(UNITS)
        for q in range(2):
            s_at[q].close(16 * BODIES)


def stage_fold(p, loads, products, out):
    nc = p.nc
    s_ld, s_pe, s_ev = p.sig("load"), p.sig("pe_out"), p.sig("ev_act")
    with ExitStack() as ctx:
        ps = [bank(ctx, nc, f"pf{q}") for q in range(2)]
        with nc.Block() as block:
            @block.sync
            def _(sp):
                for dst, src in loads:
                    sp.dma_start(dst, src).then_inc(s_ld.sem, 16)

            @block.tensor
            def _(pe):
                pe.wait_ge(s_ld.sem, s_ld.at(16 * len(loads)))
                for j, (o, pairs) in enumerate(products):
                    if j >= 2:
                        pe.wait_ge(s_ev.sem, s_ev.at(j - 1))
                    for m, (lhs, rhs) in enumerate(pairs):
                        last = pe.matmul(ps[j % 2][0:o.shape[0], 0:o.shape[1]], lhs, rhs,
                                         start=m == 0, stop=m == len(pairs) - 1)
                    last.then_inc(s_pe.sem, 1)

            @block.scalar
            def _(act):
                for j, (o, pairs) in enumerate(products):
                    act.wait_ge(s_pe.sem, s_pe.at(j + 1))
                    act.copy(o, ps[j % 2][0:o.shape[0], 0:o.shape[1]]).then_inc(s_ev.sem, 1)
        s_ld.close(16 * len(loads)), s_pe.close(len(products)), s_ev.close(len(products))


def stage_gates(p, k, sums, folded, tail, tail_w, ht, whh, rz, nn):
    nc = p.nc
    s_pe, s_ev, s_g, s_a, s_v = p.sig("turn"), p.sig("turned"), p.sig("pe_out"), p.sig("ev_act"), p.sig("ev_dve")
    chunks, nt = len(folded), tail_w.shape[0]
    with ExitStack() as ctx:
        tp = [bank(ctx, nc, f"gt{q}") for q in range(2)]
        tq = [bank(ctx, nc, f"gq{q}") for q in range(2)]
        ps = [bank(ctx, nc, f"gp{q}") for q in range(2)]
        st = f32(ctx, nc, "gst", [P, 2, chunks * P])
        tt = f32(ctx, nc, "gtt", [nt, 2, P])
        with nc.Block() as block:
            @block.tensor
            def _(pe):
                def turn(b):
                    if b >= 2:
                        pe.wait_ge(s_ev.sem, s_ev.at(b - 1))
                    for c in range(chunks):
                        pe.transpose(tp[b % 2][:, c * P:(c + 1) * P], sums(b, c), k["ident"][:])
                    pe.transpose(tq[b % 2][0:nt, 0:P], tail(b), k["ident"][:]).then_inc(s_pe.sem, 1)

                turn(0)
                for b in range(NB):
                    if b + 1 < NB:
                        turn(b + 1)
                    pe.wait_ge(s_ev.sem, s_ev.at(b + 1))
                    if b >= 2:
                        pe.wait_ge(s_a.sem, s_a.at(b - 1))
                        pe.wait_ge(s_v.sem, s_v.at(b - 1))
                    o = ps[b % 2]
                    pe.matmul(o[:], tt[:, b % 2, :], tail_w, start=True, stop=False)
                    for c in range(chunks):
                        pe.matmul(o[:, 0:G3], st[:, b % 2, c * P:(c + 1) * P], folded[c], start=False, stop=False)
                    hb = ht[:, b * P:(b + 1) * P]
                    pe.matmul(o[:, 0:2 * D], hb, whh[:, 0:2 * D], start=False, stop=False)
                    pe.matmul(o[:, G3:G3 + D], hb, whh[:, 2 * D:G3], start=False, stop=True).then_inc(s_g.sem, 1)

            @block.scalar
            def _(act):
                def copy(b):
                    act.wait_ge(s_pe.sem, s_pe.at(b + 1))
                    if b >= 2:
                        act.wait_ge(s_g.sem, s_g.at(b - 1))
                    act.copy(st[:, b % 2, :], tp[b % 2][:, 0:chunks * P])
                    act.copy(tt[:, b % 2, :], tq[b % 2][0:nt, 0:P]).then_inc(s_ev.sem, 1)

                copy(0)
                for b in range(NB):
                    if b + 1 < NB:
                        copy(b + 1)
                    act.wait_ge(s_g.sem, s_g.at(b + 1))
                    act.activation(rz[:, b, :], ps[b % 2][:, 0:2 * D], ACT.Sigmoid).then_inc(s_a.sem, 1)

            @block.vector
            def _(dve):
                for b in range(NB):
                    dve.wait_ge(s_a.sem, s_a.at(b + 1))
                    dve.tensor_copy(nn[:, b, :], ps[b % 2][:, 2 * D:4 * D]).then_inc(s_v.sem, 1)
        for s in (s_pe, s_ev, s_g, s_a, s_v):
            s.close(NB)


def stage_gru_end(p, rz, nn, h, extra=None):
    nc = p.nc
    s_dve, s_var, s_std = p.sig("dve_chain"), p.sig("var"), p.sig("std")
    n = [0]
    with nc.Block() as block:
        @block.vector
        def _(dve):
            def chain(ins):
                link(p, dve, s_dve, ins, n)
            r, z = rz[:, :, 0:D], rz[:, :, D:2 * D]
            ni, ns = nn[:, :, 0:D], nn[:, :, D:2 * D]
            chain(dve.tensor_tensor(ns, ns, r, ALU.mult))
            dve.tensor_tensor(ni, ni, ns, ALU.add).then_inc(s_var.sem, 1)
            dve.wait_ge(s_std.sem, s_std.at(1))
            chain(dve.tensor_tensor(h[:], h[:], ni, ALU.subtract))
            chain(dve.tensor_tensor(h[:], h[:], z, ALU.mult))
            chain(dve.tensor_tensor(h[:], h[:], ni, ALU.add))
            if extra is not None:
                chain(dve.tensor_tensor(extra[:], extra[:], h[:], ALU.add))

        @block.scalar
        def _(act):
            act.wait_ge(s_var.sem, s_var.at(1))
            act.activation(nn[:, :, 0:D], nn[:, :, 0:D], ACT.Tanh).then_inc(s_std.sem, 1)
    s_dve.close(n[0]), s_var.close(1), s_std.close(1)


def layer_relational(p, k):
    nc, d = p.nc, p.d
    with ExitStack() as ctx:
        acc = f32(ctx, nc, "acc", [P, NB, D])
        stage_relation_sum(p, k, acc)
        stage_relation_add(p, k, acc)


def layer_edge_mlp(p, k, rounds=2):
    nc, d = p.nc, p.d
    stage_norm(p, k["x"], k["h"])
    for r in range(rounds):
        with ExitStack() as ctx:
            ht = f32(ctx, nc, "ht", [P, NPAD])
            acc = f32(ctx, nc, "acc", [P, NB, MH + 3])
            w1 = f32(ctx, nc, "w1", [P, 2, MH])
            b1 = f32(ctx, nc, "b1", [1, MH])
            wf = f32(ctx, nc, "wf", [AR, MH])
            wc = bf16(ctx, nc, "wc", [AR, PARTS, MH])
            stage_turn(p, k, k["h"], ht)
            with ExitStack() as c2:
                pdst = bf16(c2, nc, "pdst", [P, NB, PARTS, MH])
                stage_edge_parts(p, k, r, ht, w1, b1, wf, wc, pdst)
                stage_edge_mlp(p, k, r, pdst, acc, wc)
            with ExitStack() as c2:
                w2t = f32(c2, nc, "w2t", [P, 2, MH])
                wih = f32(c2, nc, "wih", [P, 2, G3])
                whh = f32(c2, nc, "whh", [P, G3])
                b2 = f32(c2, nc, "b2", [P, 2])
                fold = f32(c2, nc, "fold", [P, 2, G3])
                tail = f32(c2, nc, "tail", [3, 4 * D])
                nn = f32(c2, nc, "nn", [P, NB, 2 * D])
                rz = f32(c2, nc, "rz", [P, NB, 2 * D])
                with nc.Block() as block:
                    @block.vector
                    def _(dve):
                        dve.memset(tail[:], 0.0)
                        dve.memset(acc[:, :, MH + 1:MH + 3], 1.0)
                stage_fold(p, [(w2t[:], d["w2_t"][r].rearrange("(c p) m -> p c m", p=P)),
                               (wih[:], d["wih_t"][r].rearrange("(c p) g -> p c g", p=P)),
                               (whh[:], d["whh_t"][r]),
                               (b2[:], d["b2_c"][r]),
                               (tail[1:2, 0:G3], d["L1_gnn_gru_bih"][r:r + 1, :]),
                               (tail[2:3, 0:2 * D], d["L1_gnn_gru_bhh"][r:r + 1, 0:2 * D]),
                               (tail[2:3, G3:4 * D], d["L1_gnn_gru_bhh"][r:r + 1, 2 * D:G3])],
                           [(fold[:, m, :], [(w2t[:, c, m * P:(m + 1) * P], wih[:, c, :]) for c in range(2)]) for m in range(2)]
                           + [(tail[0:1, 0:G3], [(b2[:, c:c + 1], wih[:, c, :]) for c in range(2)])], None)
                stage_gates(p, k, lambda b, c: acc[:, b, c * P:(c + 1) * P], [fold[:, c, :] for c in range(2)],
                            lambda b: acc[:, b, MH:MH + 3], tail[:], ht, whh[:], rz, nn)
                stage_gru_end(p, rz, nn, k["h"], k["x"] if r == rounds - 1 else None)



SC = 4 * HEADS
MASKED = -BIG


def stage_attention_constants(p, a):
    nc = p.nc
    s_c, s_d = p.sig("const"), p.sig("dve_chain")
    n = [0]
    with ExitStack() as ctx:
        row = i32(ctx, nc, "row", [P, 1])
        ri = i32(ctx, nc, "ri", [P, 3])
        rf = f32(ctx, nc, "rf", [P, 3])
        ts = f32(ctx, nc, "ts", [P, GT])
        with nc.Block() as block:
            @block.gpsimd
            def _(pool):
                pool.iota(row[:], pattern=[[0, 1]], base=0, channel_multiplier=1).then_inc(s_c.sem, 1)

            @block.vector
            def _(dve):
                def chain(ins):
                    link(p, dve, s_d, ins, n)
                dve.wait_ge(s_c.sem, s_c.at(1))
                dve.tensor_scalar(ri[:, 0:1], row[:], 3, None, ALU.bitwise_and)
                dve.tensor_scalar(ri[:, 1:2], row[:], SC - 1, None, ALU.bitwise_and)
                chain(dve.tensor_scalar(ri[:, 2:3], row[:], 4, None, ALU.arith_shift_right))
                chain(dve.tensor_copy(rf[:], ri[:]))
                chain(dve.tensor_scalar(rf[:, 1:2], rf[:, 1:2], float(HEADS), None, ALU.is_ge))
                dve.tensor_scalar(a["head"][:], a["iota"][:, 0:HEADS], rf[:, 0:1], rf[:, 1:2], ALU.is_equal, ALU.mult)
                chain(dve.tensor_scalar(ts[:], a["iota"][:, 0:GT], rf[:, 2:3], None, ALU.is_equal))
                dve.tensor_copy(a["tile"][:], ts[:].unsqueeze(2).to_broadcast([P, GT, P]))
                for h in range(HEADS):
                    dve.tensor_scalar(a["masked"][:, h, :], a["ident"][:], MASKED, None, ALU.mult)
        s_c.close(1), s_d.close(n[0])


def stage_score_table(p, score, table):
    nc = p.nc
    s_dve, s_st = p.sig("dve_chain"), p.sig("store0")
    n = [0]
    with ExitStack() as ctx:
        row = f32(ctx, nc, "srow", [P, NB, SC])
        half = ctx.enter_context(nc.sbuf_tensor(unique("half"), [P, NB, HEADS], mybir.dt.bfloat16))
        left = f32(ctx, nc, "left", [P, NB, HEADS])
        with nc.Block() as block:
            @block.vector
            def _(dve):
                def chain(ins):
                    link(p, dve, s_dve, ins, n)
                chain(dve.tensor_copy(row[:, :, 0:HEADS], score))
                chain(dve.tensor_copy(left[:], score))
                for part in range(1, 4):
                    out = row[:, :, part * HEADS:(part + 1) * HEADS]
                    chain(dve.tensor_copy(half[:], left[:]))
                    chain(dve.tensor_copy(out, half[:]))
                    chain(dve.tensor_tensor(left[:], left[:], out, ALU.subtract))

            @block.sync
            def _(sp):
                sp.wait_ge(s_dve.sem, s_dve.at(n[0]))
                sp.dma_start(table.rearrange("(b p) f -> p b f", p=P), row[:]).then_inc(s_st.sem, 16)
                sp.wait_ge(s_st.sem, s_st.at(16))
        s_dve.close(n[0]), s_st.close(16)


def stage_edge_max(p, k, a, score, mx):
    nc, d = p.nc, p.d
    BF = mybir.dt.bfloat16
    s_oh, s_turn, s_spread = p.sig("onehot"), p.sig("turn"), p.sig("spread")
    s_bank, s_red, s_max, s_se = p.sig("pre"), p.sig("added"), p.sig("acc"), p.sig("scaled")
    with ExitStack() as ctx:
        ga = Gather(p, ctx, d["t_score"], k["src"], SC)
        away = ctx.enter_context(nc.sbuf_tensor(unique("away"), [P, 2, GT, P], BF))
        spread = ctx.enter_context(nc.sbuf_tensor(unique("spread"), [P, 2, HEADS, P], BF))
        tmax = f32(ctx, nc, "tmax", [P, GU, HEADS])
        tb = [bank(ctx, nc, f"tb{q}") for q in range(2)]
        vb = ctx.enter_context(nc.psum_tensor(unique("vb"), [P, 4, 512], F32))
        with nc.Block() as block:
            @block.gpsimd
            def _(pool):
                ga.program(pool)

            @block.scalar
            def _(act):
                ga.feed(act, 0, 0)

                def body(i, first, last):
                    for q in range(2):
                        g = 2 * i + q
                        if not (last and q == 1):
                            if not (first and q == 0):
                                act.wait_ge(s_se.sem, s_se.at(g))
                                p.apart(act)
                                act.wait_ge(s_turn.sem, s_turn.at(g))
                                p.apart(act)
                            ga.feed(act, g + 1, 1 - q)
                        for v in range(GU):
                            act.wait_ge(ga.s_row[GU * q + v].sem, ga.s_row[GU * q + v].at(32 * (i + 1)))
                            p.apart(act)
                        act.copy(score[:, bass.ds(g * GT, GT), :], ga.rows[:, q, :, 0:HEADS]).then_inc(s_se.sem, 1)
                over_bodies(act, body)

            @block.tensor
            def _(pe):
                def turn(i, g, q, first):
                    for v in range(GU):
                        pe.wait_ge(ga.s_row[GU * q + v].sem, ga.s_row[GU * q + v].at(32 * (i + 1)))
                    if not first:
                        pe.wait_ge(s_spread.sem, s_spread.at(g - 1))
                    pe.transpose(tb[q][:, 0:P], ga.rows[:, q].rearrange("p t c -> p (t c)"), k["ident"][:]).then_inc(s_turn.sem, 1)
                turn(0, 0, 0, True)

                def body(i, first, last):
                    for q in range(2):
                        g = 2 * i + q
                        pe.wait_ge(s_oh.sem, s_oh.at(g + 1))
                        pe.wait_ge(s_spread.sem, s_spread.at(g + 1))
                        for v in range(GU):
                            u = 4 * g + v
                            if not (first and q == 0 and v < 2):
                                pe.wait_ge(s_red.sem, s_red.at(u - 1))
                            for t in range(2):
                                o, j = vb[:, 2 * (v % 2) + t, :], 2 * v + t
                                pe.matmul(o, away[:, q, j, :], a["masked"][:].rearrange("p h e -> p (h e)"), start=True, stop=False)
                                mm = pe.matmul(o, a["tile"][:, j, :], spread[:, q].rearrange("p h e -> p (h e)"), start=False, stop=True)
                            mm.then_inc(s_bank.sem, 1)
                            if v == 2 and not (last and q == 1):
                                turn(i + q, g + 1, 1 - q, first and q == 0)
                over_bodies(pe, body)

            @block.vector
            def _(dve):
                def masks(g, q):
                    onehot16(dve, k, away, g, q, ALU.not_equal).then_inc(s_oh.sem, 1)

                def parts(g, q):
                    dve.wait_ge(s_turn.sem, s_turn.at(g + 1))
                    dve.tensor_tensor(spread[:, q], tb[q][:, 0:P].unsqueeze(1).to_broadcast([P, HEADS, P]),
                                      a["head"][:].unsqueeze(2).to_broadcast([P, HEADS, P]), ALU.mult).then_inc(s_spread.sem, 1)

                def merge(u, o, b):
                    dve.wait_ge(s_red.sem, s_red.at(u + 1))
                    if not (isinstance(u, int) and u == 0):
                        dve.wait_ge(s_max.sem, s_max.at(u))
                    m = mx[:, bass.ds(b, 1), :].rearrange("p a h -> p (a h)")
                    dve.tensor_tensor(m, m, tmax[:, o, :], ALU.max).then_inc(s_max.sem, 1)
                masks(0, 0)
                parts(0, 0)

                def body(i, first, last):
                    for q in range(2):
                        g = 2 * i + q
                        blocks = unit_blocks(nc, dve, k, g, 1)
                        for v in range(GU):
                            u = 4 * g + v
                            dve.wait_ge(s_bank.sem, s_bank.at(u + 1))
                            dve.tensor_reduce(tmax[:, v, :], vb[:, 2 * (v % 2):2 * (v % 2) + 2, :].rearrange("p t (h e) -> p h t e", h=HEADS),
                                              AX.XY, ALU.max).then_inc(s_red.sem, 1)
                            if v == 1 and not (last and q == 1):
                                if not (first and q == 0):
                                    dve.wait_ge(s_bank.sem, s_bank.at(4 * g))
                                masks(g + 1, 1 - q)
                            if v == 3 and not (last and q == 1):
                                parts(g + 1, 1 - q)
                            if not (first and q == 0 and v == 0):
                                merge(u - 1, (v - 1) % GU, blocks[v])
                over_bodies(dve, body)
                merge(UNITS - 1, GU - 1, unit_blocks(nc, dve, k, GROUPS, 1)[0])
        ga.close()
        for s in (s_oh, s_turn, s_spread, s_se):
            s.close(GROUPS)
        for s in (s_bank, s_red, s_max):
            s.close(UNITS)


def stage_shift(p, k, sd, mx, adm3, ss=None, xw=None, acc=None):
    nc = p.nc
    s_dve, s_var, s_std = p.sig("dve_chain"), p.sig("var"), p.sig("std")
    n = [0]
    with ExitStack() as ctx:
        t = f32(ctx, nc, "shift", [P, NB, HEADS])
        adm = f32(ctx, nc, "adm", [P, NB, 2 * HEADS])
        e = f32(ctx, nc, "self", [P, NB, HEADS])
        with nc.Block() as block:
            @block.vector
            def _(dve):
                def chain(ins):
                    link(p, dve, s_dve, ins, n)
                ad, m = adm[:, :, 0:HEADS], adm[:, :, HEADS:2 * HEADS]
                chain(dve.tensor_copy(ad, sd))
                chain(dve.tensor_tensor(t[:], mx[:], ad, ALU.add))
                chain(dve.scalar_tensor_tensor(out=m, in0=t[:], scalar=SLOPE, in1=t[:], op0=ALU.mult, op1=ALU.max))
                if ss is not None:
                    chain(dve.tensor_tensor(e[:], ss, ad, ALU.add))
                    chain(dve.scalar_tensor_tensor(out=t[:], in0=e[:], scalar=SLOPE, in1=e[:], op0=ALU.mult, op1=ALU.max))
                    dve.tensor_tensor(e[:], t[:], m, ALU.subtract).then_inc(s_var.sem, 1)
                    dve.wait_ge(s_std.sem, s_std.at(1))
                    den = acc[:, :, D:D + HEADS]
                    chain(dve.tensor_copy(den, e[:]))
                    c = D // HEADS
                    for h in range(HEADS):
                        chain(dve.tensor_tensor(acc[:, :, h * c:(h + 1) * c], xw[:, :, h * c:(h + 1) * c],
                                                e[:, :, h:h + 1].to_broadcast([P, NB, c]), ALU.mult))
                else:
                    chain(dve.memset(acc[:], 0.0))
                for part in range(PARTS):
                    chain(dve.tensor_copy(adm3[:, :, part, :], adm[:]))
                    if part < PARTS - 1:
                        chain(dve.tensor_tensor(adm[:], adm[:], adm3[:, :, part, :], ALU.subtract))

            if ss is not None:
                @block.scalar
                def _(act):
                    act.wait_ge(s_var.sem, s_var.at(1))
                    act.activation(e[:], e[:], ACT.Exp).then_inc(s_std.sem, 1)
        s_dve.close(n[0])
        if ss is not None:
            s_var.close(1), s_std.close(1)


def stage_attend(p, k, table, score, adm, acc, wide):
    nc = p.nc
    W = HEADS * D if wide else D
    s_oh, s_oh16, s_turn, s_oht = p.sig("onehot"), p.sig("onehot16"), p.sig("turn"), p.sig("oht")
    s_em, s_z, s_w, s_c = p.sig("pre"), p.sig("added"), p.sig("relu"), p.sig("dve_chain")
    s_rd, s_ra, s_agg, s_acc = p.sig("scaled"), p.sig("spread"), p.sig("agg"), p.sig("acc")
    DH = HEADS // 2
    with ExitStack() as ctx:
        ga = Gather(p, ctx, table, k["src"], D)
        oh = f32(ctx, nc, "oh", [P, 2, GT, P])
        oh16 = bf16(ctx, nc, "oh16", [P, 2, GT, P])
        oht = bf16(ctx, nc, "oht", [P, 2, GT, P])
        z = f32(ctx, nc, "z", [P, 2, GT, HEADS])
        y = f32(ctx, nc, "y", [P, 2, GT, HEADS])
        if wide:
            wr = f32(ctx, nc, "wr", [P, 2, 2, W])
            w = f32(ctx, nc, "w", [P, 2, GT, HEADS])
        else:
            wr = f32(ctx, nc, "wr", [P, 2, GT, W + HEADS])
            w = wr[:, :, :, W:W + HEADS]
        tp = [ctx.enter_context(nc.psum_tensor(unique("tp"), [P, GT * P], BF16)) for q in range(2)]
        em = [bank(ctx, nc, f"em{q}") for q in range(2)]
        pa = [bank(ctx, nc, f"pa{q}") for q in range(2)]
        pd = [bank(ctx, nc, f"pd{q}") for q in range(2)] if wide else None
        with nc.Block() as block:
            @block.gpsimd
            def _(pool):
                ga.program(pool)

            @block.scalar
            def _(act):
                def onehots(g, q, first):
                    if not first:
                        act.wait_ge(s_agg.sem, s_agg.at(4 * g - 4))
                        p.apart(act)
                    act.wait_ge(s_oh16.sem, s_oh16.at(g + 1))
                    act.copy(oh[:, q].rearrange("p t n -> p (t n)"), oh16[:, q].rearrange("p t n -> p (t n)")).then_inc(s_oh.sem, 1)

                def turned(g, q, first):
                    if not first:
                        act.wait_ge(s_em.sem, s_em.at(g - 1))
                        p.apart(act)
                    act.wait_ge(s_turn.sem, s_turn.at(g + 1))
                    act.copy(oht[:, q].rearrange("p t n -> p (t n)"), tp[q][:]).then_inc(s_oht.sem, 1)

                def weights(g, q, first):
                    if not first:
                        act.wait_ge(s_agg.sem, s_agg.at(4 * g - 4))
                        p.apart(act)
                    act.wait_ge(s_z.sem, s_z.at(g + 1))
                    act.activation(w[:, q], z[:, q], ACT.Exp).then_inc(s_w.sem, 1)
                ga.feed(act, 0, 0)
                turned(0, 0, True)
                if wide:
                    onehots(0, 0, True)
                weights(0, 0, True)

                def body(i, first, last):
                    for q in range(2):
                        g = 2 * i + q
                        if not (last and q == 1):
                            if not (first and q == 0):
                                act.wait_ge(s_rd.sem, s_rd.at(4 * g))
                                p.apart(act)
                            ga.feed(act, g + 1, 1 - q)
                        for v in range(GU):
                            u = 4 * g + v
                            if wide:
                                if v == 0:
                                    act.wait_ge(s_w.sem, s_w.at(g + 1))
                                    p.apart(act)
                                act.wait_ge(ga.s_row[GU * q + v].sem, ga.s_row[GU * q + v].at(32 * (i + 1)))
                                p.apart(act)
                                if not (first and q == 0 and v < 2):
                                    act.wait_ge(s_agg.sem, s_agg.at(u - 1))
                                    p.apart(act)
                                for t in range(2):
                                    j = 2 * v + t
                                    for h in range(DH, HEADS):
                                        last_i = act.activation(wr[:, v % 2, t, h * D:(h + 1) * D], ga.rows[:, q, j, :], ACT.Copy,
                                                                scale=w[:, q, j, h:h + 1])
                                last_i.then_inc(s_ra.sem, 1)
                            if v == 1 and not (last and q == 1):
                                turned(g + 1, 1 - q, first and q == 0)
                            if v == 2 and wide and not (last and q == 1):
                                onehots(g + 1, 1 - q, first and q == 0)
                        if not (last and q == 1):
                            weights(g + 1, 1 - q, first and q == 0)
                over_bodies(act, body)

            @block.tensor
            def _(pe):
                def turn(g, q, first):
                    pe.wait_ge(s_oh16.sem, s_oh16.at(g + 1))
                    if not first:
                        pe.wait_ge(s_oht.sem, s_oht.at(g - 1))
                    turn_onehots(pe, k, oh16, tp, q, s_turn)

                def values(g, q, first):
                    if not first:
                        pe.wait_ge(s_z.sem, s_z.at(g - 1))
                    blocks = unit_blocks(nc, pe, k, g)
                    pe.wait_ge(s_oht.sem, s_oht.at(g + 1))
                    for v in range(GU):
                        for t in range(2):
                            j = 2 * v + t
                            for c in range(PARTS):
                                mm = pe.matmul(em[q][:, 8 * j:8 * j + 8], oht[:, q, j, :],
                                               adm[:, bass.ds(blocks[v], 1), c, :].rearrange("p a f -> p (a f)"),
                                               start=c == 0, stop=c == PARTS - 1)
                    mm.then_inc(s_em.sem, 1)
                turn(0, 0, True)
                values(0, 0, True)

                def body(i, first, last):
                    for q in range(2):
                        g = 2 * i + q
                        for v in range(GU):
                            u = 4 * g + v
                            pe.wait_ge(s_rd.sem, s_rd.at(u + 1))
                            if v == 0:
                                pe.wait_ge(s_w.sem, s_w.at(g + 1))
                                pe.wait_ge(s_oh.sem, s_oh.at(g + 1))
                            if wide:
                                pe.wait_ge(s_ra.sem, s_ra.at(u + 1))
                            if not (first and q == 0 and v < 2):
                                pe.wait_ge(s_acc.sem, s_acc.at(u - 1))
                            for t in range(2):
                                j = 2 * v + t
                                if wide:
                                    pe.matmul(pa[v % 2][:, 0:W], oh[:, q, j, :], wr[:, v % 2, t, :], start=t == 0, stop=t == 1)
                                    mm = pe.matmul(pd[v % 2][:, 0:HEADS], oh[:, q, j, :], w[:, q, j, :], start=t == 0, stop=t == 1)
                                else:
                                    mm = pe.matmul(pa[v % 2][:, 0:W + HEADS], oh[:, q, j, :], wr[:, q, j, :], start=t == 0, stop=t == 1)
                            mm.then_inc(s_agg.sem, 1)
                            if v == 0 and not (last and q == 1):
                                turn(g + 1, 1 - q, first and q == 0)
                            if v == 1 and not (last and q == 1):
                                values(g + 1, 1 - q, first and q == 0)
                over_bodies(pe, body)

            @block.vector
            def _(dve):
                def onehots16(g, q, first):
                    if not first:
                        dve.wait_ge(s_turn.sem, s_turn.at(g - 1))
                        if wide:
                            dve.wait_ge(s_oh.sem, s_oh.at(g - 1))
                    onehot16(dve, k, oh16, g, q).then_inc(s_oh16.sem, 1)

                def onehots(g, q, first):
                    if not first:
                        dve.wait_ge(s_agg.sem, s_agg.at(4 * g - 4))
                    onehot(p, dve, k, oh, g, q).then_inc(s_oh.sem, 1)

                def exponents(g, q, first):
                    dve.wait_ge(s_em.sem, s_em.at(g + 1))
                    if not first:
                        dve.wait_ge(s_w.sem, s_w.at(g - 1))
                    e = em[q][:, 0:8 * GT].rearrange("p (t f) -> p t f", t=GT)
                    dve.tensor_tensor(y[:, q], e[:, :, 0:HEADS], score[:, bass.ds(g * GT, GT), :], ALU.add).then_inc(s_c.sem, 1)
                    dve.wait_ge(s_c.sem, s_c.at(2 * g + 1))
                    dve.scalar_tensor_tensor(out=y[:, q], in0=y[:, q], scalar=SLOPE, in1=y[:, q],
                                             op0=ALU.mult, op1=ALU.max).then_inc(s_c.sem, 1)
                    dve.wait_ge(s_c.sem, s_c.at(2 * g + 2))
                    dve.tensor_tensor(z[:, q], y[:, q], e[:, :, HEADS:2 * HEADS], ALU.subtract).then_inc(s_z.sem, 1)

                def add(u, x, b):
                    dve.wait_ge(s_agg.sem, s_agg.at(u + 1))
                    if not (isinstance(u, int) and u == 0):
                        dve.wait_ge(s_acc.sem, s_acc.at(u))
                    n = W if wide else W + HEADS
                    a = acc[:, bass.ds(b, 1), 0:n].rearrange("p a f -> p (a f)")
                    if wide:
                        c = acc[:, bass.ds(b, 1), W:W + HEADS].rearrange("p a f -> p (a f)")
                        dve.tensor_tensor(c, c, pd[x % 2][:, 0:HEADS], ALU.add)
                    dve.tensor_tensor(a, a, pa[x % 2][:, 0:n], ALU.add).then_inc(s_acc.sem, 1)

                onehots16(0, 0, True)
                if not wide:
                    onehots(0, 0, True)
                exponents(0, 0, True)

                def body(i, first, last):
                    for q in range(2):
                        g = 2 * i + q
                        blocks = unit_blocks(nc, dve, k, g, 1)
                        for v in range(GU):
                            u, x = 4 * g + v, GU * q + v
                            dve.wait_ge(ga.s_row[x].sem, ga.s_row[x].at(32 * (i + 1)))
                            if v == 0:
                                dve.wait_ge(s_w.sem, s_w.at(g + 1))
                            if wide and not (first and x < 2):
                                dve.wait_ge(s_agg.sem, s_agg.at(u - 1))
                            if not wide and not first:
                                dve.wait_ge(s_agg.sem, s_agg.at(4 * g - 4))
                            for t in range(2):
                                j = 2 * v + t
                                if wide:
                                    last_i = dve.tensor_tensor(wr[:, v % 2, t, 0:DH * D].rearrange("p (h f) -> p h f", h=DH),
                                                               ga.rows[:, q, j, :].unsqueeze(1).to_broadcast([P, DH, D]),
                                                               w[:, q, j, 0:DH].unsqueeze(2).to_broadcast([P, DH, D]), ALU.mult)
                                else:
                                    last_i = dve.tensor_tensor(wr[:, q, j, 0:W].rearrange("p (h f) -> p h f", h=HEADS),
                                                               ga.rows[:, q, j, :].rearrange("p (h f) -> p h f", h=HEADS),
                                                               w[:, q, j, :].unsqueeze(2).to_broadcast([P, HEADS, D // HEADS]), ALU.mult)
                            last_i.then_inc(s_rd.sem, 1)
                            if not (first and x == 0):
                                add(u - 1, (x - 1) % BU, blocks[v])
                            if v == 0 and not (last and q == 1):
                                onehots16(g + 1, 1 - q, first and q == 0)
                            if v == 1 and not wide and not (last and q == 1):
                                onehots(g + 1, 1 - q, first and q == 0)
                            if v == 2 and not (last and q == 1):
                                exponents(g + 1, 1 - q, first and q == 0)
                over_bodies(dve, body)
                add(UNITS - 1, BU - 1, unit_blocks(nc, dve, k, GROUPS, 1)[0])
        ga.close()
        s_oh.close(GROUPS), s_oh16.close(GROUPS), s_turn.close(GROUPS), s_oht.close(GROUPS), s_c.close(2 * GROUPS)
        for s in (s_em, s_z, s_w):
            s.close(GROUPS)
        for s in (s_rd, s_agg, s_acc):
            s.close(UNITS)
        if wide:
            s_ra.close(UNITS)


def stage_vector(p, loads, steps):
    nc = p.nc
    s_ld, s_dve = p.sig("load"), p.sig("dve_chain")
    n = [0]
    with nc.Block() as block:
        @block.sync
        def _(sp):
            for dst, src in loads:
                sp.dma_start(dst, src).then_inc(s_ld.sem, 16)

        @block.vector
        def _(dve):
            if loads:
                dve.wait_ge(s_ld.sem, s_ld.at(16 * len(loads)))
            for step in steps:
                link(p, dve, s_dve, step(dve), n)
    s_ld.close(16 * len(loads)), s_dve.close(n[0])


def layer_attention(p, k):
    nc, d = p.nc, p.d
    BF = mybir.dt.bfloat16
    stage_norm(p, k["x"], k["h"])
    with ExitStack() as ctx:
        acc = f32(ctx, nc, "acc", [P, NB, D + HEADS])
        skip = f32(ctx, nc, "skip", [P, NB, D])
        xw = f32(ctx, nc, "xw", [P, NB, D])
        sc = f32(ctx, nc, "sc", [P, 2, NB, HEADS])
        mx = f32(ctx, nc, "mx", [P, NB, HEADS])
        adm = bf16(ctx, nc, "adm3", [P, NB, PARTS, 2 * HEADS])
        with ExitStack() as c2:
            ht = f32(c2, nc, "ht", [P, NPAD])
            xn = f32(c2, nc, "xn", [P, NB, D])
            w = f32(c2, nc, "w2", [P, 2, D])
            bp = f32(c2, nc, "bp", [1, D])
            gb = f32(c2, nc, "gb", [P, 4, D])
            tmp = f32(c2, nc, "stmp", [P, NB, D])

            def lhs(b):
                return ht[:, b * P:(b + 1) * P]
            stage_turn(p, k, k["h"], ht)
            stage_project(p, k, ht, [(w[:, 0, :], d["L2_gnn_W_proj"]), (w[:, 1, :], d["L2_gnn_W_gat"]),
                                     (bp[:], d["L2_gnn_b_proj"].rearrange("(a f) -> a f", a=1))] +
                          [(gb[:, j, :], v.partition_broadcast(P)) for j, v in enumerate(
                              (d["L2_gnn_gamma"], d["L2_gnn_beta"], d["L2_gnn_att_src"].rearrange("h c -> (h c)"),
                               d["L2_gnn_att_dst"].rearrange("h c -> (h c)")))],
                          [(0, D, lhs, w[:, 0, :]), (0, D, lambda b: k["ones"][0:1, 0:P], bp[:])], D, skip)
            stage_norm(p, k["h"], xn, relu=False, gamma=gb[:, 0, :], beta=gb[:, 1, :])
            stage_turn(p, k, xn, ht)
            stage_project(p, k, ht, [], [(0, D, lhs, w[:, 1, :])], D, xw)
            stage_store_rows(p, d["t_att"], xw[:])
            steps = []
            for j in range(2):
                steps.append(lambda dve, j=j: dve.tensor_tensor(tmp[:], xw[:], gb[:, 2 + j, :].unsqueeze(1).to_broadcast([P, NB, D]), ALU.mult))
                steps.append(lambda dve, j=j: dve.tensor_reduce(sc[:, j], tmp[:].rearrange("p b (h c) -> p b h c", h=HEADS), AX.X, ALU.add))
            steps.append(lambda dve: dve.tensor_copy(mx[:], sc[:, 0]))
            stage_vector(p, [], steps)
        stage_score_table(p, sc[:, 0], d["t_score"])
        with ExitStack() as c2:
            es = f32(c2, nc, "es", [P, TILES, HEADS])
            with ExitStack() as c3:
                a = {"iota": k["iota"], "ident": k["ident"], "head": f32(c3, nc, "head", [P, HEADS]),
                     "tile": c3.enter_context(nc.sbuf_tensor(unique("tile"), [P, GT, P], BF)),
                     "masked": c3.enter_context(nc.sbuf_tensor(unique("masked"), [P, HEADS, P], BF))}
                stage_attention_constants(p, a)
                stage_edge_max(p, k, a, es, mx)
            stage_shift(p, k, sc[:, 1], mx, adm, sc[:, 0], xw, acc)
            stage_attend(p, k, d["t_att"], es, adm, acc, False)
        with ExitStack() as c2:
            bias = f32(c2, nc, "bgat", [P, D])
            num, den = acc[:, :, 0:D], acc[:, :, D:D + HEADS]
            c = D // HEADS
            stage_vector(p, [(bias[:], d["L2_gnn_bias_gat"].partition_broadcast(P))], [
                lambda dve: dve.tensor_scalar(den, den, 1e-16, None, ALU.add),
                lambda dve: dve.reciprocal(den, den)] + [
                lambda dve, h=h: dve.tensor_tensor(acc[:, :, h * c:(h + 1) * c], acc[:, :, h * c:(h + 1) * c],
                                                   acc[:, :, D + h:D + h + 1].to_broadcast([P, NB, c]), ALU.mult) for h in range(HEADS)] + [
                lambda dve: dve.tensor_tensor(num, num, bias[:].unsqueeze(1).to_broadcast([P, NB, D]), ALU.add),
                lambda dve: dve.tensor_tensor(num, num, skip[:], ALU.add),
                lambda dve: dve.scalar_tensor_tensor(out=k["x"][:], in0=num, scalar=0.0, in1=k["x"][:], op0=ALU.max, op1=ALU.add)])


def layer_attention_gru(p, k):
    nc, d = p.nc, p.d
    BF = mybir.dt.bfloat16
    stage_norm(p, k["x"], k["h"])
    with ExitStack() as ctx:
        acc = f32(ctx, nc, "acc", [P, NB, HEADS * D + HEADS])
        ht = f32(ctx, nc, "ht", [P, NPAD])
        adm = bf16(ctx, nc, "adm3", [P, NB, PARTS, 2 * HEADS])
        fold = f32(ctx, nc, "fold", [P, HEADS, G3])
        whh = f32(ctx, nc, "whh", [P, G3])
        tail = f32(ctx, nc, "tail", [2, 4 * D])
        with ExitStack() as c1:
            es = f32(c1, nc, "es", [P, TILES, HEADS])
            sc = f32(c1, nc, "sc", [P, NB, 2 * HEADS])
            mx = f32(c1, nc, "mx", [P, NB, HEADS])
            with ExitStack() as c2:
                wt = f32(c2, nc, "wt", [P, HEADS, D])
                wih = f32(c2, nc, "wih", [P, HEADS, G3])
                at = f32(c2, nc, "at", [P, 2, HEADS])
                vec = f32(c2, nc, "vec", [P, 2 * HEADS])
                stage_vector(p, [], [lambda dve: dve.memset(tail[:], 0.0), lambda dve: dve.memset(mx[:], MASKED)])
                stage_turn(p, k, k["h"], ht)
                stage_store_rows(p, d["t_att"], k["h"][:])
                stage_fold(p, [(wt[:], d["w3_t"].rearrange("h e d -> e h d")),
                               (wih[:], d["wih3_t"].rearrange("(h e) g -> e h g", h=HEADS)),
                               (whh[:], d["whh3_t"]), (at[:], d["a3_t"]),
                               (tail[0:1, 0:G3], d["L3_gnn_b_ih"].rearrange("(a g) -> a g", a=1)),
                               (tail[1:2, 0:2 * D], d["L3_gnn_b_hh"][0:2 * D].rearrange("(a g) -> a g", a=1)),
                               (tail[1:2, G3:4 * D], d["L3_gnn_b_hh"][2 * D:G3].rearrange("(a g) -> a g", a=1))],
                           [(fold[:, h, :], [(wt[:, h, :], wih[:, h, :])]) for h in range(HEADS)] +
                           [(vec[:, j * HEADS + h:j * HEADS + h + 1], [(wt[:, h, :], at[:, j, h:h + 1])]) for j in range(2) for h in range(HEADS)], None)
                stage_project(p, k, ht, [], [(0, 2 * HEADS, lambda b: ht[:, b * P:(b + 1) * P], vec[:])], 2 * HEADS, sc)
            stage_score_table(p, sc[:, :, 0:HEADS], d["t_score"])
            with ExitStack() as c3:
                a = {"iota": k["iota"], "ident": k["ident"], "head": f32(c3, nc, "head", [P, HEADS]),
                     "tile": c3.enter_context(nc.sbuf_tensor(unique("tile"), [P, GT, P], BF)),
                     "masked": c3.enter_context(nc.sbuf_tensor(unique("masked"), [P, HEADS, P], BF))}
                stage_attention_constants(p, a)
                stage_edge_max(p, k, a, es, mx)
            stage_shift(p, k, sc[:, :, HEADS:2 * HEADS], mx, adm, acc=acc)
            stage_attend(p, k, d["t_att"], es, adm, acc, True)
        W = HEADS * D
        den = acc[:, :, W:W + HEADS]
        stage_vector(p, [], [
            lambda dve: dve.tensor_scalar(den, den, 1e-30, None, ALU.max),
            lambda dve: dve.reciprocal(den, den)] + [
            lambda dve, h=h: dve.tensor_tensor(acc[:, :, h * D:(h + 1) * D], acc[:, :, h * D:(h + 1) * D],
                                               acc[:, :, W + h:W + h + 1].to_broadcast([P, NB, D]), ALU.mult) for h in range(HEADS)])
        with ExitStack() as c2:
            rz = f32(c2, nc, "rz", [P, NB, 2 * D])
            nn = f32(c2, nc, "nn", [P, NB, 2 * D])
            stage_gates(p, k, lambda b, c: acc[:, b, c * P:(c + 1) * P], [fold[:, h, :] for h in range(HEADS)],
                        lambda b: k["ones"][:, 0:2], tail[:], ht, whh[:], rz, nn)
            stage_gru_end(p, rz, nn, k["h"], k["x"])


def build(nc, d, out):
    with ExitStack() as ctx:
        p = Program(nc, ctx, d)
        k = {"x": f32(ctx, nc, "x", [P, NB, D]), "h": f32(ctx, nc, "h", [P, NB, D]),
             "ident": f32(ctx, nc, "ident", [P, P]), "ones": f32(ctx, nc, "ones", [P, P]),
             "tri": f32(ctx, nc, "tri", [P, P]), "iota": f32(ctx, nc, "iota", [P, UNITS]),
             "iota_i": i32(ctx, nc, "iota_i", [P, UNITS]), "bmap": i32(ctx, nc, "bmap", [1, LAGS, UNITS + 8]),
             "meta": f32(ctx, nc, "meta", [P, TILES]), "src": i32(ctx, nc, "src", [P, TILES]),
             "ident16": bf16(ctx, nc, "ident16", [P, P]), "iota16": bf16(ctx, nc, "iota16", [P, P]),
             "meta16": bf16(ctx, nc, "meta16", [P, TILES])}
        stage_constants(p, k)
        with ExitStack() as c2:
            s = {"meta": f32(c2, nc, "smeta", [SORT_P, SORT_J, 4]), "pos": i32(c2, nc, "pos", [SORT_P, SORT_J])}
            ht = f32(c2, nc, "ht", [P, NPAD])
            stage_norm(p, k["x"], k["h"])
            stage_turn(p, k, k["h"], ht)
            stage_positions(p, k, s)
            stage_scatter(p, k, s, ht)
        layer_relational(p, k)
        layer_edge_mlp(p, k)
        layer_attention(p, k)
        layer_attention_gru(p, k)
        s_out = p.sig("out")
        with nc.Block() as block:
            @block.sync
            def _(sp):
                sp.dma_start(out[0:(NB - 1) * P, :].rearrange("(b p) f -> p b f", p=P), k["x"][:, 0:NB - 1, :]).then_inc(s_out.sem, 16)
                sp.dma_start(out[(NB - 1) * P:N_NODES, :], k["x"][0:LAST_ROWS, NB - 1, :]).then_inc(s_out.sem, 16)
                sp.wait_ge(s_out.sem, 32)


_INS = ["x", "src", "dst", "edge_attr_26", "edge_type_8", "edge_weight1", "L0_gnn_weight", "L0_gnn_bias",
        "L1_gnn_mlp_w1", "L1_gnn_mlp_b1", "L1_gnn_gru_bih", "L1_gnn_gru_bhh", "w2_t", "wih_t", "whh_t", "b2_c",
        "L2_gnn_gamma", "L2_gnn_beta", "L2_gnn_W_gat", "L2_gnn_att_src", "L2_gnn_att_dst", "L2_gnn_bias_gat",
        "L2_gnn_W_proj", "L2_gnn_b_proj", "w3_t", "a3_t", "wih3_t", "whh3_t", "L3_gnn_b_ih", "L3_gnn_b_hh"]
_SCRATCH = [("records", (SLOTS, REC)),  ("t_rel", (NPAD * N_REL, D)), ("t_mlp", (NPAD, MH)),
            ("t_att", (NPAD, D)), ("t_score", (NPAD, SC))]


def kernel(**inputs):
    import numpy as _np
    import concourse.bacc as _bacc
    from concourse import mybir as _mybir
    from concourse.bass_utils import run_bass_kernel_spmd as _run

    inputs = dict(inputs)
    inputs["w2_t"] = _np.transpose(inputs["L1_gnn_mlp_w2"], (0, 2, 1))
    inputs["wih_t"] = _np.transpose(inputs["L1_gnn_gru_wih"], (0, 2, 1))
    inputs["whh_t"] = _np.transpose(inputs["L1_gnn_gru_whh"], (0, 2, 1))
    inputs["b2_c"] = _np.transpose(_np.reshape(inputs["L1_gnn_mlp_b2"], (2, 2, 128)), (0, 2, 1))
    inputs["w3_t"] = _np.transpose(inputs["L3_gnn_W"], (0, 2, 1))
    inputs["a3_t"] = _np.transpose(_np.reshape(inputs["L3_gnn_a"], (4, 2, 128)), (2, 1, 0))
    inputs["wih3_t"] = _np.transpose(inputs["L3_gnn_W_ih"])
    inputs["whh3_t"] = _np.transpose(inputs["L3_gnn_W_hh"])
    nc = _bacc.Bacc("TRN2", target_bir_lowering=False, num_devices=1)
    arrays, d = {}, {}
    for name in _INS:
        a = _np.ascontiguousarray(inputs[name])
        arrays[f"in_{name}"] = a
        d[name] = nc.dram_tensor(f"in_{name}", a.shape, _mybir.dt.from_np(a.dtype), kind="ExternalInput").ap()
    d["attr_t"] = nc.dram_tensor("attr_t", (AR, SLOTS), BF16).ap()
    for name, shape in _SCRATCH:
        d[name] = nc.dram_tensor(name, shape, F32).ap()
    out = nc.dram_tensor("out_0", (N_NODES, D), F32, kind="ExternalOutput").ap()
    build(nc, d, out)
    return _run(nc, [arrays], core_ids=[0]).results[0]["out_0"]
```

```python
from contextlib import ExitStack

import concourse.bass as bass
from concourse import mybir

F32 = mybir.dt.float32
I32 = mybir.dt.int32
BF16 = mybir.dt.bfloat16
ALU = mybir.AluOpType
ACT = mybir.ActivationFunctionType
AX = mybir.AxisListType

P = 128
N_NODES, D = 3125, 128
N_EDGES = 100000
N_ATTR = 26
N_REL = 8
HEADS = 4
MH = 256
NB = -(-N_NODES // P)
NPAD = NB * P
LAST_ROWS = N_NODES - (NB - 1) * P
G3 = 3 * D

SORT_P = 125
SORT_J = N_EDGES // SORT_P
UNIT = 2 * P
UNITS = -(-(N_EDGES + NB * (UNIT - 1)) // UNIT)
GT = 8
GU = GT // 2
GROUPS = -(-UNITS // GU)
UNITS = GROUPS * GU
TILES = GROUPS * GT
SLOTS = TILES * P
BODIES = GROUPS // 2
BU = 2 * GU
PARTS = 3
AR = 96
REC = AR // 2 + 4
F_NORM, F_DST, F_SRC, F_HW = (AR // 2 + j for j in range(4))
LAGS = 3
BIG = 1.0e30
EPS = 1e-5
SLOPE = 0.2
INIT = 8

ROWS = PARTS * N_ATTR
PACK = PARTS * ROWS // 2
CUT = PACK - ROWS
PIECES = [[(0, 0, ROWS, 0), (ROWS, 0, CUT, 1)],
          [(0, CUT, ROWS - CUT, 1), (ROWS - CUT, 0, ROWS, 2)]]


class Signal:

    def __init__(self, sem):
        self.sem = sem
        self.base = 0

    def at(self, n):
        return n + self.base

    def close(self, n):
        self.base += n


class Program:
    def __init__(self, nc, ctx, dram):
        self.nc, self.ctx, self.d = nc, ctx, dram
        self.signals = {}

    def sig(self, name):
        if name not in self.signals:
            self.signals[name] = Signal(self.ctx.enter_context(self.nc.semaphore(name)))
        return self.signals[name]

    def apart(self, eng):
        eng.sem_inc(self.sig("apart").sem, 1)


def unique(name, used={}):
    used[name] = used.get(name, 0) + 1
    return f"{name}_{used[name]}"


def f32(ctx, nc, name, shape):
    return ctx.enter_context(nc.sbuf_tensor(unique(name), shape, F32))


def i32(ctx, nc, name, shape):
    return ctx.enter_context(nc.sbuf_tensor(unique(name), shape, I32))


def bf16(ctx, nc, name, shape):
    return ctx.enter_context(nc.sbuf_tensor(unique(name), shape, BF16))


def unit_blocks(nc, eng, k, g, lag=0):
    _, blocks = nc.values_load_multi_w_load_instructions(
        k["bmap"][0:1, lag, bass.ds(4 * g, 4)], engines=[eng.engine], min_val=0, max_val=NB - 1,
        skip_runtime_bounds_check_because="an entry counts which of the first NB - 1 blocks end before the unit")
    return blocks


def bank(ctx, nc, name):
    return ctx.enter_context(nc.psum_tensor(unique(name), [P, 512], F32))


def link(p, eng, s, ins, count):
    ins.then_inc(s.sem, 1)
    count[0] += 1
    eng.wait_ge(s.sem, s.at(count[0]))


def stage_constants(p, k, s, blank):
    nc, d = p.nc, p.d
    s_ld, s_c, s_z = p.sig("load"), p.sig("const"), p.sig("zero")
    s_init, s_e = p.sig("init"), p.sig("edges")
    with nc.Block() as block:
        @block.vector
        def _(dve):
            dve.memset(k["x"][:], 0.0).then_inc(s_z.sem, 1)
            dve.memset(k["ones"][:], 1.0)
            dve.memset(blank[:], 0.0).then_inc(s_z.sem, 1)
            dve.wait_ge(s_z.sem, s_z.at(2))
            dve.memset(blank[:, :, F_DST:F_DST + 1], -1.0).then_inc(s_z.sem, 1)

        @block.sync
        def _(sp):
            for name, what in (("dst_i", "dst"), ("src_i", "src"), ("typ_i", "edge_type_8")):
                sp.dma_start(s[name][:], d[what].rearrange("(p j) -> p j", p=SORT_P)).then_inc(s_e.sem, 16)
            sp.dma_start(s["weight"][:], d["edge_weight1"].rearrange("(p j) a -> p (j a)", p=SORT_P)).then_inc(s_e.sem, 16)
            sp.wait_ge(s_z.sem, s_z.at(1))
            xv = d["x"][0:(NB - 1) * P, :].rearrange("(b p) f -> p b f", p=P)
            sp.dma_start(k["x"][:, 0:NB - 1, :], xv).then_inc(s_ld.sem, 16)
            sp.dma_start(k["x"][0:LAST_ROWS, NB - 1, :], d["x"][(NB - 1) * P:N_NODES, :]).then_inc(s_ld.sem, 16)
            sp.wait_ge(s_z.sem, s_z.at(3))
            rv = d["records"].rearrange("(p c r) f -> c p (r f)", p=P, c=INIT)
            for c in range(INIT):
                sp.dma_start(rv[c], blank[:].rearrange("p r f -> p (r f)")).then_inc(s_init.sem, 16)
            sp.wait_ge(s_ld.sem, s_ld.at(32))

        @block.gpsimd
        def _(pool):
            pool.memset(k["ident"][:], 0.0).then_inc(s_c.sem, 1)
            pool.memset(k["tri"][:], 1.0).then_inc(s_c.sem, 1)
            pool.wait_ge(s_c.sem, s_c.at(2))
            pool.affine_select(out=k["ident"][:], in_=k["ident"][:], compare_op=ALU.not_equal, fill=1.0,
                               base=0, pattern=[[-1, P]], channel_multiplier=1)
            pool.affine_select(out=k["tri"][:], in_=k["tri"][:], compare_op=ALU.is_gt, fill=0.0,
                               base=0, pattern=[[1, P]], channel_multiplier=-1)
            pool.iota(k["iota_i"][:], pattern=[[1, UNITS]], base=0, channel_multiplier=0).then_inc(s_c.sem, 1)
            pool.wait_ge(s_c.sem, s_c.at(3))
            pool.tensor_copy(k["iota"][:], k["iota_i"][:])
            pool.tensor_copy(k["ident16"][:], k["ident"][:])
            pool.tensor_copy(k["iota16"][:], k["iota_i"][:, 0:P])
    s_ld.close(32), s_c.close(3), s_z.close(3)


def stage_counts(p, k, s):
    nc, d = p.nc, p.d
    s_e, s_dve, s_pe, s_cnt = p.sig("edges"), p.sig("dve_chain"), p.sig("pe_out"), p.sig("counts")
    n = [0]
    with ExitStack() as ctx:
        tmp_i = i32(ctx, nc, "tmp_i", [SORT_P, 2, SORT_J])
        eq = f32(ctx, nc, "eq", [SORT_P, 2, SORT_J])
        typf = f32(ctx, nc, "typf", [SORT_P, SORT_J])
        cnt = f32(ctx, nc, "cnt", [SORT_P, NB])
        tot_i = i32(ctx, nc, "tot_i", [P, NB])
        totf = f32(ctx, nc, "totf", [P, NB])
        unitf = f32(ctx, nc, "unitf", [P, NB])
        pads = f32(ctx, nc, "pads", [P, NB])
        ps = bank(ctx, nc, "ps")
        dst_i, src_i, typ_i, weight = (s[name] for name in ("dst_i", "src_i", "typ_i", "weight"))
        key, meta, run, uend = s["key"], s["meta"], s["run"], s["uend"]
        with nc.Block() as block:
            @block.tensor
            def _(pe):
                pe.wait_ge(s_cnt.sem, s_cnt.at(NB))
                pe.matmul(ps[0:SORT_P, 0:NB], k["tri"][0:SORT_P, 0:SORT_P], cnt[:], start=True, stop=True)
                pe.matmul(ps[:, 32:32 + NB], k["ones"][0:SORT_P, 0:P], cnt[:], start=True, stop=True).then_inc(s_pe.sem, 1)

            @block.vector
            def _(dve):
                def chain(ins):
                    link(p, dve, s_dve, ins, n)
                dve.wait_ge(s_e.sem, s_e.at(64))
                chain(dve.tensor_scalar(tmp_i[:, 0], dst_i[:], 7, None, ALU.arith_shift_right))
                chain(dve.tensor_copy(key[:], tmp_i[:, 0]))
                for b in range(NB):
                    if b >= 2:
                        dve.wait_ge(s_cnt.sem, s_cnt.at(b - 1))
                    dve.tensor_scalar(eq[:, b % 2], key[:], float(b), None, ALU.is_equal, ALU.add,
                                      accum_out=cnt[:, b:b + 1]).then_inc(s_cnt.sem, 1)
                dve.tensor_copy(meta[:, :, 0], weight[:])
                dve.tensor_copy(meta[:, :, 2], src_i[:])
                dve.tensor_scalar(tmp_i[:, 1], dst_i[:], P - 1, None, ALU.bitwise_and)
                chain(dve.tensor_copy(typf[:], typ_i[:]))
                dve.tensor_copy(meta[:, :, 1], tmp_i[:, 1])
                chain(dve.scalar_tensor_tensor(out=meta[:, :, 3], in0=meta[:, :, 2], scalar=float(N_REL),
                                               in1=typf[:], op0=ALU.mult, op1=ALU.add))
                dve.wait_ge(s_pe.sem, s_pe.at(1))
                chain(dve.tensor_scalar(totf[:], ps[:, 32:32 + NB], float(UNIT - 1), None, ALU.add))
                chain(dve.tensor_copy(tot_i[:], totf[:]))
                chain(dve.tensor_scalar(tot_i[:], tot_i[:], 8, None, ALU.arith_shift_right))
                chain(dve.tensor_copy(unitf[:], tot_i[:]))
                chain(dve.tensor_tensor_scan(uend[:], k["ones"][:, 0:NB], unitf[:], 0.0, ALU.mult, ALU.add))
                chain(dve.tensor_tensor(pads[:], uend[:], unitf[:], ALU.subtract))
                chain(dve.scalar_tensor_tensor(out=run[:], in0=pads[0:SORT_P, :], scalar=float(UNIT),
                                               in1=ps[0:SORT_P, 0:NB], op0=ALU.mult, op1=ALU.add))
                chain(dve.tensor_scalar(run[:], run[:], -1.0, None, ALU.add))
        s_e.close(64), s_dve.close(n[0]), s_pe.close(1), s_cnt.close(NB)


SJ = 16
STEPS = SORT_J // SJ


def stage_scatter(p, k, s, ht):
    nc, d = p.nc, p.d
    s_init, s_attr = p.sig("init"), [p.sig("attr0"), p.sig("attr1")]
    s_rec, s_sc, s_c = p.sig("rec"), [p.sig("scat0"), p.sig("scat1")], p.sig("dve_chain")
    s_z, s_ld, s_pe = p.sig("zero"), p.sig("load"), p.sig("pe_out")
    s_a, s_st = p.sig("ev_act"), [p.sig("store0"), p.sig("store1")]
    s_map, s_norm, s_var, s_std, s_h = p.sig("map_chain"), p.sig("norm_chain"), p.sig("var"), p.sig("std"), p.sig("features")
    s_tp, s_ht = p.sig("turn"), p.sig("turned")
    tv = d["t_rel"].rearrange("(b p r) f -> b p (r f)", p=P, r=N_REL)
    W = SJ * N_ATTR
    LINKS = 15
    rounds = -(-NB // 4)
    nm, nn = [0], [0]
    with ExitStack() as ctx:
        attr = f32(ctx, nc, "attr", [SORT_P, 2, SJ, N_ATTR])
        rest = f32(ctx, nc, "rest", [SORT_P, 2, SJ, N_ATTR])
        rec = f32(ctx, nc, "rec", [SORT_P, 2, SJ, REC])
        idx = i32(ctx, nc, "idx", [SORT_P, 2, SJ])
        eq = f32(ctx, nc, "eq", [SORT_P, NB, SJ])
        rank = f32(ctx, nc, "rank", [SORT_P, NB, SJ])
        more = f32(ctx, nc, "more", [SORT_P, NB, SJ])
        posf = f32(ctx, nc, "posf", [SORT_P, SJ])
        pos = i32(ctx, nc, "pos", [SORT_P, SJ])
        slot = i32(ctx, nc, "slot", [SORT_P, SJ])
        tile = i32(ctx, nc, "tile", [SORT_P, SJ])
        bmf = f32(ctx, nc, "bmf", [1, UNITS])
        tmp = f32(ctx, nc, "ntmp", [P, NB, D])
        stat = f32(ctx, nc, "nstat", [P, 2, NB])
        w = f32(ctx, nc, "w0", [P, N_REL, D])
        row = f32(ctx, nc, "row0", [P, 2, N_REL * D])
        ps = [bank(ctx, nc, f"ph{q}") for q in range(4)]
        pt = [bank(ctx, nc, f"pt{q}") for q in range(2)]
        av = d["edge_attr_26"].rearrange("(p j) f -> p (j f)", p=SORT_P)
        with nc.Block() as block:
            @block.sync
            def _(sp):
                def load(i, q):
                    sp.dma_start(attr[:, q].rearrange("p j f -> p (j f)"), av[:, bass.ds((2 * i + q) * W, W)]).then_inc(s_attr[q].sem, 16)
                for q in range(2):
                    load(0, q)
                sp.dma_start(w[:], d["L0_gnn_weight"].rearrange("r i o -> i r o")).then_inc(s_ld.sem, 16)
                with sp.Fori(1, STEPS // 2) as i:
                    for q in range(2):
                        sp.wait_ge(s_rec.sem, s_rec.at(2 * i + q - 1))
                        p.apart(sp)
                        load(i, q)

            @block.vector
            def _(dve):
                dve.memset(rec[:], 0.0).then_inc(s_z.sem, 1)
                dve.memset(more[:], 1.0).then_inc(s_z.sem, 1)
                dve.wait_ge(s_z.sem, s_z.at(2))
                dve.memset(more[:, :, 0:1], 0.0).then_inc(s_z.sem, 1)
                dve.wait_ge(s_z.sem, s_z.at(3))

                def body(i, first):
                    for q in range(2):
                        j0, n = (2 * i + q) * SJ, LINKS * (2 * i + q)
                        parts = rec[:, q].bitcast(BF16)
                        hi, mid, lo = (parts[:, :, c * N_ATTR:(c + 1) * N_ATTR] for c in range(PARTS))
                        dve.tensor_tensor(eq[:], s["key"][:, bass.ds(j0, SJ)].unsqueeze(1).to_broadcast([SORT_P, NB, SJ]),
                                          k["iota"][0:SORT_P, 0:NB].unsqueeze(2).to_broadcast([SORT_P, NB, SJ]),
                                          ALU.is_equal).then_inc(s_c.sem, 1)
                        dve.wait_ge(s_c.sem, s_c.at(n + 1))
                        dve.tensor_tensor_scan(rank[:].rearrange("p b j -> p (b j)"), more[:].rearrange("p b j -> p (b j)"),
                                               eq[:].rearrange("p b j -> p (b j)"), 0.0, ALU.mult, ALU.add).then_inc(s_c.sem, 1)
                        dve.wait_ge(s_c.sem, s_c.at(n + 2))
                        dve.tensor_tensor(rank[:], rank[:], s["run"][:].unsqueeze(2).to_broadcast([SORT_P, NB, SJ]),
                                          ALU.add).then_inc(s_c.sem, 1)
                        dve.wait_ge(s_c.sem, s_c.at(n + 3))
                        dve.tensor_copy(s["run"][:], rank[:, :, SJ - 1])
                        dve.tensor_tensor(eq[:], eq[:], rank[:], ALU.mult).then_inc(s_c.sem, 1)
                        dve.wait_ge(s_c.sem, s_c.at(n + 4))
                        dve.tensor_reduce(posf[:], eq[:].rearrange("p b j -> p j b"), AX.X, ALU.add).then_inc(s_c.sem, 1)
                        dve.wait_ge(s_c.sem, s_c.at(n + 5))
                        dve.tensor_copy(pos[:], posf[:]).then_inc(s_c.sem, 1)
                        dve.wait_ge(s_c.sem, s_c.at(n + 6))
                        dve.tensor_scalar(slot[:], pos[:], P - 1, None, ALU.bitwise_and).then_inc(s_c.sem, 1)
                        dve.tensor_scalar(tile[:], pos[:], 7, GT - 1, ALU.arith_shift_right, ALU.bitwise_and)
                        dve.wait_ge(s_c.sem, s_c.at(n + 7))
                        dve.tensor_scalar(slot[:], slot[:], 3, None, ALU.logical_shift_left).then_inc(s_c.sem, 1)
                        dve.tensor_scalar(pos[:], pos[:], 10, None, ALU.arith_shift_right).then_inc(s_c.sem, 1)
                        dve.wait_ge(s_c.sem, s_c.at(n + 9))
                        dve.tensor_tensor(slot[:], slot[:], tile[:], ALU.bitwise_or).then_inc(s_c.sem, 1)
                        dve.tensor_scalar(pos[:], pos[:], 10, None, ALU.logical_shift_left).then_inc(s_c.sem, 1)
                        dve.wait_ge(s_c.sem, s_c.at(n + 11))
                        if not first:
                            dve.wait_ge(s_sc[q].sem, s_sc[q].at(16 * SJ * i))
                        dve.tensor_tensor(idx[:, q, :], pos[:], slot[:], ALU.bitwise_or).then_inc(s_c.sem, 1)
                        dve.wait_ge(s_attr[q].sem, s_attr[q].at(16 * (i + 1)))
                        dve.tensor_copy(hi, attr[:, q]).then_inc(s_c.sem, 1)
                        dve.tensor_scalar(rec[:, q, :, F_NORM:F_NORM + 4], s["meta"][:, bass.ds(j0, SJ), :], 0.0, None, ALU.add)
                        dve.wait_ge(s_c.sem, s_c.at(n + 13))
                        dve.tensor_tensor(rest[:, q], attr[:, q], hi, ALU.subtract).then_inc(s_c.sem, 1)
                        dve.wait_ge(s_c.sem, s_c.at(n + 14))
                        dve.tensor_copy(mid, rest[:, q]).then_inc(s_c.sem, 1)
                        dve.wait_ge(s_c.sem, s_c.at(n + 15))
                        dve.tensor_tensor(lo, rest[:, q], mid, ALU.subtract).then_inc(s_rec.sem, 1)
                body(0, True)

                def map_chain(ins):
                    link(p, dve, s_map, ins, nm)
                map_chain(dve.memset(bmf[:], 0.0))
                for b in range(NB - 1):
                    map_chain(dve.scalar_tensor_tensor(out=bmf[:], in0=k["iota"][0:1, :], scalar=s["uend"][0:1, b:b + 1],
                                                       in1=bmf[:], op0=ALU.is_ge, op1=ALU.add))
                map_chain(dve.memset(k["bmap"][:], 0))
                for lag in range(LAGS):
                    dve.tensor_copy(k["bmap"][:, lag, lag:lag + UNITS], bmf[:])
                body(1, False)

                def norm_chain(ins):
                    link(p, dve, s_norm, ins, nn)
                norm_steps(dve, k["x"], k["h"], tmp, stat, norm_chain, s_var)
                dve.wait_ge(s_std.sem, s_std.at(1))
                norm_chain(dve.reciprocal(stat[:, 1, :], stat[:, 1, :]))
                norm_chain(dve.tensor_tensor(k["h"][:], k["h"][:], stat[:, 1, :].unsqueeze(2).to_broadcast([P, NB, D]), ALU.mult))
                dve.tensor_scalar(k["h"][:], k["h"][:], 0.0, None, ALU.max).then_inc(s_h.sem, 1)
                with dve.Fori(2, STEPS // 2) as i:
                    body(i, False)

            @block.gpsimd
            def _(pool):
                pool.wait_ge(s_init.sem, s_init.at(16 * INIT))
                with pool.Fori(0, STEPS // 2) as i:
                    for q in range(2):
                        pool.wait_ge(s_rec.sem, s_rec.at(2 * i + q + 1))
                        p.apart(pool)
                        for j in range(SJ):
                            pool.indirect_dma_start(
                                out=d["records"], out_offset=bass.IndirectOffsetOnAxis(ap=idx[:, q, j:j + 1], axis=0),
                                in_=rec[:, q, j, :], in_offset=None).then_inc(s_sc[q].sem, 16)
                for q in range(2):
                    pool.wait_ge(s_sc[q].sem, s_sc[q].at(16 * SJ * (STEPS // 2)))

            @block.tensor
            def _(pe):
                pe.wait_ge(s_h.sem, s_h.at(1))
                for r in range(rounds):
                    if r >= 2:
                        pe.wait_ge(s_ht.sem, s_ht.at(r - 1))
                    for b in range(4 * r, min(NB, 4 * r + 4)):
                        last = pe.transpose(pt[r % 2][:, (b % 4) * P:(b % 4 + 1) * P], k["h"][:, b, :], k["ident"][:])
                    last.then_inc(s_tp.sem, 1)
                pe.wait_ge(s_ld.sem, s_ld.at(16))
                pe.wait_ge(s_ht.sem, s_ht.at(rounds))
                for b in range(NB):
                    if b >= 2:
                        pe.wait_ge(s_a.sem, s_a.at(b - 1))
                    for h in range(2):
                        last = pe.matmul(ps[2 * (b % 2) + h][:], ht[:, b * P:(b + 1) * P],
                                         w[:, 4 * h:4 * h + 4, :].rearrange("p r f -> p (r f)"), start=True, stop=True)
                    last.then_inc(s_pe.sem, 1)

            @block.scalar
            def _(act):
                act.wait_ge(s_var.sem, s_var.at(1))
                act.activation(stat[:, 1, :], stat[:, 1, :], ACT.Sqrt).then_inc(s_std.sem, 1)
                for r in range(rounds):
                    n = (min(NB, 4 * r + 4) - 4 * r) * P
                    act.wait_ge(s_tp.sem, s_tp.at(r + 1))
                    act.copy(ht[:, 4 * r * P:4 * r * P + n], pt[r % 2][:, 0:n]).then_inc(s_ht.sem, 1)
                for b in range(NB):
                    act.wait_ge(s_pe.sem, s_pe.at(b + 1))
                    if b >= 2:
                        act.wait_ge(s_st[b % 2].sem, s_st[b % 2].at(16 * (b // 2)))
                    for h in range(2):
                        last = act.copy(row[:, b % 2, 512 * h:512 * h + 512], ps[2 * (b % 2) + h][:])
                    last.then_inc(s_a.sem, 1)
                    act.wait_ge(s_a.sem, s_a.at(b + 1))
                    act.dma_start(tv[b], row[:, b % 2, :]).then_inc(s_st[b % 2].sem, 16)
                for q in range(2):
                    act.wait_ge(s_st[q].sem, s_st[q].at(16 * ((NB + 1 - q) // 2)))
        s_z.close(3), s_init.close(16 * INIT), s_rec.close(STEPS), s_c.close(LINKS * STEPS)
        s_ld.close(16), s_pe.close(NB), s_a.close(NB), s_tp.close(rounds), s_ht.close(rounds)
        s_map.close(nm[0]), s_norm.close(nn[0])
        for one in (s_var, s_std, s_h):
            one.close(1)
        for q in range(2):
            s_attr[q].close(16 * (STEPS // 2)), s_sc[q].close(16 * SJ * (STEPS // 2))
            s_st[q].close(16 * ((NB + 1 - q) // 2))


def norm_steps(dve, x, out, tmp, stat, chain, s_var):
    chain(dve.tensor_reduce(stat[:, 0, :], x[:], AX.X, ALU.add))
    chain(dve.tensor_scalar(stat[:, 0, :], stat[:, 0, :], 1.0 / D, None, ALU.mult))
    mean = stat[:, 0, :].unsqueeze(2).to_broadcast([P, NB, D])
    chain(dve.tensor_tensor(out[:], x[:], mean, ALU.subtract))
    chain(dve.tensor_tensor(tmp[:], out[:], out[:], ALU.mult))
    chain(dve.tensor_reduce(stat[:, 1, :], tmp[:], AX.X, ALU.add))
    dve.tensor_scalar(stat[:, 1, :], stat[:, 1, :], 1.0 / D, EPS, ALU.mult, ALU.add).then_inc(s_var.sem, 1)


def stage_norm(p, x, out, relu=True, gamma=None, beta=None):
    nc = p.nc
    s_dve, s_var, s_std = p.sig("dve_chain"), p.sig("var"), p.sig("std")
    n = [0]
    with ExitStack() as ctx:
        tmp = f32(ctx, nc, "ntmp", [P, NB, D])
        stat = f32(ctx, nc, "nstat", [P, 2, NB])
        with nc.Block() as block:
            @block.vector
            def _(dve):
                def chain(ins):
                    link(p, dve, s_dve, ins, n)
                norm_steps(dve, x, out, tmp, stat, chain, s_var)
                dve.wait_ge(s_std.sem, s_std.at(1))
                chain(dve.reciprocal(stat[:, 1, :], stat[:, 1, :]))
                rstd = stat[:, 1, :].unsqueeze(2).to_broadcast([P, NB, D])
                chain(dve.tensor_tensor(out[:], out[:], rstd, ALU.mult))
                if relu:
                    chain(dve.tensor_scalar(out[:], out[:], 0.0, None, ALU.max))
                if gamma is not None:
                    chain(dve.tensor_tensor(out[:], out[:], gamma.unsqueeze(1).to_broadcast([P, NB, D]), ALU.mult))
                    chain(dve.tensor_tensor(out[:], out[:], beta.unsqueeze(1).to_broadcast([P, NB, D]), ALU.add))

            @block.scalar
            def _(act):
                act.wait_ge(s_var.sem, s_var.at(1))
                act.activation(stat[:, 1, :], stat[:, 1, :], ACT.Sqrt).then_inc(s_std.sem, 1)
        s_dve.close(n[0]), s_var.close(1), s_std.close(1)


def stage_turn(p, k, h, ht):
    nc = p.nc
    s_pe, s_ev = p.sig("pe_out"), p.sig("turned")
    rounds = -(-NB // 4)
    with ExitStack() as ctx:
        ps = [bank(ctx, nc, f"pt{q}") for q in range(2)]
        with nc.Block() as block:
            @block.tensor
            def _(pe):
                for r in range(rounds):
                    if r >= 2:
                        pe.wait_ge(s_ev.sem, s_ev.at(r - 1))
                    for b in range(4 * r, min(NB, 4 * r + 4)):
                        last = pe.transpose(ps[r % 2][:, (b % 4) * P:(b % 4 + 1) * P], h[:, b, :], k["ident"][:])
                    last.then_inc(s_pe.sem, 1)

            @block.scalar
            def _(act):
                for r in range(rounds):
                    w = (min(NB, 4 * r + 4) - 4 * r) * P
                    act.wait_ge(s_pe.sem, s_pe.at(r + 1))
                    act.copy(ht[:, 4 * r * P:4 * r * P + w], ps[r % 2][:, 0:w]).then_inc(s_ev.sem, 1)
        s_pe.close(rounds), s_ev.close(rounds)


def stage_project(p, k, ht, loads, products, width, out):
    nc = p.nc
    s_ld, s_pe, s_ev = p.sig("load"), p.sig("pe_out"), p.sig("ev_act")
    with ExitStack() as ctx:
        ps = [bank(ctx, nc, f"pj{q}") for q in range(2)]
        with nc.Block() as block:
            @block.sync
            def _(sp):
                for dst, src in loads:
                    sp.dma_start(dst, src).then_inc(s_ld.sem, 16)

            @block.tensor
            def _(pe):
                if loads:
                    pe.wait_ge(s_ld.sem, s_ld.at(16 * len(loads)))
                for b in range(NB):
                    if b >= 2:
                        pe.wait_ge(s_ev.sem, s_ev.at(b - 1))
                    for m, (c0, c1, lhs, rhs) in enumerate(products):
                        last = pe.matmul(ps[b % 2][:, c0:c1], lhs(b), rhs, start=m == 0, stop=m == len(products) - 1)
                    last.then_inc(s_pe.sem, 1)

            @block.scalar
            def _(act):
                for b in range(NB):
                    act.wait_ge(s_pe.sem, s_pe.at(b + 1))
                    act.copy(out[:, b, 0:width], ps[b % 2][:, 0:width]).then_inc(s_ev.sem, 1)
        s_ld.close(16 * len(loads)), s_pe.close(NB), s_ev.close(NB)


def stage_edge_parts(p, k, r, ht, w1, b1, wf, wp, pds):
    nc, d = p.nc, p.d
    s_ld, s_pe, s_z = p.sig("load"), p.sig("pe_out"), p.sig("zero")
    s_a, s_hi, s_r, s_mid, s_lo = p.sig("ev_act"), p.sig("turn"), p.sig("turned"), p.sig("oht"), p.sig("ev_dve")
    s_st, s_c, s_wc, s_wp = [p.sig("store0"), p.sig("store1")], p.sig("dve_chain"), p.sig("weight_parts"), p.sig("packed")
    w1d = d["L1_gnn_mlp_w1"][r]
    loads = 2 + PARTS
    n = [0]
    with ExitStack() as ctx:
        row = f32(ctx, nc, "prow", [P, 2, MH])
        rest = f32(ctx, nc, "prest", [P, 2, MH])
        wrest = f32(ctx, nc, "wrest", [AR, MH])
        wc = bf16(ctx, nc, "wc", [AR, PARTS, MH])
        ps = [bank(ctx, nc, f"ps{q}") for q in range(2)]
        pd = [bank(ctx, nc, f"pd{q}") for q in range(2)]
        tv = d["t_mlp"].rearrange("(b p) f -> b p f", p=P)
        with nc.Block() as block:
            @block.sync
            def _(sp):
                sp.dma_start(w1[:], w1d[0:2 * D, :].rearrange("(a i) o -> i a o", a=2)).then_inc(s_ld.sem, 16)
                sp.dma_start(b1[:], d["L1_gnn_mlp_b1"][r:r + 1, :]).then_inc(s_ld.sem, 16)
                sp.wait_ge(s_z.sem, s_z.at(1))
                for c in range(PARTS):
                    sp.dma_start(wf[c * N_ATTR:(c + 1) * N_ATTR, :], w1d[2 * D:2 * D + N_ATTR, :]).then_inc(s_ld.sem, 16)
                for b in range(NB):
                    sp.wait_ge(s_a.sem, s_a.at(b + 1))
                    sp.dma_start(tv[b], row[:, b % 2, :]).then_inc(s_st[b % 2].sem, 16)
                sp.wait_ge(s_wc.sem, s_wc.at(1))
                for j, pieces in enumerate(PIECES):
                    for at, first, rows, c in pieces:
                        sp.dma_start(wp[at:at + rows, j, :], wc[first:first + rows, c, :]).then_inc(s_wp.sem, 16)
                sp.wait_ge(s_wp.sem, s_wp.at(64))
                for q in range(2):
                    sp.wait_ge(s_st[q].sem, s_st[q].at(16 * ((NB + 1 - q) // 2)))

            @block.tensor
            def _(pe):
                pe.wait_ge(s_ld.sem, s_ld.at(16 * loads))
                for b in range(NB):
                    hb = ht[:, b * P:(b + 1) * P]
                    if b >= 2:
                        pe.wait_ge(s_a.sem, s_a.at(b - 1))
                    pe.matmul(ps[b % 2][:, 0:MH], hb, w1[:, 1, :], start=True, stop=True)
                    if b >= 2:
                        pe.wait_ge(s_r.sem, s_r.at(b - 1))
                    pe.matmul(pd[b % 2][:, 0:MH], hb, w1[:, 0, :], start=True, stop=False)
                    pe.matmul(pd[b % 2][:, 0:MH], k["ones"][0:1, 0:P], b1[:], start=False, stop=True).then_inc(s_pe.sem, 1)

            @block.scalar
            def _(act):
                def middle(b):
                    act.wait_ge(s_r.sem, s_r.at(b + 1))
                    act.copy(pds[:, b, 1, :], rest[:, b % 2, :]).then_inc(s_mid.sem, 1)
                for b in range(NB):
                    act.wait_ge(s_pe.sem, s_pe.at(b + 1))
                    act.copy(pds[:, b, 0, :], pd[b % 2][:, 0:MH]).then_inc(s_hi.sem, 1)
                    if b >= 2:
                        act.wait_ge(s_st[b % 2].sem, s_st[b % 2].at(16 * (b // 2)))
                    act.copy(row[:, b % 2, :], ps[b % 2][:, 0:MH]).then_inc(s_a.sem, 1)
                    if b >= 1:
                        middle(b - 1)
                middle(NB - 1)

            @block.vector
            def _(dve):
                def chain(ins):
                    link(p, dve, s_c, ins, n)
                dve.memset(wf[:], 0.0).then_inc(s_z.sem, 1)
                dve.wait_ge(s_ld.sem, s_ld.at(16 * loads))
                chain(dve.tensor_copy(wc[:, 0, :], wf[:]))
                chain(dve.tensor_tensor(wrest[:], wf[:], wc[:, 0, :], ALU.subtract))
                chain(dve.tensor_copy(wc[:, 1, :], wrest[:]))
                dve.tensor_tensor(wc[:, 2, :], wrest[:], wc[:, 1, :], ALU.subtract).then_inc(s_wc.sem, 1)

                def low(b):
                    dve.wait_ge(s_mid.sem, s_mid.at(b + 1))
                    dve.tensor_tensor(pds[:, b, 2, :], rest[:, b % 2, :], pds[:, b, 1, :], ALU.subtract).then_inc(s_lo.sem, 1)
                for b in range(NB):
                    dve.wait_ge(s_hi.sem, s_hi.at(b + 1))
                    if b >= 2:
                        dve.wait_ge(s_lo.sem, s_lo.at(b - 1))
                    dve.tensor_tensor(rest[:, b % 2, :], pd[b % 2][:, 0:MH], pds[:, b, 0, :], ALU.subtract).then_inc(s_r.sem, 1)
                    if b >= 1:
                        low(b - 1)
                low(NB - 1)
        s_ld.close(16 * loads), s_z.close(1), s_c.close(n[0]), s_wc.close(1), s_wp.close(64)
        for s in (s_pe, s_a, s_hi, s_r, s_mid, s_lo):
            s.close(NB)
        for q in range(2):
            s_st[q].close(16 * ((NB + 1 - q) // 2))


def stage_store_rows(p, out_dram, rows):
    nc = p.nc
    s_st = p.sig("store0")
    with nc.Block() as block:
        @block.sync
        def _(sp):
            sp.dma_start(out_dram.rearrange("(b p) f -> p b f", p=P), rows).then_inc(s_st.sem, 16)
            sp.wait_ge(s_st.sem, s_st.at(16))
    s_st.close(16)


def over_bodies(eng, body):
    body(0, True, False)
    with eng.Fori(1, BODIES - 1) as i:
        body(i, False, False)
    body(BODIES - 1, False, True)


class Gather:

    def __init__(self, p, ctx, table, index, width):
        self.p, self.table, self.index, self.width = p, table, index, width
        self.rows = f32(ctx, p.nc, "rows", [P, 2, GT, width])
        self.idx = i32(ctx, p.nc, "gidx", [P, 2, GT])
        self.s_idx = p.sig("idx")
        self.s_row = [p.sig(f"row{u}") for u in range(BU)]

    def feed(self, act, g, q):
        act.copy(self.idx[:, q, :], self.index[:, bass.ds(g * GT, GT)]).then_inc(self.s_idx.sem, 1)

    def program(self, pool):
        p = self.p
        with pool.Fori(0, BODIES) as i:
            for q in range(2):
                pool.wait_ge(self.s_idx.sem, self.s_idx.at(2 * i + q + 1))
                p.apart(pool)
                for t in range(GT):
                    pool.indirect_dma_start(
                        out=self.rows[:, q, t, :], out_offset=None, in_=self.table,
                        in_offset=bass.IndirectOffsetOnAxis(ap=self.idx[:, q, t:t + 1], axis=0),
                    ).then_inc(self.s_row[GU * q + t // 2].sem, 16)

    def close(self):
        self.s_idx.close(GROUPS)
        for s in self.s_row:
            s.close(32 * BODIES)


def onehot(p, dve, k, oh, g, q):
    dst = k["meta"][:, bass.ds(g * GT, GT)].unsqueeze(2).to_broadcast([P, GT, P])
    nodes = k["iota"][:, 0:P].unsqueeze(1).to_broadcast([P, GT, P])
    return dve.tensor_tensor(oh[:, q], nodes, dst, ALU.is_equal)


def onehot16(dve, k, oh, g, q, op=ALU.is_equal):
    dst = k["meta16"][:, bass.ds(g * GT, GT)].unsqueeze(2).to_broadcast([P, GT, P])
    nodes = k["iota16"][:].unsqueeze(1).to_broadcast([P, GT, P])
    return dve.tensor_tensor(oh[:, q], nodes, dst, op)


def stage_relation_sum(p, k, acc):
    nc, d = p.nc, p.d
    s_oh, s_agg, s_acc = p.sig("onehot"), p.sig("agg"), p.sig("acc")
    s_z, s_turn, s_cp, s_ra = p.sig("zero"), p.sig("turn"), p.sig("oht"), p.sig("relu")
    s_rl, s_st = [p.sig("attr0"), p.sig("attr1")], [p.sig("store0"), p.sig("store1")]
    with ExitStack() as ctx:
        ga = Gather(p, ctx, d["t_rel"], None, D)
        buf = f32(ctx, nc, "rbuf", [P, 2, GT, REC])
        out = bf16(ctx, nc, "rout", [AR, 2, GT * P])
        oh = f32(ctx, nc, "oh", [P, 2, GT, P])
        wr = f32(ctx, nc, "wr", [P, 2, GT, D])
        ps = [bank(ctx, nc, f"pa{q}") for q in range(2)]
        tp = [ctx.enter_context(nc.psum_tensor(unique("pr"), [P, GT * P], BF16)) for q in range(2)]
        rv = d["records"].rearrange("(g p i) f -> p g (i f)", p=P, i=GT)
        with nc.Block() as block:
            @block.gpsimd
            def _(pool):
                ga.program(pool)

            @block.sync
            def _(sp):
                def load(g, q):
                    sp.dma_start(buf[:, q].rearrange("p i f -> p (i f)"),
                                 rv[:, bass.ds(g, 1), :].rearrange("p g f -> p (g f)")).then_inc(s_rl[q].sem, 16)

                def store(g, q):
                    sp.wait_ge(s_cp.sem, s_cp.at(g + 1))
                    p.apart(sp)
                    sp.dma_start(d["attr_t"][:, bass.ds(g * GT * P, GT * P)], out[:, q, :]).then_inc(s_st[q].sem, 16)
                for q in range(2):
                    load(q, q)
                with sp.Fori(0, BODIES - 1) as i:
                    for q in range(2):
                        g = 2 * i + q
                        store(g, q)
                        sp.wait_ge(s_ra.sem, s_ra.at(4 * g + 4))
                        p.apart(sp)
                        sp.wait_ge(s_oh.sem, s_oh.at(g + 1))
                        p.apart(sp)
                        load(g + 2, q)
                for q in range(2):
                    store(GROUPS - 2 + q, q)
                for q in range(2):
                    sp.wait_ge(s_st[q].sem, s_st[q].at(16 * BODIES))

            @block.scalar
            def _(act):
                def body(i, first, last):
                    for q in range(2):
                        g = 2 * i + q
                        act.wait_ge(s_turn.sem, s_turn.at(g + 1))
                        if not first:
                            p.apart(act)
                            act.wait_ge(s_st[q].sem, s_st[q].at(16 * i))
                        act.copy(out[:, q, :], tp[q][0:AR, :]).then_inc(s_cp.sem, 1)
                        if not first:
                            act.wait_ge(s_agg.sem, s_agg.at(4 * g - 4))
                        for t in range(GT):
                            if t % 2 == 0:
                                row = ga.s_row[GU * q + t // 2]
                                act.wait_ge(row.sem, row.at(32 * (i + 1)))
                            ins = act.activation(wr[:, q, t, :], ga.rows[:, q, t, :], ACT.Copy, scale=buf[:, q, t, F_NORM:F_NORM + 1])
                            if t % 2 == 1:
                                ins.then_inc(s_ra.sem, 1)
                over_bodies(act, body)

            @block.tensor
            def _(pe):
                def body(i, first, last):
                    for q in range(2):
                        g = 2 * i + q
                        pe.wait_ge(s_rl[q].sem, s_rl[q].at(16 * (i + 1)))
                        if not first:
                            pe.wait_ge(s_cp.sem, s_cp.at(g - 1))
                        for t in range(GT):
                            mm = pe.transpose(tp[q][0:AR, t * P:(t + 1) * P], buf[:, q, t, 0:AR // 2].bitcast(BF16), k["ident16"][:])
                        mm.then_inc(s_turn.sem, 1)
                        for v in range(GU):
                            u = 4 * g + v
                            if v == 0:
                                pe.wait_ge(s_oh.sem, s_oh.at(g + 1))
                            pe.wait_ge(s_ra.sem, s_ra.at(u + 1))
                            if not (first and q == 0 and v < 2):
                                pe.wait_ge(s_acc.sem, s_acc.at(u - 1))
                            o = ps[v % 2][:, 0:D]
                            for t in range(2):
                                mm = pe.matmul(o, oh[:, q, 2 * v + t, :], wr[:, q, 2 * v + t, :], start=t == 0, stop=t == 1)
                            mm.then_inc(s_agg.sem, 1)
                over_bodies(pe, body)

            @block.vector
            def _(dve):
                dve.memset(acc[:], 0.0).then_inc(s_z.sem, 1)

                def prepare(i, g, q, first):
                    dve.wait_ge(s_rl[q].sem, s_rl[q].at(16 * (i + 1)))
                    if not first:
                        dve.wait_ge(s_ra.sem, s_ra.at(4 * g - 4))
                    dve.tensor_scalar(ga.idx[:, q, :], buf[:, q, :, F_HW], 0.0, None, ALU.add).then_inc(ga.s_idx.sem, 1)
                    dve.tensor_scalar(k["meta"][:, bass.ds(g * GT, GT)], buf[:, q, :, F_DST], 0.0, None, ALU.add)
                    dve.tensor_scalar(k["meta16"][:, bass.ds(g * GT, GT)], buf[:, q, :, F_DST], 0.0, None, ALU.add)
                    dve.tensor_scalar(k["src"][:, bass.ds(g * GT, GT)], buf[:, q, :, F_SRC], 0.0, None, ALU.add)
                    if not first:
                        dve.wait_ge(s_agg.sem, s_agg.at(4 * g - 4))
                    dve.tensor_tensor(oh[:, q], k["iota"][:, 0:P].unsqueeze(1).to_broadcast([P, GT, P]),
                                      buf[:, q, :, F_DST:F_DST + 1].to_broadcast([P, GT, P]), ALU.is_equal).then_inc(s_oh.sem, 1)
                prepare(0, 0, 0, True)
                dve.wait_ge(s_z.sem, s_z.at(1))

                def body(i, first, last):
                    for q in range(2):
                        g = 2 * i + q
                        blocks = unit_blocks(nc, dve, k, g)
                        for v in range(GU):
                            u = 4 * g + v
                            dve.wait_ge(s_agg.sem, s_agg.at(u + 1))
                            if not (first and q == 0 and v == 0):
                                dve.wait_ge(s_acc.sem, s_acc.at(u))
                            a = acc[:, bass.ds(blocks[v], 1), :].rearrange("p a f -> p (a f)")
                            dve.tensor_tensor(a, a, ps[v % 2][:, 0:D], ALU.add).then_inc(s_acc.sem, 1)
                            if v == 0 and not (last and q == 1):
                                prepare(i + q, g + 1, 1 - q, first and q == 0)
                over_bodies(dve, body)
        ga.close()
        s_z.close(1), s_acc.close(UNITS), s_agg.close(UNITS), s_ra.close(UNITS)
        for s in (s_oh, s_turn, s_cp):
            s.close(GROUPS)
        for q in range(2):
            s_rl[q].close(16 * BODIES), s_st[q].close(16 * BODIES)


def stage_relation_add(p, k, acc):
    nc, d = p.nc, p.d
    s_ld, s_dve = p.sig("load"), p.sig("dve_chain")
    n = [0]
    with ExitStack() as ctx:
        bias = f32(ctx, nc, "b0", [P, D])
        with nc.Block() as block:
            @block.sync
            def _(sp):
                sp.dma_start(bias[:], d["L0_gnn_bias"].partition_broadcast(P)).then_inc(s_ld.sem, 16)

            @block.vector
            def _(dve):
                def chain(ins):
                    link(p, dve, s_dve, ins, n)
                dve.wait_ge(s_ld.sem, s_ld.at(16))
                chain(dve.tensor_tensor(acc[:], acc[:], bias[:].unsqueeze(1).to_broadcast([P, NB, D]), ALU.add))
                chain(dve.scalar_tensor_tensor(out=k["x"][:], in0=acc[:], scalar=0.0, in1=k["x"][:],
                                               op0=ALU.max, op1=ALU.add))
        s_ld.close(16), s_dve.close(n[0])


def turn_onehots(pe, k, oh, tp, q, s_turn):
    for t in range(GT):
        mm = pe.transpose(tp[q][:, t * P:(t + 1) * P], oh[:, q, t, :], k["ident16"][:])
    mm.then_inc(s_turn.sem, 1)


def stage_edge_mlp(p, k, pdst, acc, wp):
    nc, d = p.nc, p.d
    s_oh, s_oh16, s_turn, s_oht = p.sig("onehot"), p.sig("onehot16"), p.sig("turn"), p.sig("oht")
    s_pre, s_add, s_relu = p.sig("pre"), p.sig("added"), p.sig("relu")
    s_agg, s_acc, s_z = p.sig("agg"), p.sig("acc"), p.sig("zero")
    s_at = [p.sig("attr0"), p.sig("attr1")]
    with ExitStack() as ctx:
        ga = Gather(p, ctx, d["t_mlp"], k["src"], MH)
        oh = f32(ctx, nc, "oh", [P, 2, GT, P])
        oh16 = bf16(ctx, nc, "oh16", [P, 2, GT, P])
        oht = bf16(ctx, nc, "oht", [P, 2, GT, P])
        at = bf16(ctx, nc, "at", [PACK, 2, 2, GT * P])
        hs = f32(ctx, nc, "hs", [P, 2, 2, MH])
        h1 = f32(ctx, nc, "h1", [P, 2, 2, MH + 1])
        tp = [ctx.enter_context(nc.psum_tensor(unique("tp"), [P, GT * P], BF16)) for q in range(2)]
        pp = [bank(ctx, nc, f"pp{q}") for q in range(2)]
        pa = [bank(ctx, nc, f"pa{q}") for q in range(2)]
        LAG = 2
        with nc.Block() as block:
            @block.gpsimd
            def _(pool):
                ga.program(pool)

            @block.sync
            def _(sp):
                def load(g, q):
                    for j, pieces in enumerate(PIECES):
                        for to, first, rows, _ in pieces:
                            sp.dma_start(at[to:to + rows, q, j, :],
                                         d["attr_t"][first:first + rows, bass.ds(g * GT * P, GT * P)]).then_inc(s_at[q].sem, 16)
                for q in range(2):
                    load(q, q)
                with sp.Fori(0, BODIES - 1) as i:
                    for q in range(2):
                        sp.wait_ge(s_pre.sem, s_pre.at(4 * (2 * i + q + 1)))
                        p.apart(sp)
                        load(2 * i + q + 2, q)

            @block.scalar
            def _(act):
                def turned(g, q, first):
                    if not first:
                        act.wait_ge(s_pre.sem, s_pre.at(4 * g - 4))
                        p.apart(act)
                    act.wait_ge(s_turn.sem, s_turn.at(g + 1))
                    act.copy(oht[:, q].rearrange("p t n -> p (t n)"), tp[q][:]).then_inc(s_oht.sem, 1)
                ga.feed(act, 0, 0)
                turned(0, 0, True)

                def body(i, first, last):
                    for q in range(2):
                        g = 2 * i + q
                        if not (last and q == 1):
                            if not (first and q == 0):
                                act.wait_ge(s_add.sem, s_add.at(4 * g))
                                p.apart(act)
                            ga.feed(act, g + 1, 1 - q)
                        for v in range(GU):
                            u = 4 * g + v
                            act.wait_ge(s_add.sem, s_add.at(u + 1))
                            p.apart(act)
                            if not (first and q == 0 and v < 2):
                                act.wait_ge(s_agg.sem, s_agg.at(u - 1))
                                p.apart(act)
                            act.activation(h1[:, v % 2, :, 0:MH], hs[:, v % 2], ACT.Relu).then_inc(s_relu.sem, 1)
                            if v == 1 and not (last and q == 1):
                                turned(g + 1, 1 - q, first and q == 0)
                over_bodies(act, body)

            @block.tensor
            def _(pe):
                def agg(u, w):
                    pe.wait_ge(s_relu.sem, s_relu.at(u + 1))
                    if not (isinstance(u, int) and u < 2):
                        pe.wait_ge(s_acc.sem, s_acc.at(u - 1))
                    for t in range(2):
                        mm = pe.matmul(pa[w % 2][:, 0:MH + 1], oh[:, w // GU, 2 * (w % GU) + t, :], h1[:, w % 2, t, :],
                                       start=t == 0, stop=t == 1)
                    mm.then_inc(s_agg.sem, 1)

                def turn(g, q, first):
                    pe.wait_ge(s_oh16.sem, s_oh16.at(g + 1))
                    if not first:
                        pe.wait_ge(s_oht.sem, s_oht.at(g - 1))
                    turn_onehots(pe, k, oh16, tp, q, s_turn)
                turn(0, 0, True)

                def body(i, first, last):
                    for q in range(2):
                        g = 2 * i + q
                        blocks = unit_blocks(nc, pe, k, g)
                        pe.wait_ge(s_at[q].sem, s_at[q].at(64 * (i + 1)))
                        for v in range(GU):
                            u, w = 4 * g + v, GU * q + v
                            if v == 0:
                                pe.wait_ge(s_oht.sem, s_oht.at(g + 1))
                            if v == LAG:
                                pe.wait_ge(s_oh.sem, s_oh.at(g + 1))
                            if not (first and w < 2):
                                pe.wait_ge(s_add.sem, s_add.at(u - 1))
                            for t in range(2):
                                o = pp[v % 2][:, t * MH:(t + 1) * MH]
                                j = 2 * v + t
                                for c in range(2):
                                    pe.matmul(o, at[:, q, c, j * P:(j + 1) * P], wp[:, c, :], start=c == 0, stop=False)
                                for c in range(PARTS):
                                    mm = pe.matmul(o, oht[:, q, j, :], pdst[:, bass.ds(blocks[v], 1), c, :].rearrange("p a f -> p (a f)"),
                                                   start=False, stop=c == PARTS - 1)
                            mm.then_inc(s_pre.sem, 1)
                            if not (first and w < LAG):
                                agg(u - LAG, (w - LAG) % BU)
                            if v == 1 and not (last and q == 1):
                                turn(g + 1, 1 - q, first and q == 0)
                over_bodies(pe, body)
                for u in range(UNITS - LAG, UNITS):
                    agg(u, u % BU)

            @block.vector
            def _(dve):
                dve.memset(acc[:], 0.0).then_inc(s_z.sem, 1)
                dve.memset(h1[:, :, :, MH:MH + 1], 1.0).then_inc(s_z.sem, 1)
                onehot16(dve, k, oh16, 0, 0).then_inc(s_oh16.sem, 1)
                onehot(p, dve, k, oh, 0, 0).then_inc(s_oh.sem, 1)
                dve.wait_ge(s_z.sem, s_z.at(2))

                def add(u, w, b):
                    dve.wait_ge(s_agg.sem, s_agg.at(u + 1))
                    if not (isinstance(u, int) and u == 0):
                        dve.wait_ge(s_acc.sem, s_acc.at(u))
                    a = acc[:, bass.ds(b, 1), 0:MH + 1].rearrange("p a f -> p (a f)")
                    dve.tensor_tensor(a, a, pa[w % 2][:, 0:MH + 1], ALU.add).then_inc(s_acc.sem, 1)

                def body(i, first, last):
                    for q in range(2):
                        g = 2 * i + q
                        blocks = unit_blocks(nc, dve, k, g, LAG)
                        for v in range(GU):
                            u, w = 4 * g + v, GU * q + v
                            dve.wait_ge(ga.s_row[w].sem, ga.s_row[w].at(32 * (i + 1)))
                            dve.wait_ge(s_pre.sem, s_pre.at(u + 1))
                            if not (first and w < 2):
                                dve.wait_ge(s_relu.sem, s_relu.at(u - 1))
                            dve.tensor_tensor(hs[:, v % 2].rearrange("p t f -> p (t f)"), pp[v % 2][:],
                                              ga.rows[:, q, 2 * v:2 * v + 2, :].rearrange("p t f -> p (t f)"),
                                              ALU.add).then_inc(s_add.sem, 1)
                            if not (first and w < LAG):
                                add(u - LAG, (w - LAG) % BU, blocks[v])
                            if v == 0 and not (last and q == 1):
                                if not (first and q == 0):
                                    dve.wait_ge(s_turn.sem, s_turn.at(g))
                                onehot16(dve, k, oh16, g + 1, 1 - q).then_inc(s_oh16.sem, 1)
                            if v == 2 and not (last and q == 1):
                                if not (first and q == 0):
                                    dve.wait_ge(s_agg.sem, s_agg.at(4 * g))
                                onehot(p, dve, k, oh, g + 1, 1 - q).then_inc(s_oh.sem, 1)
                over_bodies(dve, body)
                blocks = unit_blocks(nc, dve, k, GROUPS, LAG)
                for v in range(LAG):
                    u = UNITS - LAG + v
                    add(u, u % BU, blocks[v])
        ga.close()
        s_z.close(2), s_oh.close(GROUPS), s_oh16.close(GROUPS), s_turn.close(GROUPS), s_oht.close(GROUPS)
        for s in (s_pre, s_add, s_relu, s_agg, s_acc):
            s.close(UNITS)
        for q in range(2):
            s_at[q].close(64 * BODIES)


def stage_fold(p, loads, products, out):
    nc = p.nc
    s_ld, s_pe, s_ev = p.sig("load"), p.sig("pe_out"), p.sig("ev_act")
    with ExitStack() as ctx:
        ps = [bank(ctx, nc, f"pf{q}") for q in range(2)]
        with nc.Block() as block:
            @block.sync
            def _(sp):
                for dst, src in loads:
                    sp.dma_start(dst, src).then_inc(s_ld.sem, 16)

            @block.tensor
            def _(pe):
                pe.wait_ge(s_ld.sem, s_ld.at(16 * len(loads)))
                for j, (o, pairs) in enumerate(products):
                    if j >= 2:
                        pe.wait_ge(s_ev.sem, s_ev.at(j - 1))
                    for m, (lhs, rhs) in enumerate(pairs):
                        last = pe.matmul(ps[j % 2][0:o.shape[0], 0:o.shape[1]], lhs, rhs,
                                         start=m == 0, stop=m == len(pairs) - 1)
                    last.then_inc(s_pe.sem, 1)

            @block.scalar
            def _(act):
                for j, (o, pairs) in enumerate(products):
                    act.wait_ge(s_pe.sem, s_pe.at(j + 1))
                    act.copy(o, ps[j % 2][0:o.shape[0], 0:o.shape[1]]).then_inc(s_ev.sem, 1)
        s_ld.close(16 * len(loads)), s_pe.close(len(products)), s_ev.close(len(products))


def stage_gates(p, k, sums, folded, tail, tail_w, ht, whh, rz, nn):
    nc = p.nc
    s_pe, s_ev, s_g, s_a, s_v = p.sig("turn"), p.sig("turned"), p.sig("pe_out"), p.sig("ev_act"), p.sig("ev_dve")
    chunks, nt = len(folded), tail_w.shape[0]
    with ExitStack() as ctx:
        tp = [bank(ctx, nc, f"gt{q}") for q in range(2)]
        tq = [bank(ctx, nc, f"gq{q}") for q in range(2)]
        ps = [bank(ctx, nc, f"gp{q}") for q in range(2)]
        st = f32(ctx, nc, "gst", [P, 2, chunks * P])
        tt = f32(ctx, nc, "gtt", [nt, 2, P])
        with nc.Block() as block:
            @block.tensor
            def _(pe):
                def turn(b):
                    if b >= 2:
                        pe.wait_ge(s_ev.sem, s_ev.at(b - 1))
                    for c in range(chunks):
                        pe.transpose(tp[b % 2][:, c * P:(c + 1) * P], sums(b, c), k["ident"][:])
                    pe.transpose(tq[b % 2][0:nt, 0:P], tail(b), k["ident"][:]).then_inc(s_pe.sem, 1)

                turn(0)
                for b in range(NB):
                    if b + 1 < NB:
                        turn(b + 1)
                    pe.wait_ge(s_ev.sem, s_ev.at(b + 1))
                    if b >= 2:
                        pe.wait_ge(s_a.sem, s_a.at(b - 1))
                        pe.wait_ge(s_v.sem, s_v.at(b - 1))
                    o = ps[b % 2]
                    pe.matmul(o[:], tt[:, b % 2, :], tail_w, start=True, stop=False)
                    for c in range(chunks):
                        pe.matmul(o[:, 0:G3], st[:, b % 2, c * P:(c + 1) * P], folded[c], start=False, stop=False)
                    hb = ht[:, b * P:(b + 1) * P]
                    pe.matmul(o[:, 0:2 * D], hb, whh[:, 0:2 * D], start=False, stop=False)
                    pe.matmul(o[:, G3:G3 + D], hb, whh[:, 2 * D:G3], start=False, stop=True).then_inc(s_g.sem, 1)

            @block.scalar
            def _(act):
                def copy(b):
                    act.wait_ge(s_pe.sem, s_pe.at(b + 1))
                    if b >= 2:
                        act.wait_ge(s_g.sem, s_g.at(b - 1))
                    act.copy(st[:, b % 2, :], tp[b % 2][:, 0:chunks * P])
                    act.copy(tt[:, b % 2, :], tq[b % 2][0:nt, 0:P]).then_inc(s_ev.sem, 1)

                copy(0)
                for b in range(NB):
                    if b + 1 < NB:
                        copy(b + 1)
                    act.wait_ge(s_g.sem, s_g.at(b + 1))
                    act.activation(rz[:, b, :], ps[b % 2][:, 0:2 * D], ACT.Sigmoid).then_inc(s_a.sem, 1)

            @block.vector
            def _(dve):
                for b in range(NB):
                    dve.wait_ge(s_a.sem, s_a.at(b + 1))
                    dve.tensor_copy(nn[:, b, :], ps[b % 2][:, 2 * D:4 * D]).then_inc(s_v.sem, 1)
        for s in (s_pe, s_ev, s_g, s_a, s_v):
            s.close(NB)


def stage_gru_end(p, rz, nn, h, extra=None):
    nc = p.nc
    s_dve, s_var, s_std = p.sig("dve_chain"), p.sig("var"), p.sig("std")
    n = [0]
    with nc.Block() as block:
        @block.vector
        def _(dve):
            def chain(ins):
                link(p, dve, s_dve, ins, n)
            r, z = rz[:, :, 0:D], rz[:, :, D:2 * D]
            ni, ns = nn[:, :, 0:D], nn[:, :, D:2 * D]
            chain(dve.tensor_tensor(ns, ns, r, ALU.mult))
            dve.tensor_tensor(ni, ni, ns, ALU.add).then_inc(s_var.sem, 1)
            dve.wait_ge(s_std.sem, s_std.at(1))
            chain(dve.tensor_tensor(h[:], h[:], ni, ALU.subtract))
            chain(dve.tensor_tensor(h[:], h[:], z, ALU.mult))
            chain(dve.tensor_tensor(h[:], h[:], ni, ALU.add))
            if extra is not None:
                chain(dve.tensor_tensor(extra[:], extra[:], h[:], ALU.add))

        @block.scalar
        def _(act):
            act.wait_ge(s_var.sem, s_var.at(1))
            act.activation(nn[:, :, 0:D], nn[:, :, 0:D], ACT.Tanh).then_inc(s_std.sem, 1)
    s_dve.close(n[0]), s_var.close(1), s_std.close(1)


def layer_relational(p, k):
    nc, d = p.nc, p.d
    with ExitStack() as ctx:
        acc = f32(ctx, nc, "acc", [P, NB, D])
        stage_relation_sum(p, k, acc)
        stage_relation_add(p, k, acc)


def layer_edge_mlp(p, k, rounds=2):
    nc, d = p.nc, p.d
    stage_norm(p, k["x"], k["h"])
    for r in range(rounds):
        with ExitStack() as ctx:
            ht = f32(ctx, nc, "ht", [P, NPAD])
            acc = f32(ctx, nc, "acc", [P, NB, MH + 3])
            w1 = f32(ctx, nc, "w1", [P, 2, MH])
            b1 = f32(ctx, nc, "b1", [1, MH])
            wf = f32(ctx, nc, "wf", [AR, MH])
            wp = bf16(ctx, nc, "wp", [PACK, 2, MH])
            stage_turn(p, k, k["h"], ht)
            with ExitStack() as c2:
                pdst = bf16(c2, nc, "pdst", [P, NB, PARTS, MH])
                stage_edge_parts(p, k, r, ht, w1, b1, wf, wp, pdst)
                stage_edge_mlp(p, k, pdst, acc, wp)
            with ExitStack() as c2:
                w2t = f32(c2, nc, "w2t", [P, 2, MH])
                wih = f32(c2, nc, "wih", [P, 2, G3])
                whh = f32(c2, nc, "whh", [P, G3])
                b2 = f32(c2, nc, "b2", [P, 2])
                fold = f32(c2, nc, "fold", [P, 2, G3])
                tail = f32(c2, nc, "tail", [3, 4 * D])
                nn = f32(c2, nc, "nn", [P, NB, 2 * D])
                rz = f32(c2, nc, "rz", [P, NB, 2 * D])
                with nc.Block() as block:
                    @block.vector
                    def _(dve):
                        dve.memset(tail[:], 0.0)
                        dve.memset(acc[:, :, MH + 1:MH + 3], 1.0)
                stage_fold(p, [(w2t[:], d["w2_t"][r].rearrange("(c p) m -> p c m", p=P)),
                               (wih[:], d["wih_t"][r].rearrange("(c p) g -> p c g", p=P)),
                               (whh[:], d["whh_t"][r]),
                               (b2[:], d["b2_c"][r]),
                               (tail[1:2, 0:G3], d["L1_gnn_gru_bih"][r:r + 1, :]),
                               (tail[2:3, 0:2 * D], d["L1_gnn_gru_bhh"][r:r + 1, 0:2 * D]),
                               (tail[2:3, G3:4 * D], d["L1_gnn_gru_bhh"][r:r + 1, 2 * D:G3])],
                           [(fold[:, m, :], [(w2t[:, c, m * P:(m + 1) * P], wih[:, c, :]) for c in range(2)]) for m in range(2)]
                           + [(tail[0:1, 0:G3], [(b2[:, c:c + 1], wih[:, c, :]) for c in range(2)])], None)
                stage_gates(p, k, lambda b, c: acc[:, b, c * P:(c + 1) * P], [fold[:, c, :] for c in range(2)],
                            lambda b: acc[:, b, MH:MH + 3], tail[:], ht, whh[:], rz, nn)
                stage_gru_end(p, rz, nn, k["h"], k["x"] if r == rounds - 1 else None)


SC = 4 * HEADS
MASKED = -BIG


def stage_attention_constants(p, a):
    nc = p.nc
    s_c, s_d = p.sig("const"), p.sig("dve_chain")
    n = [0]
    with ExitStack() as ctx:
        row = i32(ctx, nc, "row", [P, 1])
        ri = i32(ctx, nc, "ri", [P, 3])
        rf = f32(ctx, nc, "rf", [P, 3])
        ts = f32(ctx, nc, "ts", [P, GT])
        with nc.Block() as block:
            @block.gpsimd
            def _(pool):
                pool.iota(row[:], pattern=[[0, 1]], base=0, channel_multiplier=1).then_inc(s_c.sem, 1)

            @block.vector
            def _(dve):
                def chain(ins):
                    link(p, dve, s_d, ins, n)
                dve.wait_ge(s_c.sem, s_c.at(1))
                dve.tensor_scalar(ri[:, 0:1], row[:], 3, None, ALU.bitwise_and)
                dve.tensor_scalar(ri[:, 1:2], row[:], SC - 1, None, ALU.bitwise_and)
                chain(dve.tensor_scalar(ri[:, 2:3], row[:], 4, None, ALU.arith_shift_right))
                chain(dve.tensor_copy(rf[:], ri[:]))
                chain(dve.tensor_scalar(rf[:, 1:2], rf[:, 1:2], float(HEADS), None, ALU.is_ge))
                dve.tensor_scalar(a["head"][:], a["iota"][:, 0:HEADS], rf[:, 0:1], rf[:, 1:2], ALU.is_equal, ALU.mult)
                chain(dve.tensor_scalar(ts[:], a["iota"][:, 0:GT], rf[:, 2:3], None, ALU.is_equal))
                dve.tensor_copy(a["tile"][:], ts[:].unsqueeze(2).to_broadcast([P, GT, P]))
                for h in range(HEADS):
                    dve.tensor_scalar(a["masked"][:, h, :], a["ident"][:], MASKED, None, ALU.mult)
        s_c.close(1), s_d.close(n[0])


def stage_score_table(p, score, table):
    nc = p.nc
    s_dve, s_st = p.sig("dve_chain"), p.sig("store0")
    n = [0]
    with ExitStack() as ctx:
        row = f32(ctx, nc, "srow", [P, NB, SC])
        half = ctx.enter_context(nc.sbuf_tensor(unique("half"), [P, NB, HEADS], mybir.dt.bfloat16))
        left = f32(ctx, nc, "left", [P, NB, HEADS])
        with nc.Block() as block:
            @block.vector
            def _(dve):
                def chain(ins):
                    link(p, dve, s_dve, ins, n)
                chain(dve.tensor_copy(row[:, :, 0:HEADS], score))
                chain(dve.tensor_copy(left[:], score))
                for part in range(1, 4):
                    out = row[:, :, part * HEADS:(part + 1) * HEADS]
                    chain(dve.tensor_copy(half[:], left[:]))
                    chain(dve.tensor_copy(out, half[:]))
                    chain(dve.tensor_tensor(left[:], left[:], out, ALU.subtract))

            @block.sync
            def _(sp):
                sp.wait_ge(s_dve.sem, s_dve.at(n[0]))
                sp.dma_start(table.rearrange("(b p) f -> p b f", p=P), row[:]).then_inc(s_st.sem, 16)
                sp.wait_ge(s_st.sem, s_st.at(16))
        s_dve.close(n[0]), s_st.close(16)


def stage_edge_max(p, k, a, score, mx, table, kept=None):
    nc, d = p.nc, p.d
    BF = mybir.dt.bfloat16
    s_oh, s_turn, s_spread = p.sig("onehot"), p.sig("turn"), p.sig("spread")
    s_bank, s_red, s_max, s_se = p.sig("pre"), p.sig("added"), p.sig("acc"), p.sig("scaled")
    s_st = [p.sig("store0"), p.sig("store1")]
    with ExitStack() as ctx:
        ga = Gather(p, ctx, table, k["src"], SC + (D if kept is not None else 0))
        parts16 = f32(ctx, nc, "score_parts", [P, 2, GT, SC])
        away = ctx.enter_context(nc.sbuf_tensor(unique("away"), [P, 2, GT, P], BF))
        spread = ctx.enter_context(nc.sbuf_tensor(unique("spread"), [P, 2, HEADS, P], BF))
        tmax = f32(ctx, nc, "tmax", [P, GU, HEADS])
        tb = [bank(ctx, nc, f"tb{q}") for q in range(2)]
        vb = ctx.enter_context(nc.psum_tensor(unique("vb"), [P, 4, 512], F32))
        with nc.Block() as block:
            @block.gpsimd
            def _(pool):
                ga.program(pool)

            if kept is not None:
                @block.sync
                def _(sp):
                    kv = kept.rearrange("(g p) f -> p g f", p=P)
                    with sp.Fori(0, BODIES) as i:
                        for q in range(2):
                            for v in range(GU):
                                row = ga.s_row[GU * q + v]
                                sp.wait_ge(row.sem, row.at(32 * (i + 1)))
                                p.apart(sp)
                            sp.dma_start(kv[:, bass.ds(2 * i + q, 1), :].rearrange("p g (t f) -> p (g t) f", t=GT),
                                         ga.rows[:, q, :, SC:SC + D]).then_inc(s_st[q].sem, 16)
                    for q in range(2):
                        sp.wait_ge(s_st[q].sem, s_st[q].at(16 * BODIES))

            @block.scalar
            def _(act):
                ga.feed(act, 0, 0)

                def body(i, first, last):
                    for q in range(2):
                        g = 2 * i + q
                        if not (last and q == 1):
                            if not (first and q == 0):
                                act.wait_ge(s_se.sem, s_se.at(g))
                                p.apart(act)
                                if kept is not None:
                                    act.wait_ge(s_st[1 - q].sem, s_st[1 - q].at(16 * (i + q)))
                                    p.apart(act)
                            ga.feed(act, g + 1, 1 - q)
                        if not first:
                            act.wait_ge(s_turn.sem, s_turn.at(g - 1))
                            p.apart(act)
                        for v in range(GU):
                            act.wait_ge(ga.s_row[GU * q + v].sem, ga.s_row[GU * q + v].at(32 * (i + 1)))
                            p.apart(act)
                        act.copy(parts16[:, q], ga.rows[:, q, :, 0:SC])
                        act.copy(score[:, bass.ds(g * GT, GT), :], ga.rows[:, q, :, 0:HEADS]).then_inc(s_se.sem, 1)
                over_bodies(act, body)

            @block.tensor
            def _(pe):
                def turn(g, q, first):
                    pe.wait_ge(s_se.sem, s_se.at(g + 1))
                    if not first:
                        pe.wait_ge(s_spread.sem, s_spread.at(g - 1))
                    pe.transpose(tb[q][:, 0:P], parts16[:, q].rearrange("p t c -> p (t c)"), k["ident"][:]).then_inc(s_turn.sem, 1)
                turn(0, 0, True)

                def body(i, first, last):
                    for q in range(2):
                        g = 2 * i + q
                        pe.wait_ge(s_oh.sem, s_oh.at(g + 1))
                        pe.wait_ge(s_spread.sem, s_spread.at(g + 1))
                        for v in range(GU):
                            u = 4 * g + v
                            if not (first and q == 0 and v < 2):
                                pe.wait_ge(s_red.sem, s_red.at(u - 1))
                            for t in range(2):
                                o, j = vb[:, 2 * (v % 2) + t, :], 2 * v + t
                                pe.matmul(o, away[:, q, j, :], a["masked"][:].rearrange("p h e -> p (h e)"), start=True, stop=False)
                                mm = pe.matmul(o, a["tile"][:, j, :], spread[:, q].rearrange("p h e -> p (h e)"), start=False, stop=True)
                            mm.then_inc(s_bank.sem, 1)
                            if v == 2 and not (last and q == 1):
                                turn(g + 1, 1 - q, first and q == 0)
                over_bodies(pe, body)

            @block.vector
            def _(dve):
                def masks(g, q):
                    onehot16(dve, k, away, g, q, ALU.not_equal).then_inc(s_oh.sem, 1)

                def parts(g, q):
                    dve.wait_ge(s_turn.sem, s_turn.at(g + 1))
                    dve.tensor_tensor(spread[:, q], tb[q][:, 0:P].unsqueeze(1).to_broadcast([P, HEADS, P]),
                                      a["head"][:].unsqueeze(2).to_broadcast([P, HEADS, P]), ALU.mult).then_inc(s_spread.sem, 1)

                def merge(u, o, b):
                    dve.wait_ge(s_red.sem, s_red.at(u + 1))
                    if not (isinstance(u, int) and u == 0):
                        dve.wait_ge(s_max.sem, s_max.at(u))
                    m = mx[:, bass.ds(b, 1), :].rearrange("p a h -> p (a h)")
                    dve.tensor_tensor(m, m, tmax[:, o, :], ALU.max).then_inc(s_max.sem, 1)
                masks(0, 0)
                parts(0, 0)

                def body(i, first, last):
                    for q in range(2):
                        g = 2 * i + q
                        blocks = unit_blocks(nc, dve, k, g, 1)
                        for v in range(GU):
                            u = 4 * g + v
                            dve.wait_ge(s_bank.sem, s_bank.at(u + 1))
                            dve.tensor_reduce(tmax[:, v, :], vb[:, 2 * (v % 2):2 * (v % 2) + 2, :].rearrange("p t (h e) -> p h t e", h=HEADS),
                                              AX.XY, ALU.max).then_inc(s_red.sem, 1)
                            if v == 1 and not (last and q == 1):
                                if not (first and q == 0):
                                    dve.wait_ge(s_bank.sem, s_bank.at(4 * g))
                                masks(g + 1, 1 - q)
                            if v == 3 and not (last and q == 1):
                                parts(g + 1, 1 - q)
                            if not (first and q == 0 and v == 0):
                                merge(u - 1, (v - 1) % GU, blocks[v])
                over_bodies(dve, body)
                merge(UNITS - 1, GU - 1, unit_blocks(nc, dve, k, GROUPS, 1)[0])
        ga.close()
        if kept is not None:
            s_st[0].close(16 * BODIES), s_st[1].close(16 * BODIES)
        for s in (s_oh, s_turn, s_spread, s_se):
            s.close(GROUPS)
        for s in (s_bank, s_red, s_max):
            s.close(UNITS)


def stage_shift(p, k, sd, mx, adm3, ss=None, xw=None, acc=None):
    nc = p.nc
    s_dve, s_var, s_std = p.sig("dve_chain"), p.sig("var"), p.sig("std")
    n = [0]
    with ExitStack() as ctx:
        t = f32(ctx, nc, "shift", [P, NB, HEADS])
        adm = f32(ctx, nc, "adm", [P, NB, 2 * HEADS])
        e = f32(ctx, nc, "self", [P, NB, HEADS])
        with nc.Block() as block:
            @block.vector
            def _(dve):
                def chain(ins):
                    link(p, dve, s_dve, ins, n)
                ad, m = adm[:, :, 0:HEADS], adm[:, :, HEADS:2 * HEADS]
                chain(dve.tensor_copy(ad, sd))
                chain(dve.tensor_tensor(t[:], mx[:], ad, ALU.add))
                chain(dve.scalar_tensor_tensor(out=m, in0=t[:], scalar=SLOPE, in1=t[:], op0=ALU.mult, op1=ALU.max))
                if ss is not None:
                    chain(dve.tensor_tensor(e[:], ss, ad, ALU.add))
                    chain(dve.scalar_tensor_tensor(out=t[:], in0=e[:], scalar=SLOPE, in1=e[:], op0=ALU.mult, op1=ALU.max))
                    dve.tensor_tensor(e[:], t[:], m, ALU.subtract).then_inc(s_var.sem, 1)
                    dve.wait_ge(s_std.sem, s_std.at(1))
                    den = acc[:, :, D:D + HEADS]
                    chain(dve.tensor_copy(den, e[:]))
                    c = D // HEADS
                    for h in range(HEADS):
                        chain(dve.tensor_tensor(acc[:, :, h * c:(h + 1) * c], xw[:, :, h * c:(h + 1) * c],
                                                e[:, :, h:h + 1].to_broadcast([P, NB, c]), ALU.mult))
                else:
                    chain(dve.memset(acc[:], 0.0))
                for part in range(PARTS):
                    chain(dve.tensor_copy(adm3[:, :, part, :], adm[:]))
                    if part < PARTS - 1:
                        chain(dve.tensor_tensor(adm[:], adm[:], adm3[:, :, part, :], ALU.subtract))

            if ss is not None:
                @block.scalar
                def _(act):
                    act.wait_ge(s_var.sem, s_var.at(1))
                    act.activation(e[:], e[:], ACT.Exp).then_inc(s_std.sem, 1)
        s_dve.close(n[0])
        if ss is not None:
            s_var.close(1), s_std.close(1)


def stage_attend(p, k, score, adm, acc, table=None, kept=None):
    nc = p.nc
    wide = kept is None
    W = HEADS * D if wide else D
    s_oh, s_oh16, s_turn, s_oht = p.sig("onehot"), p.sig("onehot16"), p.sig("turn"), p.sig("oht")
    s_em, s_z, s_w, s_c = p.sig("pre"), p.sig("added"), p.sig("relu"), p.sig("dve_chain")
    s_rd, s_ra, s_agg, s_acc = p.sig("scaled"), p.sig("spread"), p.sig("agg"), p.sig("acc")
    LAG = 2
    A = PARTS * 2 * HEADS
    DH = HEADS // 2
    with ExitStack() as ctx:
        if wide:
            ga = Gather(p, ctx, table, k["src"], D)
            rows, s_row, landed = ga.rows, ga.s_row, 32
        else:
            rows, landed = f32(ctx, nc, "rows", [P, 2, GT, D]), 16
            s_row = [p.sig(f"kept{q}") for q in range(2) for _ in range(GU)]
        oh = f32(ctx, nc, "oh", [P, 2, GT, P])
        oh16 = bf16(ctx, nc, "oh16", [P, 2, GT, P])
        oht = bf16(ctx, nc, "oht", [P, 2, GT, P])
        ad = f32(ctx, nc, "ad", [P, 2, GT, 2 * HEADS])
        z = f32(ctx, nc, "z", [P, 2, GT, HEADS])
        y = f32(ctx, nc, "y", [P, 2, GT, HEADS])
        if wide:
            wr = f32(ctx, nc, "wr", [P, GU, 2, W])
            w = f32(ctx, nc, "w", [P, 2, GT, HEADS])
        else:
            wr = f32(ctx, nc, "wr", [P, 2, GT, W + HEADS])
            w = wr[:, :, :, W:W + HEADS]
        tp = [ctx.enter_context(nc.psum_tensor(unique("tp"), [P, GT * P], BF16)) for q in range(2)]
        em = [bank(ctx, nc, f"em{q}") for q in range(2)]
        pa = [bank(ctx, nc, f"pa{q}") for q in range(2)]
        pd = [bank(ctx, nc, f"pd{q}") for q in range(2)] if wide else None
        with nc.Block() as block:
            if wide:
                @block.gpsimd
                def _(pool):
                    ga.program(pool)
            else:
                @block.sync
                def _(sp):
                    kv = kept.rearrange("(g p) f -> p g f", p=P)

                    def load(g, q):
                        sp.dma_start(rows[:, q].rearrange("p t f -> p (t f)"),
                                     kv[:, bass.ds(g, 1), :].rearrange("p g f -> p (g f)")).then_inc(s_row[GU * q].sem, 16)
                    for q in range(2):
                        load(q, q)
                    with sp.Fori(0, BODIES - 1) as i:
                        for q in range(2):
                            sp.wait_ge(s_rd.sem, s_rd.at(4 * (2 * i + q + 1)))
                            p.apart(sp)
                            load(2 * i + q + 2, q)

            @block.scalar
            def _(act):
                def onehots(g, q, first):
                    if not first:
                        act.wait_ge(s_agg.sem, s_agg.at(4 * g - 4))
                        p.apart(act)
                    act.wait_ge(s_oh16.sem, s_oh16.at(g + 1))
                    act.copy(oh[:, q].rearrange("p t n -> p (t n)"), oh16[:, q].rearrange("p t n -> p (t n)")).then_inc(s_oh.sem, 1)

                def turned(g, q, first):
                    if not first:
                        act.wait_ge(s_em.sem, s_em.at(g - 1))
                        p.apart(act)
                    act.wait_ge(s_turn.sem, s_turn.at(g + 1))
                    act.copy(oht[:, q].rearrange("p t n -> p (t n)"), tp[q][:]).then_inc(s_oht.sem, 1)

                def weights(g, q, first):
                    if not first:
                        act.wait_ge(s_agg.sem, s_agg.at(4 * g - 4))
                        p.apart(act)
                    act.wait_ge(s_z.sem, s_z.at(g + 1))
                    act.activation(w[:, q], z[:, q], ACT.Exp).then_inc(s_w.sem, 1)
                if wide:
                    ga.feed(act, 0, 0)
                turned(0, 0, True)
                onehots(0, 0, True)
                weights(0, 0, True)

                def body(i, first, last):
                    for q in range(2):
                        g = 2 * i + q
                        if wide and not (last and q == 1):
                            if not (first and q == 0):
                                act.wait_ge(s_rd.sem, s_rd.at(4 * g))
                                p.apart(act)
                            ga.feed(act, g + 1, 1 - q)
                        for v in range(GU):
                            u = 4 * g + v
                            if wide:
                                if v == 0:
                                    act.wait_ge(s_w.sem, s_w.at(g + 1))
                                    p.apart(act)
                                act.wait_ge(s_row[GU * q + v].sem, s_row[GU * q + v].at(landed * (i + 1)))
                                p.apart(act)
                                if not (first and q == 0):
                                    act.wait_ge(s_agg.sem, s_agg.at(u - GU + 1))
                                    p.apart(act)
                                for t in range(2):
                                    j = 2 * v + t
                                    for h in range(DH, HEADS):
                                        last_i = act.activation(wr[:, v, t, h * D:(h + 1) * D], rows[:, q, j, :], ACT.Copy,
                                                                scale=w[:, q, j, h:h + 1])
                                last_i.then_inc(s_ra.sem, 1)
                            if v == 0 and not (last and q == 1):
                                turned(g + 1, 1 - q, first and q == 0)
                            if v == 1 and not (last and q == 1):
                                onehots(g + 1, 1 - q, first and q == 0)
                        if not (last and q == 1):
                            weights(g + 1, 1 - q, first and q == 0)
                over_bodies(act, body)

            @block.tensor
            def _(pe):
                def turn(g, q, first):
                    pe.wait_ge(s_oh16.sem, s_oh16.at(g + 1))
                    if not first:
                        pe.wait_ge(s_oht.sem, s_oht.at(g - 1))
                    turn_onehots(pe, k, oh16, tp, q, s_turn)

                def values(g, q, first):
                    if not first:
                        pe.wait_ge(s_z.sem, s_z.at(g - 1))
                    blocks = unit_blocks(nc, pe, k, g)
                    pe.wait_ge(s_oht.sem, s_oht.at(g + 1))
                    for v in range(GU):
                        for t in range(2):
                            j = 2 * v + t
                            mm = pe.matmul(em[q][:, A * j:A * j + A], oht[:, q, j, :],
                                           adm[:, bass.ds(blocks[v], 1), :, :].rearrange("p a c f -> p (a c f)"), start=True, stop=True)
                    mm.then_inc(s_em.sem, 1)
                turn(0, 0, True)
                values(0, 0, True)
                turn(1, 1, True)

                def body(i, first, last):
                    for q in range(2):
                        g = 2 * i + q
                        for v in range(GU):
                            u = 4 * g + v
                            pe.wait_ge(s_rd.sem, s_rd.at(u + 1))
                            if v == 0:
                                pe.wait_ge(s_w.sem, s_w.at(g + 1))
                                pe.wait_ge(s_oh.sem, s_oh.at(g + 1))
                            if wide:
                                pe.wait_ge(s_ra.sem, s_ra.at(u + 1))
                            if not (first and q == 0 and v < 2):
                                pe.wait_ge(s_acc.sem, s_acc.at(u - 1))
                            for t in range(2):
                                j = 2 * v + t
                                if wide:
                                    pe.matmul(pa[v % 2][:, 0:W], oh[:, q, j, :], wr[:, v, t, :], start=t == 0, stop=t == 1)
                                    mm = pe.matmul(pd[v % 2][:, 0:HEADS], oh[:, q, j, :], w[:, q, j, :], start=t == 0, stop=t == 1)
                                else:
                                    mm = pe.matmul(pa[v % 2][:, 0:W + HEADS], oh[:, q, j, :], wr[:, q, j, :], start=t == 0, stop=t == 1)
                            mm.then_inc(s_agg.sem, 1)
                            if v == 1 and not (last and q == 1):
                                values(g + 1, 1 - q, first and q == 0)
                            if v == 2 and not last:
                                turn(g + 2, q, False)
                over_bodies(pe, body)

            @block.vector
            def _(dve):
                def onehots16(g, q, first):
                    if not first:
                        dve.wait_ge(s_turn.sem, s_turn.at(g - 1))
                        dve.wait_ge(s_oh.sem, s_oh.at(g - 1))
                    onehot16(dve, k, oh16, g, q).then_inc(s_oh16.sem, 1)

                def exponents(g, q, first):
                    dve.wait_ge(s_em.sem, s_em.at(g + 1))
                    if not first:
                        dve.wait_ge(s_w.sem, s_w.at(g - 1))
                    dve.tensor_reduce(ad[:, q], em[q][:, 0:A * GT].rearrange("p (t c f) -> p t f c", t=GT, c=PARTS), AX.X,
                                      ALU.add).then_inc(s_c.sem, 1)
                    dve.wait_ge(s_c.sem, s_c.at(3 * g + 1))
                    dve.tensor_tensor(y[:, q], ad[:, q, :, 0:HEADS], score[:, bass.ds(g * GT, GT), :], ALU.add).then_inc(s_c.sem, 1)
                    dve.wait_ge(s_c.sem, s_c.at(3 * g + 2))
                    dve.scalar_tensor_tensor(out=y[:, q], in0=y[:, q], scalar=SLOPE, in1=y[:, q],
                                             op0=ALU.mult, op1=ALU.max).then_inc(s_c.sem, 1)
                    dve.wait_ge(s_c.sem, s_c.at(3 * g + 3))
                    dve.tensor_tensor(z[:, q], y[:, q], ad[:, q, :, HEADS:2 * HEADS], ALU.subtract).then_inc(s_z.sem, 1)

                def add(u, x, b):
                    dve.wait_ge(s_agg.sem, s_agg.at(u + 1))
                    if not (isinstance(u, int) and u == 0):
                        dve.wait_ge(s_acc.sem, s_acc.at(u))
                    n = W if wide else W + HEADS
                    a = acc[:, bass.ds(b, 1), 0:n].rearrange("p a f -> p (a f)")
                    if wide:
                        c = acc[:, bass.ds(b, 1), W:W + HEADS].rearrange("p a f -> p (a f)")
                        dve.tensor_tensor(c, c, pd[x % 2][:, 0:HEADS], ALU.add)
                    dve.tensor_tensor(a, a, pa[x % 2][:, 0:n], ALU.add).then_inc(s_acc.sem, 1)

                onehots16(0, 0, True)
                onehots16(1, 1, True)
                exponents(0, 0, True)

                def body(i, first, last):
                    for q in range(2):
                        g = 2 * i + q
                        blocks = unit_blocks(nc, dve, k, g, LAG)
                        for v in range(GU):
                            u, x = 4 * g + v, GU * q + v
                            dve.wait_ge(s_row[x].sem, s_row[x].at(landed * (i + 1)))
                            if v == 0:
                                dve.wait_ge(s_w.sem, s_w.at(g + 1))
                            if wide and not (first and q == 0):
                                dve.wait_ge(s_agg.sem, s_agg.at(u - GU + 1))
                            if not wide and not first:
                                dve.wait_ge(s_agg.sem, s_agg.at(4 * g - 4))
                            for t in range(2):
                                j = 2 * v + t
                                if wide:
                                    last_i = dve.tensor_tensor(wr[:, v, t, 0:DH * D].rearrange("p (h f) -> p h f", h=DH),
                                                               rows[:, q, j, :].unsqueeze(1).to_broadcast([P, DH, D]),
                                                               w[:, q, j, 0:DH].unsqueeze(2).to_broadcast([P, DH, D]), ALU.mult)
                                else:
                                    last_i = dve.tensor_tensor(wr[:, q, j, 0:W].rearrange("p (h f) -> p h f", h=HEADS),
                                                               rows[:, q, j, :].rearrange("p (h f) -> p h f", h=HEADS),
                                                               w[:, q, j, :].unsqueeze(2).to_broadcast([P, HEADS, D // HEADS]), ALU.mult)
                            last_i.then_inc(s_rd.sem, 1)
                            if not (first and x < LAG):
                                add(u - LAG, (x - LAG) % BU, blocks[v])
                            if v == 1 and not last:
                                onehots16(g + 2, q, False)
                            if v == 2 and not (last and q == 1):
                                exponents(g + 1, 1 - q, first and q == 0)
                over_bodies(dve, body)
                blocks = unit_blocks(nc, dve, k, GROUPS, LAG)
                for v in range(LAG):
                    u = UNITS - LAG + v
                    add(u, u % BU, blocks[v])
        if wide:
            ga.close()
        else:
            s_row[0].close(16 * BODIES), s_row[GU].close(16 * BODIES)
        s_oh.close(GROUPS), s_oh16.close(GROUPS), s_turn.close(GROUPS), s_oht.close(GROUPS), s_c.close(3 * GROUPS)
        for s in (s_em, s_z, s_w):
            s.close(GROUPS)
        for s in (s_rd, s_agg, s_acc):
            s.close(UNITS)
        if wide:
            s_ra.close(UNITS)


def stage_vector(p, loads, steps):
    nc = p.nc
    s_ld, s_dve = p.sig("load"), p.sig("dve_chain")
    n = [0]
    with nc.Block() as block:
        @block.sync
        def _(sp):
            for dst, src in loads:
                sp.dma_start(dst, src).then_inc(s_ld.sem, 16)

        @block.vector
        def _(dve):
            if loads:
                dve.wait_ge(s_ld.sem, s_ld.at(16 * len(loads)))
            for step in steps:
                link(p, dve, s_dve, step(dve), n)
    s_ld.close(16 * len(loads)), s_dve.close(n[0])


def layer_attention(p, k):
    nc, d = p.nc, p.d
    BF = mybir.dt.bfloat16
    stage_norm(p, k["x"], k["h"])
    with ExitStack() as ctx:
        acc = f32(ctx, nc, "acc", [P, NB, D + HEADS])
        skip = f32(ctx, nc, "skip", [P, NB, D])
        xw = f32(ctx, nc, "xw", [P, NB, D])
        sc = f32(ctx, nc, "sc", [P, 2, NB, HEADS])
        mx = f32(ctx, nc, "mx", [P, NB, HEADS])
        adm = bf16(ctx, nc, "adm3", [P, NB, PARTS, 2 * HEADS])
        with ExitStack() as c2:
            ht = f32(c2, nc, "ht", [P, NPAD])
            xn = f32(c2, nc, "xn", [P, NB, D])
            w = f32(c2, nc, "w2", [P, 2, D])
            bp = f32(c2, nc, "bp", [1, D])
            gb = f32(c2, nc, "gb", [P, 4, D])
            tmp = f32(c2, nc, "stmp", [P, NB, D])

            def lhs(b):
                return ht[:, b * P:(b + 1) * P]
            stage_turn(p, k, k["h"], ht)
            stage_project(p, k, ht, [(w[:, 0, :], d["L2_gnn_W_proj"]), (w[:, 1, :], d["L2_gnn_W_gat"]),
                                     (bp[:], d["L2_gnn_b_proj"].rearrange("(a f) -> a f", a=1))] +
                          [(gb[:, j, :], v.partition_broadcast(P)) for j, v in enumerate(
                              (d["L2_gnn_gamma"], d["L2_gnn_beta"], d["L2_gnn_att_src"].rearrange("h c -> (h c)"),
                               d["L2_gnn_att_dst"].rearrange("h c -> (h c)")))],
                          [(0, D, lhs, w[:, 0, :]), (0, D, lambda b: k["ones"][0:1, 0:P], bp[:])], D, skip)
            stage_norm(p, k["h"], xn, relu=False, gamma=gb[:, 0, :], beta=gb[:, 1, :])
            stage_turn(p, k, xn, ht)
            stage_project(p, k, ht, [], [(0, D, lhs, w[:, 1, :])], D, xw)
            stage_store_rows(p, d["t_both"][:, SC:SC + D], xw[:])
            steps = []
            for j in range(2):
                steps.append(lambda dve, j=j: dve.tensor_tensor(tmp[:], xw[:], gb[:, 2 + j, :].unsqueeze(1).to_broadcast([P, NB, D]), ALU.mult))
                steps.append(lambda dve, j=j: dve.tensor_reduce(sc[:, j], tmp[:].rearrange("p b (h c) -> p b h c", h=HEADS), AX.X, ALU.add))
            steps.append(lambda dve: dve.tensor_copy(mx[:], sc[:, 0]))
            stage_vector(p, [], steps)
        stage_score_table(p, sc[:, 0], d["t_both"][:, 0:SC])
        with ExitStack() as c2:
            es = f32(c2, nc, "es", [P, TILES, HEADS])
            with ExitStack() as c3:
                a = {"iota": k["iota"], "ident": k["ident"], "head": f32(c3, nc, "head", [P, HEADS]),
                     "tile": c3.enter_context(nc.sbuf_tensor(unique("tile"), [P, GT, P], BF)),
                     "masked": c3.enter_context(nc.sbuf_tensor(unique("masked"), [P, HEADS, P], BF))}
                stage_attention_constants(p, a)
                stage_edge_max(p, k, a, es, mx, d["t_both"], d["edge_rows"])
            stage_shift(p, k, sc[:, 1], mx, adm, sc[:, 0], xw, acc)
            stage_attend(p, k, es, adm, acc, kept=d["edge_rows"])
        with ExitStack() as c2:
            bias = f32(c2, nc, "bgat", [P, D])
            num, den = acc[:, :, 0:D], acc[:, :, D:D + HEADS]
            c = D // HEADS
            stage_vector(p, [(bias[:], d["L2_gnn_bias_gat"].partition_broadcast(P))], [
                lambda dve: dve.tensor_scalar(den, den, 1e-16, None, ALU.add),
                lambda dve: dve.reciprocal(den, den)] + [
                lambda dve, h=h: dve.tensor_tensor(acc[:, :, h * c:(h + 1) * c], acc[:, :, h * c:(h + 1) * c],
                                                   acc[:, :, D + h:D + h + 1].to_broadcast([P, NB, c]), ALU.mult) for h in range(HEADS)] + [
                lambda dve: dve.tensor_tensor(num, num, bias[:].unsqueeze(1).to_broadcast([P, NB, D]), ALU.add),
                lambda dve: dve.tensor_tensor(num, num, skip[:], ALU.add),
                lambda dve: dve.scalar_tensor_tensor(out=k["x"][:], in0=num, scalar=0.0, in1=k["x"][:], op0=ALU.max, op1=ALU.add)])


def layer_attention_gru(p, k):
    nc, d = p.nc, p.d
    BF = mybir.dt.bfloat16
    stage_norm(p, k["x"], k["h"])
    with ExitStack() as ctx:
        acc = f32(ctx, nc, "acc", [P, NB, HEADS * D + HEADS])
        ht = f32(ctx, nc, "ht", [P, NPAD])
        adm = bf16(ctx, nc, "adm3", [P, NB, PARTS, 2 * HEADS])
        fold = f32(ctx, nc, "fold", [P, HEADS, G3])
        whh = f32(ctx, nc, "whh", [P, G3])
        tail = f32(ctx, nc, "tail", [2, 4 * D])
        with ExitStack() as c1:
            es = f32(c1, nc, "es", [P, TILES, HEADS])
            sc = f32(c1, nc, "sc", [P, NB, 2 * HEADS])
            mx = f32(c1, nc, "mx", [P, NB, HEADS])
            with ExitStack() as c2:
                wt = f32(c2, nc, "wt", [P, HEADS, D])
                wih = f32(c2, nc, "wih", [P, HEADS, G3])
                at = f32(c2, nc, "at", [P, 2, HEADS])
                vec = f32(c2, nc, "vec", [P, 2 * HEADS])
                stage_vector(p, [], [lambda dve: dve.memset(tail[:], 0.0), lambda dve: dve.memset(mx[:], MASKED)])
                stage_turn(p, k, k["h"], ht)
                stage_store_rows(p, d["t_att"], k["h"][:])
                stage_fold(p, [(wt[:], d["w3_t"].rearrange("h e d -> e h d")),
                               (wih[:], d["wih3_t"].rearrange("(h e) g -> e h g", h=HEADS)),
                               (whh[:], d["whh3_t"]), (at[:], d["a3_t"]),
                               (tail[0:1, 0:G3], d["L3_gnn_b_ih"].rearrange("(a g) -> a g", a=1)),
                               (tail[1:2, 0:2 * D], d["L3_gnn_b_hh"][0:2 * D].rearrange("(a g) -> a g", a=1)),
                               (tail[1:2, G3:4 * D], d["L3_gnn_b_hh"][2 * D:G3].rearrange("(a g) -> a g", a=1))],
                           [(fold[:, h, :], [(wt[:, h, :], wih[:, h, :])]) for h in range(HEADS)] +
                           [(vec[:, j * HEADS + h:j * HEADS + h + 1], [(wt[:, h, :], at[:, j, h:h + 1])]) for j in range(2) for h in range(HEADS)], None)
                stage_project(p, k, ht, [], [(0, 2 * HEADS, lambda b: ht[:, b * P:(b + 1) * P], vec[:])], 2 * HEADS, sc)
            stage_score_table(p, sc[:, :, 0:HEADS], d["t_score"])
            with ExitStack() as c3:
                a = {"iota": k["iota"], "ident": k["ident"], "head": f32(c3, nc, "head", [P, HEADS]),
                     "tile": c3.enter_context(nc.sbuf_tensor(unique("tile"), [P, GT, P], BF)),
                     "masked": c3.enter_context(nc.sbuf_tensor(unique("masked"), [P, HEADS, P], BF))}
                stage_attention_constants(p, a)
                stage_edge_max(p, k, a, es, mx, d["t_score"])
            stage_shift(p, k, sc[:, :, HEADS:2 * HEADS], mx, adm, acc=acc)
            stage_attend(p, k, es, adm, acc, table=d["t_att"])
        W = HEADS * D
        den = acc[:, :, W:W + HEADS]
        stage_vector(p, [], [
            lambda dve: dve.tensor_scalar(den, den, 1e-30, None, ALU.max),
            lambda dve: dve.reciprocal(den, den)] + [
            lambda dve, h=h: dve.tensor_tensor(acc[:, :, h * D:(h + 1) * D], acc[:, :, h * D:(h + 1) * D],
                                               acc[:, :, W + h:W + h + 1].to_broadcast([P, NB, D]), ALU.mult) for h in range(HEADS)])
        with ExitStack() as c2:
            rz = f32(c2, nc, "rz", [P, NB, 2 * D])
            nn = f32(c2, nc, "nn", [P, NB, 2 * D])
            stage_gates(p, k, lambda b, c: acc[:, b, c * P:(c + 1) * P], [fold[:, h, :] for h in range(HEADS)],
                        lambda b: k["ones"][:, 0:2], tail[:], ht, whh[:], rz, nn)
            stage_gru_end(p, rz, nn, k["h"], k["x"])


def build(nc, d, out):
    with ExitStack() as ctx:
        p = Program(nc, ctx, d)
        k = {"x": f32(ctx, nc, "x", [P, NB, D]), "h": f32(ctx, nc, "h", [P, NB, D]),
             "ident": f32(ctx, nc, "ident", [P, P]), "ones": f32(ctx, nc, "ones", [P, P]),
             "tri": f32(ctx, nc, "tri", [P, P]), "iota": f32(ctx, nc, "iota", [P, UNITS]),
             "iota_i": i32(ctx, nc, "iota_i", [P, UNITS]), "bmap": i32(ctx, nc, "bmap", [1, LAGS, UNITS + 8]),
             "meta": f32(ctx, nc, "meta", [P, TILES]), "src": i32(ctx, nc, "src", [P, TILES]),
             "ident16": bf16(ctx, nc, "ident16", [P, P]), "iota16": bf16(ctx, nc, "iota16", [P, P]),
             "meta16": bf16(ctx, nc, "meta16", [P, TILES])}
        with ExitStack() as c2:
            s = {"meta": f32(c2, nc, "smeta", [SORT_P, SORT_J, 4]), "key": f32(c2, nc, "key", [SORT_P, SORT_J]),
                 "dst_i": i32(c2, nc, "dst_i", [SORT_P, SORT_J]), "src_i": i32(c2, nc, "src_i", [SORT_P, SORT_J]),
                 "typ_i": i32(c2, nc, "typ_i", [SORT_P, SORT_J]), "weight": f32(c2, nc, "weight", [SORT_P, SORT_J]),
                 "run": f32(c2, nc, "run", [SORT_P, NB]), "uend": f32(c2, nc, "uend", [P, NB])}
            blank = f32(c2, nc, "blank", [P, TILES // INIT, REC])
            ht = f32(c2, nc, "ht", [P, NPAD])
            stage_constants(p, k, s, blank)
            stage_counts(p, k, s)
            stage_scatter(p, k, s, ht)
        layer_relational(p, k)
        layer_edge_mlp(p, k)
        layer_attention(p, k)
        layer_attention_gru(p, k)
        s_out = p.sig("out")
        with nc.Block() as block:
            @block.sync
            def _(sp):
                sp.dma_start(out[0:(NB - 1) * P, :].rearrange("(b p) f -> p b f", p=P), k["x"][:, 0:NB - 1, :]).then_inc(s_out.sem, 16)
                sp.dma_start(out[(NB - 1) * P:N_NODES, :], k["x"][0:LAST_ROWS, NB - 1, :]).then_inc(s_out.sem, 16)
                sp.wait_ge(s_out.sem, 32)


_INS = ["x", "src", "dst", "edge_attr_26", "edge_type_8", "edge_weight1", "L0_gnn_weight", "L0_gnn_bias",
        "L1_gnn_mlp_w1", "L1_gnn_mlp_b1", "L1_gnn_gru_bih", "L1_gnn_gru_bhh", "w2_t", "wih_t", "whh_t", "b2_c",
        "L2_gnn_gamma", "L2_gnn_beta", "L2_gnn_W_gat", "L2_gnn_att_src", "L2_gnn_att_dst", "L2_gnn_bias_gat",
        "L2_gnn_W_proj", "L2_gnn_b_proj", "w3_t", "a3_t", "wih3_t", "whh3_t", "L3_gnn_b_ih", "L3_gnn_b_hh"]
_SCRATCH = [("records", (SLOTS, REC)),  ("t_rel", (NPAD * N_REL, D)), ("t_mlp", (NPAD, MH)),
            ("t_att", (NPAD, D)), ("t_score", (NPAD, SC)), ("t_both", (NPAD, SC + D)),
            ("edge_rows", (GROUPS * P, GT * D))]


def kernel(**inputs):
    import numpy as _np
    import concourse.bacc as _bacc
    from concourse import mybir as _mybir
    from concourse.bass_utils import run_bass_kernel_spmd as _run

    inputs = dict(inputs)
    inputs["w2_t"] = _np.transpose(inputs["L1_gnn_mlp_w2"], (0, 2, 1))
    inputs["wih_t"] = _np.transpose(inputs["L1_gnn_gru_wih"], (0, 2, 1))
    inputs["whh_t"] = _np.transpose(inputs["L1_gnn_gru_whh"], (0, 2, 1))
    inputs["b2_c"] = _np.transpose(_np.reshape(inputs["L1_gnn_mlp_b2"], (2, 2, 128)), (0, 2, 1))
    inputs["w3_t"] = _np.transpose(inputs["L3_gnn_W"], (0, 2, 1))
    inputs["a3_t"] = _np.transpose(_np.reshape(inputs["L3_gnn_a"], (4, 2, 128)), (2, 1, 0))
    inputs["wih3_t"] = _np.transpose(inputs["L3_gnn_W_ih"])
    inputs["whh3_t"] = _np.transpose(inputs["L3_gnn_W_hh"])
    nc = _bacc.Bacc("TRN2", target_bir_lowering=False, num_devices=1)
    arrays, d = {}, {}
    for name in _INS:
        a = _np.ascontiguousarray(inputs[name])
        arrays[f"in_{name}"] = a
        d[name] = nc.dram_tensor(f"in_{name}", a.shape, _mybir.dt.from_np(a.dtype), kind="ExternalInput").ap()
    d["attr_t"] = nc.dram_tensor("attr_t", (AR, SLOTS), BF16).ap()
    for name, shape in _SCRATCH:
        d[name] = nc.dram_tensor(name, shape, F32).ap()
    out = nc.dram_tensor("out_0", (N_NODES, D), F32, kind="ExternalOutput").ap()
    build(nc, d, out)
    return _run(nc, [arrays], core_ids=[0]).results[0]["out_0"]
```
